# Optimizing a Trainium2 kernel written in Bass

```python
import numpy as np
import jax
import jax.numpy as jnp

def _softmax(x, axis=-1):
    return jax.nn.softmax(x, axis=axis)

def _gelu(x):
    return jax.nn.gelu(x, approximate=True)

def _silu(x):
    return jax.nn.silu(x)

def _sigmoid(x):
    return jax.nn.sigmoid(x)

def _layernorm(x, axis=-1, eps=1e-05):
    m = jnp.mean(x, axis=axis, keepdims=True)
    v = jnp.var(x, axis=axis, keepdims=True)
    return (x - m) / jnp.sqrt(v + eps)

def _scatter_add(tgt, idx, src, axis=0):
    return tgt.at[idx].add(src)

def _segment_sum(src, seg, n):
    return jax.ops.segment_sum(src, seg, n)
kernel_name = 'mk_decoder_postln_d4_seqx_r8_0194cb'

def setup_inputs(seed: int=0):
    np.random.seed(seed)
    _w = jnp.asarray

    def _rec_inputs():
        import jax
        import jax.numpy as jnp
        _rk = jax.random.key(seed)
        x = -0.0003929 + 0.9999 * jax.random.normal(jax.random.fold_in(_rk, 1), (4, 256, 128), jnp.float32)
        _lenS = 256 - jax.random.randint(jax.random.fold_in(_rk, 7), (4,), 0, max(1, 256 // 4) + 1, jnp.int32)
        _lenS2 = 256 - jax.random.randint(jax.random.fold_in(_rk, 8), (4,), 0, max(1, 256 // 4) + 1, jnp.int32)
        _ctx_1024P = jax.random.normal(jax.random.fold_in(_rk, 11), (4, 16, 128), jnp.float32)
        _ctx_1024c = jax.random.dirichlet(jax.random.fold_in(_rk, 511), 0.3 * jnp.ones((16,), jnp.float32), (4, 256))
        _ctx_1024t = jnp.einsum('bsk,bkd->bsd', _ctx_1024c, _ctx_1024P)
        _ctx_1024t = _ctx_1024t * jax.lax.rsqrt(jnp.mean(jnp.square(_ctx_1024t)) + 1e-12) * 0.953939
        ctx_1024 = 4.13588e-05 + 0.999923 * (_ctx_1024t + 0.3 * jax.random.normal(jax.random.fold_in(_rk, 611), (4, 256, 128), jnp.float32))
        _validS = jnp.arange(256)[None, :] < _lenS[:, None]
        _validS2 = jnp.arange(256)[None, :] < _lenS2[:, None]
        _causal = jnp.tril(jnp.ones((256, 256), dtype=bool))
        mask_BxSxS2_bk1 = jnp.broadcast_to(_validS2[:, None, :], (4, 256, 256))
        return (x, ctx_1024, mask_BxSxS2_bk1)
    x, ctx_1024, mask_BxSxS2_bk1 = _rec_inputs()

    def _L0_attn_setup():
        import jax, jax.numpy as jnp
        import numpy as np
        B, T, C = (64, 32, 128)
        N_HEAD, HEAD_SIZE, KV_RANK = (16, 64, 128)
        BLOCK_SIZE = 32
        key = jax.random.key(seed)
        ks = jax.random.split(key, 5)
        HD = N_HEAD * HEAD_SIZE

        def init(k, shape):
            fan_in = shape[0]
            bound = 1.0 / np.sqrt(fan_in)
            return jax.random.uniform(k, shape, jnp.float32, -bound, bound)
        return {'x': jax.random.normal(ks[0], (B, T, C), jnp.float32), 'w_kv_down': init(ks[1], (C, KV_RANK)), 'w_kv_up': init(ks[2], (KV_RANK, 2 * HD)), 'w_q': init(ks[3], (C, HD)), 'w_out': init(ks[4], (HD, C))}
    _L0_attn_all = _L0_attn_setup()
    _L0_attn_in = {k: v for k, v in _L0_attn_all.items() if k in ('w_kv_down', 'w_kv_up', 'w_q', 'w_out')}
    del _L0_attn_all

    def _L0_xattn_setup():
        import jax, jax.numpy as jnp
        import numpy as np
        H = 128
        B = 8
        L_CHAR = 256
        L_SUB = 128

        def _linear(x, W, b):
            return jnp.einsum('blh,oh->blo', x, W) + b

        def _interp_linear(x, out_len):
            L_in = x.shape[1]
            pos = (jnp.arange(out_len, dtype=x.dtype) + 0.5) * (L_in / out_len) - 0.5
            pos = jnp.clip(pos, 0.0, L_in - 1)
            lo = jnp.floor(pos).astype(jnp.int32)
            hi = jnp.minimum(lo + 1, L_in - 1)
            w = (pos - lo.astype(x.dtype))[None, :, None]
            return x[:, lo] * (1 - w) + x[:, hi] * w
        key = jax.random.key(seed)
        ks = jax.random.split(key, 18)
        s = 0.02
        inp = {'char_emb': jax.random.normal(ks[0], (B, L_CHAR, H), jnp.float32), 'subword_emb': jax.random.normal(ks[1], (B, L_SUB, H), jnp.float32)}
        names = ['Wq_c', 'Wk_s', 'Wv_s', 'Wq_s', 'Wk_c', 'Wv_c']
        for i, n in enumerate(names):
            inp[n] = jax.random.normal(ks[2 + 2 * i], (H, H), jnp.float32) * s
            inp['b' + n[1:]] = jax.random.normal(ks[3 + 2 * i], (H,), jnp.float32) * s
        inp['Wg'] = jax.random.normal(ks[14], (H, 2 * H), jnp.float32) * s
        inp['bg'] = jax.random.normal(ks[15], (H,), jnp.float32) * s
        return inp
    _L0_xattn_all = _L0_xattn_setup()
    _L0_xattn_in = {k: v for k, v in _L0_xattn_all.items() if k in ('Wq_c', 'bq_c', 'Wk_s', 'bk_s', 'Wv_s', 'bv_s', 'Wq_s', 'bq_s', 'Wk_c', 'bk_c', 'Wv_c', 'bv_c', 'Wg', 'bg')}
    del _L0_xattn_all

    def _L0_ffn_setup():
        import jax, jax.numpy as jnp
        import numpy as np
        DIM = 128
        DEPTH = 2
        HEADS = 8
        DIM_HEAD = 64
        WINDOW = 64
        INNER = HEADS * DIM_HEAD
        HID = int(DIM * 4 * 2 / 3)
        B, N = (2, 1024)
        QK_SCALE = 8.0

        def shift_token(t):
            t1, t2 = jnp.split(t, 2, axis=-1)
            t2 = jnp.pad(t2, ((0, 0), (1, 0), (0, 0)))[:, :-1]
            return jnp.concatenate([t1, t2], axis=-1)

        def l2norm(t):
            return t / jnp.clip(jnp.linalg.norm(t, axis=-1, keepdims=True), 1e-12)

        def rotate_half(x):
            x1, x2 = jnp.split(x, 2, axis=-1)
            return jnp.concatenate([-x2, x1], axis=-1)

        def rotary_xpos(q, k):
            n = q.shape[-2]
            half_idx = jnp.arange(0, DIM_HEAD, 2, dtype=jnp.float32)
            inv_freq = 1.0 / 10000.0 ** (half_idx / DIM_HEAD)
            t = jnp.arange(n, dtype=jnp.float32)
            freqs = t[:, None] * inv_freq[None, :]
            freqs = jnp.concatenate([freqs, freqs], axis=-1)
            base = (half_idx + 0.4 * DIM_HEAD) / (1.4 * DIM_HEAD)
            power = (t - n // 2) / float(WINDOW // 2)
            scale = base[None, :] ** power[:, None]
            scale = jnp.concatenate([scale, scale], axis=-1)
            cos, sin = (jnp.cos(freqs), jnp.sin(freqs))
            q = q * cos * scale + rotate_half(q) * sin * scale
            k = k * cos / scale + rotate_half(k) * sin / scale
            return (q, k)

        def local_attention(q, k, v):
            b, h, n, d = q.shape
            w = n // WINDOW
            bq = q.reshape(b, h, w, WINDOW, d) * QK_SCALE
            bk = k.reshape(b, h, w, WINDOW, d)
            bv = v.reshape(b, h, w, WINDOW, d)

            def look_around(t):
                p = jnp.pad(t, ((0, 0), (0, 0), (1, 0), (0, 0), (0, 0)))
                return jnp.concatenate([p[:, :, :w], p[:, :, 1:]], axis=3)
            bk, bv = (look_around(bk), look_around(bv))
            bt = jnp.arange(n).reshape(w, WINDOW)
            btp = jnp.pad(bt, ((1, 0), (0, 0)), constant_values=-1)
            btk = jnp.concatenate([btp[:w], btp[1:]], axis=1)
            sim = jnp.einsum('bhwid,bhwjd->bhwij', bq, bk)
            i = bt[:, :, None]
            j = btk[:, None, :]
            mask = (i < j) | (i > j + WINDOW) | (j == -1)
            sim = jnp.where(mask, -jnp.finfo(sim.dtype).max, sim)
            attn = jax.nn.softmax(sim, axis=-1)
            out = jnp.einsum('bhwij,bhwjd->bhwid', attn, bv)
            return out.reshape(b, h, n, d)

        def _layer(x, wqkv, qs, ksc, wo, lg, lb, w1, b1, w2, b2):
            b, n, _ = x.shape
            h = shift_token(x)
            qkv = h @ wqkv
            q, k, v = jnp.split(qkv, 3, axis=-1)
            to_heads = lambda t: t.reshape(b, n, HEADS, DIM_HEAD).transpose(0, 2, 1, 3)
            q, k, v = (to_heads(q), to_heads(k), to_heads(v))
            q = l2norm(q) * qs
            k = l2norm(k) * ksc
            q, k = rotary_xpos(q, k)
            o = local_attention(q, k, v)
            o = o.transpose(0, 2, 1, 3).reshape(b, n, INNER)
            x = x + o @ wo
            h = shift_token(x)
            mu = h.mean(-1, keepdims=True)
            var = h.var(-1, keepdims=True)
            h = (h - mu) / jnp.sqrt(var + 1e-05) * lg + lb
            h = h @ w1 + b1
            a, g = jnp.split(h, 2, axis=-1)
            h = a * jax.nn.gelu(g, approximate=False)
            x = x + h @ w2 + b2
            return x
        key = jax.random.key(seed)
        ks = jax.random.split(key, 6)
        return {'x': jax.random.normal(ks[0], (B, N, DIM), jnp.float32), 'wqkv': jax.random.normal(ks[1], (DEPTH, DIM, 3 * INNER), jnp.float32) * 0.02, 'q_scale': jnp.ones((DEPTH, DIM_HEAD), jnp.float32), 'k_scale': jnp.ones((DEPTH, DIM_HEAD), jnp.float32), 'wo': jax.random.normal(ks[2], (DEPTH, INNER, DIM), jnp.float32) * 0.02, 'ln_g': jnp.ones((DEPTH, DIM), jnp.float32), 'ln_b': jnp.zeros((DEPTH, DIM), jnp.float32), 'w1': jax.random.normal(ks[3], (DEPTH, DIM, 2 * HID), jnp.float32) * 0.02, 'b1': jnp.zeros((DEPTH, 2 * HID), jnp.float32), 'w2': jax.random.normal(ks[4], (DEPTH, HID, DIM), jnp.float32) * 0.02, 'b2': jnp.zeros((DEPTH, DIM), jnp.float32)}
    _L0_ffn_all = _L0_ffn_setup()
    _L0_ffn_in = {k: v for k, v in _L0_ffn_all.items() if k in ('wqkv', 'q_scale', 'k_scale', 'wo', 'ln_g', 'ln_b', 'w1', 'b1', 'w2', 'b2')}
    del _L0_ffn_all

    def _L1_attn_setup():
        import jax, jax.numpy as jnp
        import numpy as np
        B_, L_, E_ = (2, 256, 128)
        EXPAND, DSTATE, DCONV = (2, 16, 4)
        DIN = EXPAND * E_
        DTR = E_ // 16

        def _layer_norm(x, g, b, eps=1e-05):
            mu = jnp.mean(x, axis=-1, keepdims=True)
            var = jnp.mean(jnp.square(x - mu), axis=-1, keepdims=True)
            return (x - mu) * jax.lax.rsqrt(var + eps) * g + b

        def _mamba_forward(x, ln_g, ln_b, W_in, conv_w, conv_b, W_x, W_dt, dt_bias, A_log, D, W_out):
            L = x.shape[1]
            xn = _layer_norm(x, ln_g, ln_b)
            xz = jnp.einsum('ble,de->bld', xn, W_in)
            u, z = (xz[..., :DIN], xz[..., DIN:])
            up = jnp.pad(u, ((0, 0), (DCONV - 1, 0), (0, 0)))
            uc = conv_b
            uc = sum((conv_w[:, k] * up[:, k:k + L, :] for k in range(DCONV))) + conv_b
            u = jax.nn.silu(uc)
            dbc = jnp.einsum('bld,rd->blr', u, W_x)
            dt_in = dbc[..., :DTR]
            Bm = dbc[..., DTR:DTR + DSTATE]
            Cm = dbc[..., DTR + DSTATE:]
            dt = jax.nn.softplus(jnp.einsum('blr,dr->bld', dt_in, W_dt) + dt_bias)
            A = -jnp.exp(A_log)
            dA = jnp.exp(dt[..., None] * A)
            dBu = dt[..., None] * Bm[:, :, None, :] * u[..., None]

            def step(h, e):
                da, dbu, c = e
                h = da * h + dbu
                y = jnp.einsum('bdn,bn->bd', h, c)
                return (h, y)
            elems = (jnp.moveaxis(dA, 1, 0), jnp.moveaxis(dBu, 1, 0), jnp.moveaxis(Cm, 1, 0))
            h0 = jnp.zeros((x.shape[0], DIN, DSTATE), x.dtype)
            _, ys = jax.lax.scan(step, h0, elems)
            y = jnp.moveaxis(ys, 0, 1) + u * D
            y = y * jax.nn.silu(z)
            out = jnp.einsum('bld,ed->ble', y, W_out)
            return x + out
        key = jax.random.key(seed)
        ks = jax.random.split(key, 8)
        s = 0.02
        f32 = jnp.float32
        A_log = jnp.tile(jnp.log(jnp.arange(1, DSTATE + 1, dtype=f32)), (DIN, 1))
        return {'x': jax.random.normal(ks[0], (B_, L_, E_), f32), 'ln_g': jnp.ones((E_,), f32), 'ln_b': jnp.zeros((E_,), f32), 'W_in': jax.random.normal(ks[1], (2 * DIN, E_), f32) * s, 'conv_w': jax.random.normal(ks[2], (DIN, DCONV), f32) * s, 'conv_b': jnp.zeros((DIN,), f32), 'W_x': jax.random.normal(ks[3], (DTR + 2 * DSTATE, DIN), f32) * s, 'W_dt': jax.random.normal(ks[4], (DIN, DTR), f32) * s, 'dt_bias': jax.random.normal(ks[5], (DIN,), f32) * 0.01, 'A_log': A_log, 'D': jnp.ones((DIN,), f32), 'W_out': jax.random.normal(ks[6], (E_, DIN), f32) * s}
    _L1_attn_all = _L1_attn_setup()
    _L1_attn_in = {k: v for k, v in _L1_attn_all.items() if k in ('ln_g', 'ln_b', 'W_in', 'conv_w', 'conv_b', 'W_x', 'W_dt', 'dt_bias', 'A_log', 'D', 'W_out')}
    del _L1_attn_all

    def _L1_xattn_setup():
        import jax, jax.numpy as jnp
        import numpy as np
        import math
        B, S, D, H = (4, 256, 128, 16)
        DH = D // H

        def _split_heads(x):
            b, s, _ = x.shape
            return x.reshape(b, s, H, DH).transpose(0, 2, 1, 3)
        key = jax.random.key(seed)
        ks = jax.random.split(key, 12)
        sc = 1.0 / math.sqrt(D)
        return {'x_q': jax.random.normal(ks[0], (B, S, D), jnp.float32), 'x_kv': jax.random.normal(ks[1], (B, S, D), jnp.float32), 'W_q': jax.random.normal(ks[2], (D, D), jnp.float32) * sc, 'b_q': jnp.zeros((D,), jnp.float32), 'W_k': jax.random.normal(ks[3], (D, D), jnp.float32) * sc, 'b_k': jnp.zeros((D,), jnp.float32), 'W_v': jax.random.normal(ks[4], (D, D), jnp.float32) * sc, 'b_v': jnp.zeros((D,), jnp.float32), 'W_out': jax.random.normal(ks[5], (D, D), jnp.float32) * sc, 'b_out': jnp.zeros((D,), jnp.float32)}
    _L1_xattn_all = _L1_xattn_setup()
    _L1_xattn_in = {k: v for k, v in _L1_xattn_all.items() if k in ('W_q', 'b_q', 'W_k', 'b_k', 'W_v', 'b_v', 'W_out', 'b_out')}
    del _L1_xattn_all

    def _L1_ffn_setup():
        import jax, jax.numpy as jnp
        import numpy as np
        B, S, D_MODEL, D_HIDDEN = (4, 256, 128, 512)

        def act_quant(x):
            scale = 127.0 / jnp.clip(jnp.max(jnp.abs(x), axis=-1, keepdims=True), 1e-05)
            return jnp.clip(jnp.round(x * scale), -128, 127) / scale

        def weight_quant(w):
            scale = 1.0 / jnp.clip(jnp.mean(jnp.abs(w)), 1e-05)
            return jnp.clip(jnp.round(w * scale), -1, 1) / scale

        def bit_linear(x, w):
            xq = x + jax.lax.stop_gradient(act_quant(x) - x)
            wq = w + jax.lax.stop_gradient(weight_quant(w) - w)
            return jnp.einsum('bsd,hd->bsh', xq, wq)

        def depthwise_conv1d(x_bcl, w, b):
            y = jax.lax.conv_general_dilated(x_bcl, w, window_strides=(1,), padding=[(1, 1)], dimension_numbers=('NCH', 'OIH', 'NCH'), feature_group_count=x_bcl.shape[1])
            return y + b[None, :, None]
        key = jax.random.key(seed)
        ks = jax.random.split(key, 5)
        lim1 = 1.0 / np.sqrt(D_MODEL)
        lim2 = 1.0 / np.sqrt(D_HIDDEN)
        limc = 1.0 / np.sqrt(3.0)
        return {'x': jax.random.normal(ks[0], (B, S, D_MODEL), dtype=jnp.float32), 'w1': jax.random.uniform(ks[1], (D_HIDDEN, D_MODEL), jnp.float32, -lim1, lim1), 'conv_w': jax.random.uniform(ks[2], (D_HIDDEN, 1, 3), jnp.float32, -limc, limc), 'conv_b': jax.random.uniform(ks[3], (D_HIDDEN,), jnp.float32, -limc, limc), 'w2': jax.random.uniform(ks[4], (D_MODEL, D_HIDDEN), jnp.float32, -lim2, lim2)}
    _L1_ffn_all = _L1_ffn_setup()
    _L1_ffn_in = {k: v for k, v in _L1_ffn_all.items() if k in ('w1', 'conv_w', 'conv_b', 'w2')}
    del _L1_ffn_all

    def _L2_attn_setup():
        import jax, jax.numpy as jnp
        import numpy as np
        T, B, E = (128, 4, 128)
        H = 16
        D = E // H
        L = 16
        key = jax.random.key(seed)
        ks = jax.random.split(key, 4)
        query = jax.random.normal(ks[0], (T, B, E), dtype=jnp.float32)
        in_proj_weight = jax.random.normal(ks[1], (3 * E, E), dtype=jnp.float32) * (1.0 / np.sqrt(E))
        in_proj_bias = jnp.zeros((3 * E,), dtype=jnp.float32)
        rel_pos_keys = jax.random.normal(ks[2], (2 * L + 1, E), dtype=jnp.float32) * (1.0 / np.sqrt(E))
        out_w = jax.random.normal(ks[3], (E, E), dtype=jnp.float32) * (1.0 / np.sqrt(E))
        out_b = jnp.zeros((E,), dtype=jnp.float32)
        return {'query': query, 'in_proj_weight': in_proj_weight, 'in_proj_bias': in_proj_bias, 'rel_pos_keys': rel_pos_keys, 'out_w': out_w, 'out_b': out_b}
    _L2_attn_all = _L2_attn_setup()
    _L2_attn_in = {k: v for k, v in _L2_attn_all.items() if k in ('in_proj_weight', 'in_proj_bias', 'rel_pos_keys', 'out_w', 'out_b')}
    del _L2_attn_all

    def _L2_xattn_setup():
        import jax, jax.numpy as jnp
        import numpy as np
        import math
        D_MODEL = 128
        NUM_HEADS = 16
        D_K = D_MODEL // NUM_HEADS
        key = jax.random.key(seed)
        ks = jax.random.split(key, 12)
        B, S = (4, 256)
        s = 1.0 / math.sqrt(D_MODEL)
        return {'query': jax.random.normal(ks[0], (B, S, D_MODEL), jnp.float32), 'key': jax.random.normal(ks[1], (B, S, D_MODEL), jnp.float32), 'value': jax.random.normal(ks[2], (B, S, D_MODEL), jnp.float32), 'wq': jax.random.normal(ks[3], (D_MODEL, D_MODEL), jnp.float32) * s, 'bq': jax.random.normal(ks[4], (D_MODEL,), jnp.float32) * s, 'wk': jax.random.normal(ks[5], (D_MODEL, D_MODEL), jnp.float32) * s, 'bk': jax.random.normal(ks[6], (D_MODEL,), jnp.float32) * s, 'wo': jax.random.normal(ks[7], (D_MODEL, D_MODEL), jnp.float32) * s, 'bo': jax.random.normal(ks[8], (D_MODEL,), jnp.float32) * s}
    _L2_xattn_all = _L2_xattn_setup()
    _L2_xattn_in = {k: v for k, v in _L2_xattn_all.items() if k in ('wq', 'bq', 'wk', 'bk', 'wo', 'bo')}
    del _L2_xattn_all

    def _L2_ffn_setup():
        import jax, jax.numpy as jnp
        import numpy as np
        B, S, H = (2, 512, 128)
        E, K, I = (8, 2, 176)
        key = jax.random.key(seed)
        ks = jax.random.split(key, 9)
        sc = 0.02
        return {'hidden_states': jax.random.normal(ks[0], (B, S, H), jnp.float32), 'gate_w': jax.random.normal(ks[1], (E, H), jnp.float32) * sc, 'w_gate': jax.random.normal(ks[2], (E, H, I), jnp.float32) * sc, 'w_up': jax.random.normal(ks[3], (E, H, I), jnp.float32) * sc, 'w_down': jax.random.normal(ks[4], (E, I, H), jnp.float32) * sc, 'sw_gate': jax.random.normal(ks[5], (H, I), jnp.float32) * sc, 'sw_up': jax.random.normal(ks[6], (H, I), jnp.float32) * sc, 'sw_down': jax.random.normal(ks[7], (I, H), jnp.float32) * sc, 'shared_gate_w': jax.random.normal(ks[8], (1, H), jnp.float32) * sc}
    _L2_ffn_all = _L2_ffn_setup()
    _L2_ffn_in = {k: v for k, v in _L2_ffn_all.items() if k in ('gate_w', 'w_gate', 'w_up', 'w_down', 'sw_gate', 'sw_up', 'sw_down', 'shared_gate_w')}
    del _L2_ffn_all

    def _L3_attn_setup():
        import jax, jax.numpy as jnp
        import numpy as np
        N_HEADS = 16
        WINDOW = 32
        key = jax.random.key(seed)
        ks = jax.random.split(key, 6)
        B, S, D = (2, 256, 128)
        x = jax.random.normal(ks[0], (B, S, D), dtype=jnp.float32)
        scale = 1.0 / np.sqrt(D)
        Wq = jax.random.normal(ks[1], (D, D), dtype=jnp.float32) * scale
        Wk = jax.random.normal(ks[2], (D, D), dtype=jnp.float32) * scale
        Wv = jax.random.normal(ks[3], (D, D), dtype=jnp.float32) * scale
        Wo = jax.random.normal(ks[4], (D, D), dtype=jnp.float32) * scale
        slopes = jnp.asarray(2.0 ** (-8.0 * (np.arange(1, N_HEADS + 1) / N_HEADS)), dtype=jnp.float32)
        return {'x': x, 'Wq': Wq, 'Wk': Wk, 'Wv': Wv, 'Wo': Wo, 'slopes': slopes}
    _L3_attn_all = _L3_attn_setup()
    _L3_attn_in = {k: v for k, v in _L3_attn_all.items() if k in ('Wq', 'Wk', 'Wv', 'Wo', 'slopes')}
    del _L3_attn_all

    def _L3_xattn_setup():
        import jax, jax.numpy as jnp
        import numpy as np
        DIM = 128
        HEADS = 16
        DIM_HEAD = 64
        INNER = HEADS * DIM_HEAD
        B, N = (2, 256)
        key = jax.random.key(seed)
        ks = jax.random.split(key, 8)
        q = jax.random.normal(ks[0], (B, N, DIM), dtype=jnp.float32)
        k = jax.random.normal(ks[1], (B, N, DIM), dtype=jnp.float32)
        v = jax.random.normal(ks[2], (B, N, DIM), dtype=jnp.float32)
        causal = jnp.triu(jnp.ones((N, N), dtype=jnp.bool_), k=1)
        mask = jnp.broadcast_to(causal, (B, N, N))
        s = 0.02
        Wq = jax.random.normal(ks[3], (DIM, INNER), dtype=jnp.float32) * s
        Wk = jax.random.normal(ks[4], (DIM, INNER), dtype=jnp.float32) * s
        Wv = jax.random.normal(ks[5], (DIM, INNER), dtype=jnp.float32) * s
        Wo = jax.random.normal(ks[6], (INNER, DIM), dtype=jnp.float32) * s
        bo = jnp.zeros((DIM,), dtype=jnp.float32)
        return {'q': q, 'k': k, 'v': v, 'mask': mask, 'Wq': Wq, 'Wk': Wk, 'Wv': Wv, 'Wo': Wo, 'bo': bo}
    _L3_xattn_all = _L3_xattn_setup()
    _L3_xattn_in = {k: v for k, v in _L3_xattn_all.items() if k in ('Wq', 'Wk', 'Wv', 'Wo', 'bo')}
    del _L3_xattn_all

    def _L3_ffn_setup():
        import jax, jax.numpy as jnp
        import numpy as np
        H = 128
        DFF = 512
        E_ROUTED = 7
        TOP_K = 2

        def _swiglu(flat, gate_w, up_w, down_w):
            g = flat @ gate_w.T
            up = flat @ up_w.T
            return jax.nn.silu(g) * up @ down_w.T
        key = jax.random.key(seed)
        ks = jax.random.split(key, 8)
        s = 0.02
        return {'x': jax.random.normal(ks[0], (4, 256, H), jnp.float32), 'shared_up': jax.random.normal(ks[1], (DFF, H), jnp.float32) * s, 'shared_gate': jax.random.normal(ks[2], (DFF, H), jnp.float32) * s, 'shared_down': jax.random.normal(ks[3], (H, DFF), jnp.float32) * s, 'routed_up': jax.random.normal(ks[4], (E_ROUTED, DFF, H), jnp.float32) * s, 'routed_gate': jax.random.normal(ks[5], (E_ROUTED, DFF, H), jnp.float32) * s, 'routed_down': jax.random.normal(ks[6], (E_ROUTED, H, DFF), jnp.float32) * s, 'router_w': jax.random.normal(ks[7], (E_ROUTED, H), jnp.float32) * 0.02}
    _L3_ffn_all = _L3_ffn_setup()
    _L3_ffn_in = {k: v for k, v in _L3_ffn_all.items() if k in ('shared_up', 'shared_gate', 'shared_down', 'routed_up', 'routed_gate', 'routed_down', 'router_w')}
    del _L3_ffn_all
    return {'x': x, 'ctx_1024': ctx_1024, 'mask_BxSxS2_bk1': mask_BxSxS2_bk1, 'L0_attn_w_kv_down': _L0_attn_in['w_kv_down'], 'L0_attn_w_kv_up': _L0_attn_in['w_kv_up'], 'L0_attn_w_q': _L0_attn_in['w_q'], 'L0_attn_w_out': _L0_attn_in['w_out'], 'L0_xattn_Wq_c': _L0_xattn_in['Wq_c'], 'L0_xattn_bq_c': _L0_xattn_in['bq_c'], 'L0_xattn_Wk_s': _L0_xattn_in['Wk_s'], 'L0_xattn_bk_s': _L0_xattn_in['bk_s'], 'L0_xattn_Wv_s': _L0_xattn_in['Wv_s'], 'L0_xattn_bv_s': _L0_xattn_in['bv_s'], 'L0_xattn_Wq_s': _L0_xattn_in['Wq_s'], 'L0_xattn_bq_s': _L0_xattn_in['bq_s'], 'L0_xattn_Wk_c': _L0_xattn_in['Wk_c'], 'L0_xattn_bk_c': _L0_xattn_in['bk_c'], 'L0_xattn_Wv_c': _L0_xattn_in['Wv_c'], 'L0_xattn_bv_c': _L0_xattn_in['bv_c'], 'L0_xattn_Wg': _L0_xattn_in['Wg'], 'L0_xattn_bg': _L0_xattn_in['bg'], 'L0_ffn_wqkv': _L0_ffn_in['wqkv'], 'L0_ffn_q_scale': _L0_ffn_in['q_scale'], 'L0_ffn_k_scale': _L0_ffn_in['k_scale'], 'L0_ffn_wo': _L0_ffn_in['wo'], 'L0_ffn_ln_g': _L0_ffn_in['ln_g'], 'L0_ffn_ln_b': _L0_ffn_in['ln_b'], 'L0_ffn_w1': _L0_ffn_in['w1'], 'L0_ffn_b1': _L0_ffn_in['b1'], 'L0_ffn_w2': _L0_ffn_in['w2'], 'L0_ffn_b2': _L0_ffn_in['b2'], 'L1_attn_ln_g': _L1_attn_in['ln_g'], 'L1_attn_ln_b': _L1_attn_in['ln_b'], 'L1_attn_W_in': _L1_attn_in['W_in'], 'L1_attn_conv_w': _L1_attn_in['conv_w'], 'L1_attn_conv_b': _L1_attn_in['conv_b'], 'L1_attn_W_x': _L1_attn_in['W_x'], 'L1_attn_W_dt': _L1_attn_in['W_dt'], 'L1_attn_dt_bias': _L1_attn_in['dt_bias'], 'L1_attn_A_log': _L1_attn_in['A_log'], 'L1_attn_D': _L1_attn_in['D'], 'L1_attn_W_out': _L1_attn_in['W_out'], 'L1_xattn_W_q': _L1_xattn_in['W_q'], 'L1_xattn_b_q': _L1_xattn_in['b_q'], 'L1_xattn_W_k': _L1_xattn_in['W_k'], 'L1_xattn_b_k': _L1_xattn_in['b_k'], 'L1_xattn_W_v': _L1_xattn_in['W_v'], 'L1_xattn_b_v': _L1_xattn_in['b_v'], 'L1_xattn_W_out': _L1_xattn_in['W_out'], 'L1_xattn_b_out': _L1_xattn_in['b_out'], 'L1_ffn_w1': _L1_ffn_in['w1'], 'L1_ffn_conv_w': _L1_ffn_in['conv_w'], 'L1_ffn_conv_b': _L1_ffn_in['conv_b'], 'L1_ffn_w2': _L1_ffn_in['w2'], 'L2_attn_in_proj_weight': _L2_attn_in['in_proj_weight'], 'L2_attn_in_proj_bias': _L2_attn_in['in_proj_bias'], 'L2_attn_rel_pos_keys': _L2_attn_in['rel_pos_keys'], 'L2_attn_out_w': _L2_attn_in['out_w'], 'L2_attn_out_b': _L2_attn_in['out_b'], 'L2_xattn_wq': _L2_xattn_in['wq'], 'L2_xattn_bq': _L2_xattn_in['bq'], 'L2_xattn_wk': _L2_xattn_in['wk'], 'L2_xattn_bk': _L2_xattn_in['bk'], 'L2_xattn_wo': _L2_xattn_in['wo'], 'L2_xattn_bo': _L2_xattn_in['bo'], 'L2_ffn_gate_w': _L2_ffn_in['gate_w'], 'L2_ffn_w_gate': _L2_ffn_in['w_gate'], 'L2_ffn_w_up': _L2_ffn_in['w_up'], 'L2_ffn_w_down': _L2_ffn_in['w_down'], 'L2_ffn_sw_gate': _L2_ffn_in['sw_gate'], 'L2_ffn_sw_up': _L2_ffn_in['sw_up'], 'L2_ffn_sw_down': _L2_ffn_in['sw_down'], 'L2_ffn_shared_gate_w': _L2_ffn_in['shared_gate_w'], 'L3_attn_Wq': _L3_attn_in['Wq'], 'L3_attn_Wk': _L3_attn_in['Wk'], 'L3_attn_Wv': _L3_attn_in['Wv'], 'L3_attn_Wo': _L3_attn_in['Wo'], 'L3_attn_slopes': _L3_attn_in['slopes'], 'L3_xattn_Wq': _L3_xattn_in['Wq'], 'L3_xattn_Wk': _L3_xattn_in['Wk'], 'L3_xattn_Wv': _L3_xattn_in['Wv'], 'L3_xattn_Wo': _L3_xattn_in['Wo'], 'L3_xattn_bo': _L3_xattn_in['bo'], 'L3_ffn_shared_up': _L3_ffn_in['shared_up'], 'L3_ffn_shared_gate': _L3_ffn_in['shared_gate'], 'L3_ffn_shared_down': _L3_ffn_in['shared_down'], 'L3_ffn_routed_up': _L3_ffn_in['routed_up'], 'L3_ffn_routed_gate': _L3_ffn_in['routed_gate'], 'L3_ffn_routed_down': _L3_ffn_in['routed_down'], 'L3_ffn_router_w': _L3_ffn_in['router_w']}

def reference(x, ctx_1024, mask_BxSxS2_bk1, L0_attn_w_kv_down, L0_attn_w_kv_up, L0_attn_w_q, L0_attn_w_out, L0_xattn_Wq_c, L0_xattn_bq_c, L0_xattn_Wk_s, L0_xattn_bk_s, L0_xattn_Wv_s, L0_xattn_bv_s, L0_xattn_Wq_s, L0_xattn_bq_s, L0_xattn_Wk_c, L0_xattn_bk_c, L0_xattn_Wv_c, L0_xattn_bv_c, L0_xattn_Wg, L0_xattn_bg, L0_ffn_wqkv, L0_ffn_q_scale, L0_ffn_k_scale, L0_ffn_wo, L0_ffn_ln_g, L0_ffn_ln_b, L0_ffn_w1, L0_ffn_b1, L0_ffn_w2, L0_ffn_b2, L1_attn_ln_g, L1_attn_ln_b, L1_attn_W_in, L1_attn_conv_w, L1_attn_conv_b, L1_attn_W_x, L1_attn_W_dt, L1_attn_dt_bias, L1_attn_A_log, L1_attn_D, L1_attn_W_out, L1_xattn_W_q, L1_xattn_b_q, L1_xattn_W_k, L1_xattn_b_k, L1_xattn_W_v, L1_xattn_b_v, L1_xattn_W_out, L1_xattn_b_out, L1_ffn_w1, L1_ffn_conv_w, L1_ffn_conv_b, L1_ffn_w2, L2_attn_in_proj_weight, L2_attn_in_proj_bias, L2_attn_rel_pos_keys, L2_attn_out_w, L2_attn_out_b, L2_xattn_wq, L2_xattn_bq, L2_xattn_wk, L2_xattn_bk, L2_xattn_wo, L2_xattn_bo, L2_ffn_gate_w, L2_ffn_w_gate, L2_ffn_w_up, L2_ffn_w_down, L2_ffn_sw_gate, L2_ffn_sw_up, L2_ffn_sw_down, L2_ffn_shared_gate_w, L3_attn_Wq, L3_attn_Wk, L3_attn_Wv, L3_attn_Wo, L3_attn_slopes, L3_xattn_Wq, L3_xattn_Wk, L3_xattn_Wv, L3_xattn_Wo, L3_xattn_bo, L3_ffn_shared_up, L3_ffn_shared_gate, L3_ffn_shared_down, L3_ffn_routed_up, L3_ffn_routed_gate, L3_ffn_routed_down, L3_ffn_router_w):
    import jax
    import jax.numpy as jnp

    def _L0_attn_ref(x, w_kv_down, w_kv_up, w_q, w_out):
        import jax, jax.numpy as jnp
        import numpy as np
        B, T, C = (64, 32, 128)
        N_HEAD, HEAD_SIZE, KV_RANK = (16, 64, 128)
        BLOCK_SIZE = 32
        Bx, Tx, Cx = x.shape
        HD = N_HEAD * HEAD_SIZE
        latent_kv = x @ w_kv_down
        kv = latent_kv @ w_kv_up
        k, v = (kv[..., :HD], kv[..., HD:])
        k = k.reshape(Bx, Tx, N_HEAD, HEAD_SIZE)
        v = v.reshape(Bx, Tx, N_HEAD, HEAD_SIZE)
        q = (x @ w_q).reshape(Bx, Tx, N_HEAD, HEAD_SIZE)
        scale = HEAD_SIZE ** (-0.5)
        att = jnp.einsum('bqhd,bkhd->bhqk', q, k) * scale
        causal = jnp.tril(jnp.ones((Tx, Tx), dtype=bool))
        att = jnp.where(causal, att, -jnp.inf)
        att = jax.nn.softmax(att, axis=-1)
        y = jnp.einsum('bhqk,bkhd->bqhd', att, v)
        y = y.reshape(Bx, Tx, HD)
        return y @ w_out

    def _L0_xattn_ref(char_emb, subword_emb, Wq_c, bq_c, Wk_s, bk_s, Wv_s, bv_s, Wq_s, bq_s, Wk_c, bk_c, Wv_c, bv_c, Wg, bg):
        import jax, jax.numpy as jnp
        import numpy as np
        H = 128
        B = 8
        L_CHAR = 256
        L_SUB = 128

        def _linear(x, W, b):
            return jnp.einsum('blh,oh->blo', x, W) + b

        def _interp_linear(x, out_len):
            L_in = x.shape[1]
            pos = (jnp.arange(out_len, dtype=x.dtype) + 0.5) * (L_in / out_len) - 0.5
            pos = jnp.clip(pos, 0.0, L_in - 1)
            lo = jnp.floor(pos).astype(jnp.int32)
            hi = jnp.minimum(lo + 1, L_in - 1)
            w = (pos - lo.astype(x.dtype))[None, :, None]
            return x[:, lo] * (1 - w) + x[:, hi] * w
        h = char_emb.shape[-1]
        scale = 1.0 / jnp.sqrt(jnp.asarray(h, char_emb.dtype))
        Q_char = _linear(char_emb, Wq_c, bq_c)
        K_sub = _linear(subword_emb, Wk_s, bk_s)
        V_sub = _linear(subword_emb, Wv_s, bv_s)
        scores = jnp.einsum('bqh,bkh->bqk', Q_char, K_sub) * scale
        char2sub = jnp.einsum('bqk,bkh->bqh', jax.nn.softmax(scores, axis=-1), V_sub)
        Q_sub = _linear(subword_emb, Wq_s, bq_s)
        K_char = _linear(char_emb, Wk_c, bk_c)
        V_char = _linear(char_emb, Wv_c, bv_c)
        scores2 = jnp.einsum('bqh,bkh->bqk', Q_sub, K_char) * scale
        sub2char = jnp.einsum('bqk,bkh->bqh', jax.nn.softmax(scores2, axis=-1), V_char)
        L_char = char_emb.shape[1]
        if sub2char.shape[1] != L_char:
            sub2char = _interp_linear(sub2char, L_char)
        gate_in = jnp.concatenate([char2sub, sub2char], axis=-1)
        gate = jax.nn.sigmoid(jnp.einsum('blh,oh->blo', gate_in, Wg) + bg)
        return gate * char2sub + (1 - gate) * sub2char

    def _L0_ffn_ref(x, wqkv, q_scale, k_scale, wo, ln_g, ln_b, w1, b1, w2, b2):
        import jax, jax.numpy as jnp
        import numpy as np
        DIM = 128
        DEPTH = 2
        HEADS = 8
        DIM_HEAD = 64
        WINDOW = 64
        INNER = HEADS * DIM_HEAD
        HID = int(DIM * 4 * 2 / 3)
        B, N = (2, 1024)
        QK_SCALE = 8.0

        def shift_token(t):
            t1, t2 = jnp.split(t, 2, axis=-1)
            t2 = jnp.pad(t2, ((0, 0), (1, 0), (0, 0)))[:, :-1]
            return jnp.concatenate([t1, t2], axis=-1)

        def l2norm(t):
            return t / jnp.clip(jnp.linalg.norm(t, axis=-1, keepdims=True), 1e-12)

        def rotate_half(x):
            x1, x2 = jnp.split(x, 2, axis=-1)
            return jnp.concatenate([-x2, x1], axis=-1)

        def rotary_xpos(q, k):
            n = q.shape[-2]
            half_idx = jnp.arange(0, DIM_HEAD, 2, dtype=jnp.float32)
            inv_freq = 1.0 / 10000.0 ** (half_idx / DIM_HEAD)
            t = jnp.arange(n, dtype=jnp.float32)
            freqs = t[:, None] * inv_freq[None, :]
            freqs = jnp.concatenate([freqs, freqs], axis=-1)
            base = (half_idx + 0.4 * DIM_HEAD) / (1.4 * DIM_HEAD)
            power = (t - n // 2) / float(WINDOW // 2)
            scale = base[None, :] ** power[:, None]
            scale = jnp.concatenate([scale, scale], axis=-1)
            cos, sin = (jnp.cos(freqs), jnp.sin(freqs))
            q = q * cos * scale + rotate_half(q) * sin * scale
            k = k * cos / scale + rotate_half(k) * sin / scale
            return (q, k)

        def local_attention(q, k, v):
            b, h, n, d = q.shape
            w = n // WINDOW
            bq = q.reshape(b, h, w, WINDOW, d) * QK_SCALE
            bk = k.reshape(b, h, w, WINDOW, d)
            bv = v.reshape(b, h, w, WINDOW, d)

            def look_around(t):
                p = jnp.pad(t, ((0, 0), (0, 0), (1, 0), (0, 0), (0, 0)))
                return jnp.concatenate([p[:, :, :w], p[:, :, 1:]], axis=3)
            bk, bv = (look_around(bk), look_around(bv))
            bt = jnp.arange(n).reshape(w, WINDOW)
            btp = jnp.pad(bt, ((1, 0), (0, 0)), constant_values=-1)
            btk = jnp.concatenate([btp[:w], btp[1:]], axis=1)
            sim = jnp.einsum('bhwid,bhwjd->bhwij', bq, bk)
            i = bt[:, :, None]
            j = btk[:, None, :]
            mask = (i < j) | (i > j + WINDOW) | (j == -1)
            sim = jnp.where(mask, -jnp.finfo(sim.dtype).max, sim)
            attn = jax.nn.softmax(sim, axis=-1)
            out = jnp.einsum('bhwij,bhwjd->bhwid', attn, bv)
            return out.reshape(b, h, n, d)

        def _layer(x, wqkv, qs, ksc, wo, lg, lb, w1, b1, w2, b2):
            b, n, _ = x.shape
            h = shift_token(x)
            qkv = h @ wqkv
            q, k, v = jnp.split(qkv, 3, axis=-1)
            to_heads = lambda t: t.reshape(b, n, HEADS, DIM_HEAD).transpose(0, 2, 1, 3)
            q, k, v = (to_heads(q), to_heads(k), to_heads(v))
            q = l2norm(q) * qs
            k = l2norm(k) * ksc
            q, k = rotary_xpos(q, k)
            o = local_attention(q, k, v)
            o = o.transpose(0, 2, 1, 3).reshape(b, n, INNER)
            x = x + o @ wo
            h = shift_token(x)
            mu = h.mean(-1, keepdims=True)
            var = h.var(-1, keepdims=True)
            h = (h - mu) / jnp.sqrt(var + 1e-05) * lg + lb
            h = h @ w1 + b1
            a, g = jnp.split(h, 2, axis=-1)
            h = a * jax.nn.gelu(g, approximate=False)
            x = x + h @ w2 + b2
            return x
        for l in range(DEPTH):
            x = _layer(x, wqkv[l], q_scale[l], k_scale[l], wo[l], ln_g[l], ln_b[l], w1[l], b1[l], w2[l], b2[l])
        return x

    def _L1_attn_ref(x, ln_g, ln_b, W_in, conv_w, conv_b, W_x, W_dt, dt_bias, A_log, D, W_out):
        import jax, jax.numpy as jnp
        import numpy as np
        B_, L_, E_ = (2, 256, 128)
        EXPAND, DSTATE, DCONV = (2, 16, 4)
        DIN = EXPAND * E_
        DTR = E_ // 16

        def _layer_norm(x, g, b, eps=1e-05):
            mu = jnp.mean(x, axis=-1, keepdims=True)
            var = jnp.mean(jnp.square(x - mu), axis=-1, keepdims=True)
            return (x - mu) * jax.lax.rsqrt(var + eps) * g + b

        def _mamba_forward(x, ln_g, ln_b, W_in, conv_w, conv_b, W_x, W_dt, dt_bias, A_log, D, W_out):
            L = x.shape[1]
            xn = _layer_norm(x, ln_g, ln_b)
            xz = jnp.einsum('ble,de->bld', xn, W_in)
            u, z = (xz[..., :DIN], xz[..., DIN:])
            up = jnp.pad(u, ((0, 0), (DCONV - 1, 0), (0, 0)))
            uc = conv_b
            uc = sum((conv_w[:, k] * up[:, k:k + L, :] for k in range(DCONV))) + conv_b
            u = jax.nn.silu(uc)
            dbc = jnp.einsum('bld,rd->blr', u, W_x)
            dt_in = dbc[..., :DTR]
            Bm = dbc[..., DTR:DTR + DSTATE]
            Cm = dbc[..., DTR + DSTATE:]
            dt = jax.nn.softplus(jnp.einsum('blr,dr->bld', dt_in, W_dt) + dt_bias)
            A = -jnp.exp(A_log)
            dA = jnp.exp(dt[..., None] * A)
            dBu = dt[..., None] * Bm[:, :, None, :] * u[..., None]

            def step(h, e):
                da, dbu, c = e
                h = da * h + dbu
                y = jnp.einsum('bdn,bn->bd', h, c)
                return (h, y)
            elems = (jnp.moveaxis(dA, 1, 0), jnp.moveaxis(dBu, 1, 0), jnp.moveaxis(Cm, 1, 0))
            h0 = jnp.zeros((x.shape[0], DIN, DSTATE), x.dtype)
            _, ys = jax.lax.scan(step, h0, elems)
            y = jnp.moveaxis(ys, 0, 1) + u * D
            y = y * jax.nn.silu(z)
            out = jnp.einsum('bld,ed->ble', y, W_out)
            return x + out
        return _mamba_forward(x, ln_g, ln_b, W_in, conv_w, conv_b, W_x, W_dt, dt_bias, A_log, D, W_out)

    def _L1_xattn_ref(x_q, x_kv, W_q, b_q, W_k, b_k, W_v, b_v, W_out, b_out):
        import jax, jax.numpy as jnp
        import numpy as np
        import math
        B, S, D, H = (4, 256, 128, 16)
        DH = D // H

        def _split_heads(x):
            b, s, _ = x.shape
            return x.reshape(b, s, H, DH).transpose(0, 2, 1, 3)
        q = x_q @ W_q.T + b_q
        k = x_kv @ W_k.T + b_k
        v = x_kv @ W_v.T + b_v
        qh, kh, vh = (_split_heads(q), _split_heads(k), _split_heads(v))
        scale = 1.0 / math.sqrt(DH)
        scores = jnp.einsum('bhqd,bhkd->bhqk', qh, kh) * scale
        attn = jax.nn.softmax(scores, axis=-1)
        ctx = jnp.einsum('bhqk,bhkd->bhqd', attn, vh)
        ctx = ctx.transpose(0, 2, 1, 3).reshape(x_q.shape[0], x_q.shape[1], D)
        return ctx @ W_out.T + b_out

    def _L1_ffn_ref(x, w1, conv_w, conv_b, w2):
        import jax, jax.numpy as jnp
        import numpy as np
        B, S, D_MODEL, D_HIDDEN = (4, 256, 128, 512)

        def act_quant(x):
            scale = 127.0 / jnp.clip(jnp.max(jnp.abs(x), axis=-1, keepdims=True), 1e-05)
            return jnp.clip(jnp.round(x * scale), -128, 127) / scale

        def weight_quant(w):
            scale = 1.0 / jnp.clip(jnp.mean(jnp.abs(w)), 1e-05)
            return jnp.clip(jnp.round(w * scale), -1, 1) / scale

        def bit_linear(x, w):
            xq = x + jax.lax.stop_gradient(act_quant(x) - x)
            wq = w + jax.lax.stop_gradient(weight_quant(w) - w)
            return jnp.einsum('bsd,hd->bsh', xq, wq)

        def depthwise_conv1d(x_bcl, w, b):
            y = jax.lax.conv_general_dilated(x_bcl, w, window_strides=(1,), padding=[(1, 1)], dimension_numbers=('NCH', 'OIH', 'NCH'), feature_group_count=x_bcl.shape[1])
            return y + b[None, :, None]
        h = bit_linear(x, w1)
        h = depthwise_conv1d(h.transpose(0, 2, 1), conv_w, conv_b)
        h = h.transpose(0, 2, 1)
        h = jax.nn.silu(h)
        return bit_linear(h, w2)

    def _L2_attn_ref(query, in_proj_weight, in_proj_bias, rel_pos_keys, out_w, out_b):
        import jax, jax.numpy as jnp
        import numpy as np
        T, B, E = (128, 4, 128)
        H = 16
        D = E // H
        L = 16
        t, b, e = query.shape
        scaling = D ** (-0.5)
        qkv = jnp.einsum('tbe,fe->tbf', query, in_proj_weight) + in_proj_bias
        q, k, v = jnp.split(qkv, 3, axis=-1)
        q = q * scaling

        def heads(x):
            return x.reshape(t, b * H, D).transpose(1, 0, 2)
        q, k, v = (heads(q), heads(k), heads(v))
        r = jnp.arange(t)
        dist = jnp.clip(r[None, :] - r[:, None], -L, L) + L
        rel_k = rel_pos_keys[dist][:, :, :D]
        scores = jnp.einsum('btd,bsd->bts', q, k) + jnp.einsum('btd,tsd->bts', q, rel_k)
        probs = jax.nn.softmax(scores, axis=-1)
        attn = jnp.einsum('bts,bsd->btd', probs, v)
        attn = attn.transpose(1, 0, 2).reshape(t, b, e)
        return jnp.einsum('tbe,oe->tbo', attn, out_w) + out_b

    def _L2_xattn_ref(query, key, value, wq, bq, wk, bk, wo, bo):
        import jax, jax.numpy as jnp
        import numpy as np
        import math
        D_MODEL = 128
        NUM_HEADS = 16
        D_K = D_MODEL // NUM_HEADS
        B, S, _ = query.shape
        q = query @ wq.T + bq
        k = key @ wk.T + bk
        v = value @ wk.T + bk
        q = q.reshape(B, S, NUM_HEADS, D_K).transpose(0, 2, 1, 3)
        k = k.reshape(B, S, NUM_HEADS, D_K).transpose(0, 2, 1, 3)
        v = v.reshape(B, S, NUM_HEADS, D_K).transpose(0, 2, 1, 3)
        scale = math.sqrt(D_K)
        scores = jnp.einsum('bhqd,bhkd->bhqk', q, k) / scale
        attn = jax.nn.softmax(scores, axis=-1)
        x = jnp.einsum('bhqk,bhkd->bhqd', attn, v)
        x = x.transpose(0, 2, 1, 3).reshape(B, S, D_MODEL)
        return x @ wo.T + bo

    def _L2_ffn_ref(hidden_states, gate_w, w_gate, w_up, w_down, sw_gate, sw_up, sw_down, shared_gate_w):
        import jax, jax.numpy as jnp
        import numpy as np
        B, S, H = (2, 512, 128)
        E, K, I = (8, 2, 176)
        b, s, h = hidden_states.shape
        x = hidden_states.reshape(-1, h)
        logits = jnp.einsum('th,eh->te', x, gate_w)
        probs = jax.nn.softmax(logits.astype(jnp.float32), axis=-1)
        topk_w, topk_i = jax.lax.top_k(probs, K)
        topk_w = topk_w / jnp.sum(topk_w, axis=-1, keepdims=True)
        combine = jnp.sum(jax.nn.one_hot(topk_i, E, dtype=topk_w.dtype) * topk_w[..., None], axis=1)
        combine = combine.astype(x.dtype)
        g = jnp.einsum('th,ehi->eti', x, w_gate)
        u = jnp.einsum('th,ehi->eti', x, w_up)
        eo = jnp.einsum('eti,eih->eth', jax.nn.silu(g) * u, w_down)
        out = jnp.einsum('te,eth->th', combine, eo)
        sg = jax.nn.sigmoid(jnp.einsum('th,oh->to', x, shared_gate_w))
        so = jax.nn.silu(x @ sw_gate) * (x @ sw_up) @ sw_down
        out = out + sg * so
        return out.reshape(b, s, h)

    def _L3_attn_ref(x, Wq, Wk, Wv, Wo, slopes):
        import jax, jax.numpy as jnp
        import numpy as np
        N_HEADS = 16
        WINDOW = 32
        B, S, D = x.shape
        H = N_HEADS
        dk = D // H
        q = jnp.einsum('bsd,od->bso', x, Wq).reshape(B, S, H, dk)
        k = jnp.einsum('bsd,od->bso', x, Wk).reshape(B, S, H, dk)
        v = jnp.einsum('bsd,od->bso', x, Wv).reshape(B, S, H, dk)
        scores = jnp.einsum('bqhd,bkhd->bhqk', q, k) / jnp.sqrt(jnp.asarray(dk, x.dtype))
        pos = jnp.arange(S)
        rel = (pos[:, None] - pos[None, :]).astype(x.dtype)
        scores = scores + slopes[None, :, None, None] * rel[None, None]
        window_mask = jnp.abs(pos[:, None] - pos[None, :]) <= WINDOW // 2
        scores = jnp.where(window_mask[None, None], scores, -jnp.inf)
        attn = jax.nn.softmax(scores, axis=-1)
        out = jnp.einsum('bhqk,bkhd->bqhd', attn, v).reshape(B, S, D)
        return jnp.einsum('bsd,od->bso', out, Wo)

    def _L3_xattn_ref(q, k, v, mask, Wq, Wk, Wv, Wo, bo):
        import jax, jax.numpy as jnp
        import numpy as np
        DIM = 128
        HEADS = 16
        DIM_HEAD = 64
        INNER = HEADS * DIM_HEAD
        B, N = (2, 256)
        h, d = (HEADS, DIM_HEAD)
        scale = d ** (-0.5)
        b, n, _ = q.shape

        def heads_split(x):
            return x.reshape(b, -1, h, d).transpose(0, 2, 1, 3)
        qh = heads_split(q @ Wq)
        kh = heads_split(k @ Wk)
        vh = heads_split(v @ Wv)
        dots = jnp.einsum('bhid,bhjd->bhij', qh, kh) * scale
        mask_value = -jnp.finfo(dots.dtype).max
        dots = jnp.where(mask[:, None, :, :], mask_value, dots)
        attn = jax.nn.softmax(dots, axis=-1)
        out = jnp.einsum('bhij,bhjd->bhid', attn, vh)
        out = out.transpose(0, 2, 1, 3).reshape(b, n, h * d)
        out = out @ Wo + bo
        return out

    def _L3_ffn_ref(x, shared_up, shared_gate, shared_down, routed_up, routed_gate, routed_down, router_w):
        import jax, jax.numpy as jnp
        import numpy as np
        H = 128
        DFF = 512
        E_ROUTED = 7
        TOP_K = 2

        def _swiglu(flat, gate_w, up_w, down_w):
            g = flat @ gate_w.T
            up = flat @ up_w.T
            return jax.nn.silu(g) * up @ down_w.T
        orig_shape = x.shape
        flat = x.reshape(-1, H)
        out = _swiglu(flat, shared_gate, shared_up, shared_down)
        logits = flat @ router_w.T
        probs = jax.nn.softmax(logits, axis=-1)
        top_vals, top_idx = jax.lax.top_k(probs, TOP_K)
        top_vals = top_vals / (top_vals.sum(-1, keepdims=True) + 1e-09)
        combine = jnp.sum(jax.nn.one_hot(top_idx, E_ROUTED, dtype=flat.dtype) * top_vals[..., None], axis=1)
        routed = jnp.zeros_like(flat)
        for e in range(E_ROUTED):
            eo = _swiglu(flat, routed_gate[e], routed_up[e], routed_down[e])
            routed = routed + combine[:, e:e + 1] * eo
        return (out + routed).reshape(orig_shape)
    x = _layernorm(x + _L0_attn_ref(x, L0_attn_w_kv_down, L0_attn_w_kv_up, L0_attn_w_q, L0_attn_w_out), axis=-1)
    x = _layernorm(x + _L0_xattn_ref(x, ctx_1024, L0_xattn_Wq_c, L0_xattn_bq_c, L0_xattn_Wk_s, L0_xattn_bk_s, L0_xattn_Wv_s, L0_xattn_bv_s, L0_xattn_Wq_s, L0_xattn_bq_s, L0_xattn_Wk_c, L0_xattn_bk_c, L0_xattn_Wv_c, L0_xattn_bv_c, L0_xattn_Wg, L0_xattn_bg), axis=-1)
    x = _layernorm(x + _L0_ffn_ref(x, L0_ffn_wqkv, L0_ffn_q_scale, L0_ffn_k_scale, L0_ffn_wo, L0_ffn_ln_g, L0_ffn_ln_b, L0_ffn_w1, L0_ffn_b1, L0_ffn_w2, L0_ffn_b2), axis=-1)
    x = _layernorm(x + _L1_attn_ref(x, L1_attn_ln_g, L1_attn_ln_b, L1_attn_W_in, L1_attn_conv_w, L1_attn_conv_b, L1_attn_W_x, L1_attn_W_dt, L1_attn_dt_bias, L1_attn_A_log, L1_attn_D, L1_attn_W_out), axis=-1)
    x = _layernorm(x + _L1_xattn_ref(x, ctx_1024, L1_xattn_W_q, L1_xattn_b_q, L1_xattn_W_k, L1_xattn_b_k, L1_xattn_W_v, L1_xattn_b_v, L1_xattn_W_out, L1_xattn_b_out), axis=-1)
    x = _layernorm(x + _L1_ffn_ref(x, L1_ffn_w1, L1_ffn_conv_w, L1_ffn_conv_b, L1_ffn_w2), axis=-1)
    x = _layernorm(x + _L2_attn_ref(x, L2_attn_in_proj_weight, L2_attn_in_proj_bias, L2_attn_rel_pos_keys, L2_attn_out_w, L2_attn_out_b), axis=-1)
    x = _layernorm(x + _L2_xattn_ref(x, ctx_1024, ctx_1024, L2_xattn_wq, L2_xattn_bq, L2_xattn_wk, L2_xattn_bk, L2_xattn_wo, L2_xattn_bo), axis=-1)
    x = _layernorm(x + _L2_ffn_ref(x, L2_ffn_gate_w, L2_ffn_w_gate, L2_ffn_w_up, L2_ffn_w_down, L2_ffn_sw_gate, L2_ffn_sw_up, L2_ffn_sw_down, L2_ffn_shared_gate_w), axis=-1)
    x = _layernorm(x + _L3_attn_ref(x, L3_attn_Wq, L3_attn_Wk, L3_attn_Wv, L3_attn_Wo, L3_attn_slopes), axis=-1)
    x = _layernorm(x + _L3_xattn_ref(x, ctx_1024, ctx_1024, mask_BxSxS2_bk1, L3_xattn_Wq, L3_xattn_Wk, L3_xattn_Wv, L3_xattn_Wo, L3_xattn_bo), axis=-1)
    x = _layernorm(x + _L3_ffn_ref(x, L3_ffn_shared_up, L3_ffn_shared_gate, L3_ffn_shared_down, L3_ffn_routed_up, L3_ffn_routed_gate, L3_ffn_routed_down, L3_ffn_router_w), axis=-1)
    return x

_drawn_inputs = setup_inputs


def setup_inputs(seed=0):
    import zlib

    import numpy as np

    out = dict(_drawn_inputs(seed))
    spreads = {'L0_ffn_q_scale': (1.0, 0.6),
     'L0_ffn_k_scale': (1.0, 0.6),
     'L0_ffn_ln_g': (1.0, 0.6),
     'L0_ffn_ln_b': (0.0, 0.8),
     'L0_ffn_b1': (0.0, 0.8),
     'L0_ffn_b2': (0.0, 0.1),
     'L1_attn_ln_g': (1.0, 0.6),
     'L1_attn_ln_b': (0.0, 0.8),
     'L1_attn_conv_b': (0.0, 0.8),
     'L1_attn_D': (1.0, 0.6),
     'L1_xattn_b_q': (0.0, 0.387),
     'L1_xattn_b_k': (0.0, 0.8),
     'L1_xattn_b_v': (0.0, 0.1),
     'L1_xattn_b_out': (0.0, 0.1),
     'L2_attn_in_proj_bias': (0.0, 0.1),
     'L2_attn_out_b': (0.0, 0.1),
     'L3_xattn_bo': (0.0, 0.1)}
    factors = {'L0_attn_w_q': 8.0,
     'L0_xattn_Wq_c': 8.0,
     'L0_xattn_bq_c': 8.0,
     'L0_xattn_Wk_s': 8.0,
     'L0_xattn_bk_s': 8.0,
     'L0_xattn_bv_s': 4.875,
     'L0_xattn_Wq_s': 8.0,
     'L0_xattn_bq_s': 8.0,
     'L0_xattn_Wk_c': 8.0,
     'L0_xattn_bk_c': 8.0,
     'L0_xattn_Wv_c': 7.905,
     'L0_xattn_bv_c': 4.434,
     'L0_xattn_Wg': 8.0,
     'L0_xattn_bg': 8.0,
     'L0_ffn_wqkv': 3.384,
     'L0_ffn_wo': 3.478,
     'L0_ffn_w1': 7.348,
     'L0_ffn_w2': 7.21,
     'L1_attn_W_in': 8.0,
     'L1_attn_conv_w': 8.0,
     'L1_attn_W_x': 8.0,
     'L1_attn_W_dt': 8.0,
     'L1_attn_dt_bias': 8.0,
     'L1_attn_A_log': 8.0,
     'L1_attn_W_out': 8.0,
     'L2_ffn_gate_w': 8.0,
     'L2_ffn_w_gate': 8.0,
     'L2_ffn_w_up': 8.0,
     'L2_ffn_w_down': 8.0,
     'L2_ffn_sw_gate': 8.0,
     'L2_ffn_sw_up': 8.0,
     'L2_ffn_sw_down': 8.0,
     'L2_ffn_shared_gate_w': 8.0,
     'L3_xattn_Wq': 8.0,
     'L3_xattn_Wk': 8.0,
     'L3_ffn_shared_up': 4.799,
     'L3_ffn_shared_gate': 4.8,
     'L3_ffn_shared_down': 4.748,
     'L3_ffn_routed_up': 6.658,
     'L3_ffn_routed_gate': 6.837,
     'L3_ffn_routed_down': 6.746,
     'L3_ffn_router_w': 8.0}
    for name, (base, spread) in spreads.items():
        noise = np.random.default_rng([zlib.crc32(name.encode()), seed]).standard_normal(out[name].shape)
        drawn = base * np.exp(spread * noise) if base else spread * noise
        out[name] = jnp.asarray(drawn.astype(out[name].dtype))
    for name, factor in factors.items():
        out[name] = (out[name] * factor).astype(out[name].dtype)
    return out
```

```python
import numpy as np
import concourse.bass as bass
from concourse import mybir
from contextlib import ExitStack

F32 = mybir.dt.float32
BF16 = mybir.dt.bfloat16
U8 = mybir.dt.uint8
ALU = mybir.AluOpType
ACT = mybir.ActivationFunctionType
AX = mybir.AxisListType

P = 128
B, S = 4, 256
T = B * S // P
NEG = -(2.0 ** 127)
EPS = 1e-5


class Signal:

    def __init__(self, sem, before, per):
        self.sem, self.before, self.per = sem, before, per

    def at(self, it, k):
        return it * self.per + (self.before + k)


class Signals:

    def __init__(self, ctx, nc):
        self.ctx, self.nc, self.sems, self.total = ctx, nc, {}, {}

    def __call__(self, name, per=1, iters=B):
        if name not in self.sems:
            self.sems[name] = self.ctx.enter_context(self.nc.semaphore(name))
            self.total[name] = 0
        before = self.total[name]
        self.total[name] += per * iters
        return Signal(self.sems[name], before, per)


class Steps:

    def __init__(self, sem, totals, name):
        self.sem, self.totals, self.name = sem, totals, name
        self.before, self.k, self.it, self.loops, self.per = 0, 0, None, 0, 0

    def enter(self, it):
        self.before += self.k
        self.it, self.k = it, 0
        self.per = self.totals.get((self.name, self.loops), 1)

    def leave(self, iters):
        self.totals[(self.name, self.loops)] = self.k
        self.loops += 1
        self.before += iters * self.k
        self.it, self.k = None, 0

    def value(self):
        return self.before + self.k if self.it is None else self.it * self.per + (self.before + self.k)

    def link(self, eng, ins):
        ins.then_inc(self.sem, 1)
        self.k += 1
        eng.wait_ge(self.sem, self.value())


def two(ap):
    return ap.rearrange("p (a b) -> p a b", a=2)


class Core:

    def __init__(self, ctx, nc, totals):
        self.nc = nc
        self.sig = Signals(ctx, nc)

        def sb(name, shape, dt=F32):
            return ctx.enter_context(nc.sbuf_tensor(name, shape, dt))

        self.sb = sb
        self.X = sb("X", [P, T, P])
        self.XT = sb("XT", [P, B * S])
        self.CT = sb("CT", [P, B * S])
        self.Z = sb("Z", [P, T, P])
        self.PS = ctx.enter_context(nc.psum_tensor("PS", [P, 8, 512], F32))
        self.bn = sb("bn", [P, T, 6])
        self.mv = sb("mv", [P, T, 2])
        self.sd = sb("sd", [P, T])
        self.rs = sb("rs", [P, T])
        self.rt = sb("rt", [P, T])
        self.IDB = sb("IDB", [P, P], BF16)
        self.CMB = sb("CMB", [P, P], BF16)
        self.arena = sb("arena", [P, 17600])
        self.small = sb("small", [P, 256])
        sems = {n: ctx.enter_context(nc.semaphore(n)) for n in ("dve_step", "act_step", "pool_step")}
        self.dve = Steps(sems["dve_step"], totals, "dve")
        self.act = Steps(sems["act_step"], totals, "act")
        self.pool = Steps(sems["pool_step"], totals, "pool")
        self.x_ready = self.sig("x_ready", 2, 1)

    def take(self, start, *shape):
        n = int(np.prod(shape))
        ap = self.arena[:, start:start + n]
        assert start + n <= 17600
        if len(shape) == 2:
            ap = ap.rearrange("p (a b) -> p a b", a=shape[0])
        if len(shape) == 3:
            ap = ap.rearrange("p (a b c) -> p a b c", a=shape[0], b=shape[1])
        return ap


def refine(link, v, r, a, eps, tmp):
    link(v.scalar_tensor_tensor(tmp, a, eps, r, ALU.add, ALU.mult))
    link(v.scalar_tensor_tensor(tmp, tmp, -0.5, r, ALU.mult, ALU.mult))
    link(v.scalar_tensor_tensor(r, tmp, 1.5, r, ALU.add, ALU.mult))


class LayerEnd:

    def __init__(self, c, z_ready, last=False):
        self.c, self.z_ready, self.last = c, z_ready, last
        self.var_ready = c.sig("var_ready", 1, 1)
        self.sd_ready = c.sig("sd_ready", 1, 1)
        self.x_tile = c.sig("x_tile", T, 1)
        self.xt_ps = c.sig("xt_ps", 2, 1)
        if not last:
            self.x_next = c.sig("x_ready", 2, 1)
        c.x_ready = None if last else self.x_next

    def vector(self, v):
        c = self.c
        for n in range(T):
            ins = v.bn_stats(c.bn[:, n, :], c.Z[:, n, :])
        c.dve.link(v, ins)
        for n in range(T):
            ins = v.bn_aggr(c.mv[:, n, :], c.bn[:, n, :])
        ins.then_inc(self.var_ready.sem, 1)
        v.wait_ge(self.sd_ready.sem, self.sd_ready.at(0, 1))
        c.dve.link(v, v.reciprocal(c.rs[:, :], c.sd[:, :]))
        refine(lambda ins: c.dve.link(v, ins), v, c.rs[:, :], c.mv[:, :, 1], EPS, c.rt[:, :])
        for n in range(T):
            v.tensor_scalar(c.X[:, n, :], c.Z[:, n, :], c.mv[:, n, 0:1], c.rs[:, n:n + 1],
                            ALU.subtract, ALU.mult).then_inc(self.x_tile.sem, 1)
        if not self.last:
            v.wait_ge(self.xt_ps.sem, self.xt_ps.at(0, 1))
            v.tensor_copy(c.XT[:, 0:512], c.PS[:, 0, :]).then_inc(self.x_next.sem, 1)

    def scalar(self, a):
        c = self.c
        a.wait_ge(self.var_ready.sem, self.var_ready.at(0, 1))
        a.activation(c.sd[:, :], c.mv[:, :, 1], ACT.Sqrt, bias=c.eps, scale=1.0).then_inc(self.sd_ready.sem, 1)
        if not self.last:
            a.wait_ge(self.xt_ps.sem, self.xt_ps.at(0, 2))
            a.activation(c.XT[:, 512:1024], c.PS[:, 1, :], ACT.Copy).then_inc(self.x_next.sem, 1)

    def tensor(self, pe):
        c = self.c
        if self.last:
            return
        for n in range(T):
            pe.wait_ge(self.x_tile.sem, self.x_tile.at(0, n + 1))
            ins = pe.transpose(c.PS[:, n // 4, (n % 4) * P:(n % 4) * P + P], c.X[:, n, :], c.ident)
            if n % 4 == 3:
                ins.then_inc(self.xt_ps.sem, 1)

    def gpsimd(self, g):
        pass


class Attention:

    H = 16

    def __init__(self, c, D, wq, wk, wv, wo, kv, wlat=None, causal=None, mask=None,
                 bq=None, bk=None, bv=None, bo=None, headmask=None):
        self.c, self.D, self.kv, self.causal, self.mask = c, D, kv, causal, mask
        self.wq, self.wk, self.wv, self.wo, self.wlat = wq, wk, wv, wo, wlat
        self.bq, self.bk, self.bv, self.bo, self.headmask = bq, bk, bv, bo, headmask
        self.hpc = 2 if D == 64 else 4
        self.M = P // self.hpc
        self.NC = self.H // self.hpc
        self.scale = float(D) ** -0.5
        self.qk_jobs = 8 if D == 64 else 1
        self.v_jobs = 4 if D == 64 else 1
        self.lat_jobs = 1 if wlat is not None else 0
        self.x_ready = c.x_ready
        s = c.sig
        self.src_ready = s("src_ready", 1)
        if self.lat_jobs:
            self.lat_done = s("lat_done", 1)
            self.lat_ev = s("lat_ev", 1)
        self.kp_done = s("kp_done", self.qk_jobs)
        self.qp_done = s("qp_done", self.qk_jobs)
        self.vp_done = s("vp_done", self.v_jobs)
        self.k_ev = s("k_ev", self.qk_jobs)
        self.q_ev = s("q_ev", self.qk_jobs)
        self.qz_ready = s("qz_ready", 4) if D == 8 else None
        self.v_ev = s("v_ev", self.v_jobs)
        self.mask_ready = s("mask_ready", 1) if mask is not None else None
        self.s_done = s("s_done", 16)
        self.mx_done = s("mx_done", 16)
        self.e_done = s("e_done", 16)
        self.r_done = s("r_done", 16)
        self.pn_done = s("pn_done", 16)
        self.t_done = s("t_done", 16)
        self.pt_ev = s("pt_ev", 16)
        self.o_done = s("o_done", self.NC)
        self.o_ev = s("o_ev", self.NC)
        self.y_done = s("y_done", 1)
        self.z_ready = s("z_ready", 1)
        t = c.take
        self.XB = t(0, 256)
        self.CB = t(256, 256)
        self.LT = t(512, 256)
        self.KT = t(768, 8, 256)
        self.QZ = t(2816, 16, 256)
        self.V = t(6912, 2, 1024)
        self.Pr = t(8960, 4, 512)
        self.PT = t(11008, 6, 512)
        self.OT = t(14080, 8, 256)
        self.nm = t(16128, 16, 2)
        self.ss = t(16160, 16, 2)
        self.ri = t(16192, 16, 3)
        self.QB = t(16240, 256)
        self.MB = t(16496, 256).bitcast(BF16).rearrange("p (a b) -> p a b", a=2)

    def spans(self):
        if self.causal is not None:
            return [(0, 0, 128), (128, 1, 256)]
        return [(0, 0, 256), (256, 1, 256)]

    def width(self):
        return 384 if self.causal is not None else 512

    def pt_blocks(self):
        if self.causal is not None:
            return [(0, 0), (128, 128), (256, 256)]
        return [(0, 0), (256, 128), (128, 256), (384, 384)]

    def tensor(self, pe):
        c, PS = self.c, self.c.PS
        pe.wait_ge(self.x_ready.sem, self.x_ready.at(0, 2))
        with pe.Fori(0, B) as it:
            pe.wait_ge(self.src_ready.sem, self.src_ready.at(it, 1))
            src = self.XB if self.kv == "x" else self.CB
            if self.lat_jobs:
                pe.matmul(PS[:, 4, 0:256], self.wlat, self.XB, start=True, stop=True).then_inc(self.lat_done.sem, 1)
                pe.wait_ge(self.lat_ev.sem, self.lat_ev.at(it, 1))
                src = self.LT
            for q in range(self.qk_jobs):
                if q >= 1:
                    pe.wait_ge(self.k_ev.sem, self.k_ev.at(it, q))
                pe.matmul(PS[:, 4, 0:256], self.wk[:, q * P:(q + 1) * P], src,
                          start=True, stop=True).then_inc(self.kp_done.sem, 1)
                if q >= 1:
                    pe.wait_ge(self.q_ev.sem, self.q_ev.at(it, q))
                pe.matmul(PS[:, 5, 0:256], self.wq[:, q * P:(q + 1) * P], self.XB,
                          start=True, stop=True).then_inc(self.qp_done.sem, 1)
            for n in range(self.v_jobs):
                if n == 0:
                    pe.wait_ge(self.k_ev.sem, self.k_ev.at(it, self.qk_jobs))
                if self.D == 64:
                    if n == 1:
                        pe.wait_ge(self.q_ev.sem, self.q_ev.at(it, self.qk_jobs))
                    if n >= 2:
                        pe.wait_ge(self.v_ev.sem, self.v_ev.at(it, n - 1))
                    t, h = n // 2, n % 2
                    pe.matmul(PS[:, 4 + n % 2, :], src[:, t * P:(t + 1) * P], self.wv[:, h * 512:(h + 1) * 512],
                              start=True, stop=True).then_inc(self.vp_done.sem, 1)
                else:
                    pe.matmul(PS[:, 4, 0:128], src[:, 0:P], self.wv, start=True, stop=True)
                    pe.matmul(PS[:, 4, 128:256], src[:, P:2 * P], self.wv, start=True, stop=True)\
                        .then_inc(self.vp_done.sem, 1)
            if self.mask is not None:
                pe.wait_ge(self.mask_ready.sem, self.mask_ready.at(it, 1))

            def scores(h):
                if self.D == 64:
                    pe.wait_ge(self.k_ev.sem, self.k_ev.at(it, h // 2 + 1))
                    pe.wait_ge(self.q_ev.sem, self.q_ev.at(it, h // 2 + 1))
                    keys = self.KT[:, h // 2, :]
                else:
                    if h == 0:
                        pe.wait_ge(self.k_ev.sem, self.k_ev.at(it, 1))
                    if h % 4 == 0:
                        pe.wait_ge(self.qz_ready.sem, self.qz_ready.at(it, h // 4 + 1))
                    keys = self.KT[:, 0, :]
                if h >= 2:
                    pe.wait_ge(self.e_done.sem, self.e_done.at(it, h - 1))
                for col, t, n in self.spans():
                    masked = self.causal is not None or self.mask is not None
                    ins = pe.matmul(PS[:, h % 2, col:col + n], self.QZ[:, h, t * P:(t + 1) * P], keys[:, 0:n],
                                    start=True, stop=not masked, skip_group_check=True)
                    if self.causal is not None:
                        ins = pe.matmul(PS[:, h % 2, col + n - P:col + n], c.IDB[:, :], c.CMB[:, :],
                                        start=False, stop=True, skip_group_check=True)
                    if self.mask is not None:
                        ins = pe.matmul(PS[:, h % 2, col:col + n], c.IDB[:, :], self.MB[:, t, :],
                                        start=False, stop=True, skip_group_check=True)
                ins.then_inc(self.s_done.sem, 1)

            def transposes(h):
                pe.wait_ge(self.pn_done.sem, self.pn_done.at(it, h + 1))
                if h >= 2:
                    pe.wait_ge(self.pt_ev.sem, self.pt_ev.at(it, h - 1))
                for a, b in self.pt_blocks():
                    ins = pe.transpose(PS[:, 2 + h % 2, b:b + P], self.Pr[:, h % 4, a:a + P], c.ident)
                ins.then_inc(self.t_done.sem, 1)

            def values(k):
                pe.wait_ge(self.pt_ev.sem, self.pt_ev.at(it, (k + 1) * self.hpc))
                if k == 0:
                    pe.wait_ge(self.v_ev.sem, self.v_ev.at(it, self.v_jobs))
                if k >= 2:
                    pe.wait_ge(self.o_ev.sem, self.o_ev.at(it, k - 1))
                for kt in range(2):
                    for r in range(self.hpc):
                        h = k * self.hpc + r
                        o = PS[r * self.M:(r + 1) * self.M, 6 + k % 2, 0:256]
                        pt = self.PT[:, h % 6, kt * 256:kt * 256 + 256]
                        if self.causal is not None and kt == 1:
                            o, pt = o[:, 128:256], pt[:, 0:128]
                        ins = pe.matmul(o, self.V[:, kt, h * self.M:(h + 1) * self.M], pt,
                                        start=(kt == 0), stop=(kt == 1), skip_group_check=True)
                ins.then_inc(self.o_done.sem, 1)

            for step in range(self.H + 6):
                if step < self.H:
                    scores(step)
                if 3 <= step < self.H + 3:
                    transposes(step - 3)
                h = step - 4
                if 0 <= h < self.H and h % self.hpc == self.hpc - 1:
                    values(h // self.hpc)
            pe.wait_ge(self.o_ev.sem, self.o_ev.at(it, self.NC))
            for t in range(2):
                for k in range(self.NC):
                    ins = pe.matmul(PS[:, 0, t * P:(t + 1) * P], self.OT[:, k, t * P:(t + 1) * P],
                                    self.wo[:, k, :], start=(k == 0), stop=(k == self.NC - 1))
            ins.then_inc(self.y_done.sem, 1)

    def scalar(self, a):
        c, PS = self.c, self.c.PS
        a.wait_ge(self.x_ready.sem, self.x_ready.at(0, 2))
        with a.Fori(0, B) as it:
            c.act.enter(it)
            if self.kv == "ctx":
                a.activation(self.CB, c.CT[:, bass.ds(it * S, S)], ACT.Copy)
            a.activation(self.XB, c.XT[:, bass.ds(it * S, S)], ACT.Copy).then_inc(self.src_ready.sem, 1)
            if self.lat_jobs:
                a.wait_ge(self.lat_done.sem, self.lat_done.at(it, 1))
                a.activation(self.LT, PS[:, 4, 0:256], ACT.Copy).then_inc(self.lat_ev.sem, 1)
            for q in range(self.qk_jobs):
                a.wait_ge(self.kp_done.sem, self.kp_done.at(it, q + 1))
                src = PS[:, 4, 0:256]
                if self.bk is None:
                    ins = a.activation(self.KT[:, q, :], src, ACT.Copy)
                else:
                    ins = a.activation(self.KT[:, q, :], src, ACT.Identity, bias=self.bk, scale=1.0)
                ins.then_inc(self.k_ev.sem, 1)

            def exps(h):
                a.wait_ge(self.mx_done.sem, self.mx_done.at(it, h + 1))
                if h >= 4:
                    a.wait_ge(self.t_done.sem, self.t_done.at(it, h - 3))
                for col, t, n in self.spans():
                    ins = a.activation(self.Pr[:, h % 4, col:col + n], PS[:, h % 2, col:col + n], ACT.Exp,
                                       bias=self.nm[:, h, t:t + 1], scale=1.0, accum_out=self.ss[:, h, t:t + 1])
                ins.then_inc(self.e_done.sem, 1)

            def out(k):
                a.wait_ge(self.o_done.sem, self.o_done.at(it, k + 1))
                a.activation(self.OT[:, k, :], PS[:, 6 + k % 2, 0:256], ACT.Copy)\
                    .then_inc(self.o_ev.sem, 1)

            for step in range(self.H + 6):
                if step < self.H:
                    exps(step)
                h = step - 5
                if 0 <= h < self.H and h % self.hpc == self.hpc - 1:
                    out(h // self.hpc)
        c.act.leave(B)

    def vector(self, v):
        c, PS = self.c, self.c.PS
        v.wait_ge(self.x_ready.sem, self.x_ready.at(0, 2))
        if self.causal is not None:
            v.tensor_copy(c.CMB[:, :], self.causal)
        if self.D == 64:
            v.memset(self.QZ[0:64, 1:16:2, :], 0.0)
            v.memset(self.QZ[64:128, 0:16:2, :], 0.0)
        else:
            v.memset(self.V[:, :, :], 0.0)
        ins = v.memset(self.nm[:, :, :], 0.0)
        c.dve.link(v, ins)
        with v.Fori(0, B) as it:
            c.dve.enter(it)
            if self.mask is not None:
                v.tensor_scalar(self.MB, self.mask[:, bass.ds(it * 2, 2), :], NEG, None, ALU.mult)\
                    .then_inc(self.mask_ready.sem, 1)
            for q in range(self.qk_jobs):
                v.wait_ge(self.qp_done.sem, self.qp_done.at(it, q + 1))
                if self.D == 64:
                    v.tensor_scalar(self.QZ[0:64, 2 * q, :], PS[0:64, 5, 0:256], self.scale, None, ALU.mult)
                    ins = v.tensor_scalar(self.QZ[64:128, 2 * q + 1, :], PS[64:128, 5, 0:256], self.scale, None,
                                          ALU.mult)
                else:
                    ins = v.tensor_scalar(self.QB, PS[:, 5, 0:256], self.bq, self.scale, ALU.add, ALU.mult)
                ins.then_inc(self.q_ev.sem, 1)
            for n in range(self.v_jobs):
                v.wait_ge(self.vp_done.sem, self.vp_done.at(it, n + 1))
                if self.D == 64:
                    ins = v.tensor_copy(self.V[:, n // 2, (n % 2) * 512:(n % 2) * 512 + 512],
                                        PS[:, 4 + n % 2, :])
                else:
                    for t in range(2):
                        dst = self.V[:, t, 0:512].rearrange("p (h e) -> p h e", e=32)[:, :, 0:8]
                        src = PS[:, 4, t * P:(t + 1) * P].rearrange("p (h e) -> p h e", e=8)
                        ins = v.tensor_tensor(dst, src, self.bv.rearrange("p (h e) -> p h e", e=8), ALU.add)
                ins.then_inc(self.v_ev.sem, 1)

            def maxima(h):
                v.wait_ge(self.s_done.sem, self.s_done.at(it, h + 1))
                if self.causal is not None:
                    v.tensor_reduce(self.nm[:, h, 0:1], PS[:, h % 2, 0:128], AX.X, ALU.max, negate=True)
                    ins = v.tensor_reduce(self.nm[:, h, 1:2], PS[:, h % 2, 128:384], AX.X, ALU.max, negate=True)
                else:
                    ins = v.tensor_reduce(self.nm[:, h, :], two(PS[:, h % 2, :]), AX.X, ALU.max, negate=True)
                ins.then_inc(self.mx_done.sem, 1)

            def reciprocals(h):
                v.wait_ge(self.e_done.sem, self.e_done.at(it, h + 1))
                if self.causal is not None:
                    v.reciprocal(self.ri[:, h, 0:2], self.ss[:, h, :])
                    ins = v.reciprocal(self.ri[:, h, 2:3], self.ss[:, h, 1:2])
                else:
                    ins = v.reciprocal(self.ri[:, h, 0:2], self.ss[:, h, :])
                ins.then_inc(self.r_done.sem, 1)

            def spread(h):
                v.wait_ge(self.t_done.sem, self.t_done.at(it, h + 1))
                if h >= 6:
                    v.wait_ge(self.o_done.sem, self.o_done.at(it, (h - 6) // self.hpc + 1))
                w = self.width()
                v.tensor_copy(self.PT[:, h % 6, 0:w], PS[:, 2 + h % 2, 0:w]).then_inc(self.pt_ev.sem, 1)

            for step in range(self.H + 6):
                if step < self.H:
                    maxima(step)
                if 1 <= step < self.H + 1:
                    reciprocals(step - 1)
                if 3 <= step < self.H + 3:
                    spread(step - 3)
            v.wait_ge(self.y_done.sem, self.y_done.at(it, 1))
            zt = c.Z[:, bass.ds(it * 2, 2), :]
            xt = c.X[:, bass.ds(it * 2, 2), :]
            y = two(PS[:, 0, 0:256])
            if self.bo is None:
                v.tensor_tensor(zt, y, xt, ALU.add).then_inc(self.z_ready.sem, 1)
            else:
                c.dve.link(v, v.tensor_tensor(zt, y, xt, ALU.add))
                v.tensor_tensor(zt, zt, self.bo.unsqueeze(1).to_broadcast([P, 2, P]), ALU.add)\
                    .then_inc(self.z_ready.sem, 1)
        c.dve.leave(B)
        v.wait_ge(self.z_ready.sem, self.z_ready.at(B - 1, 1))

    def gpsimd(self, g):
        c = self.c
        with g.Fori(0, B) as it:
            if self.D == 8:
                g.wait_ge(self.q_ev.sem, self.q_ev.at(it, 1))
                for k in range(4):
                    g.tensor_tensor(self.QZ[:, 4 * k:4 * k + 4, :],
                                    self.QB.unsqueeze(1).to_broadcast([P, 4, 256]),
                                    self.headmask[:, 4 * k:4 * k + 4].unsqueeze(2).to_broadcast([P, 4, 256]),
                                    ALU.mult).then_inc(self.qz_ready.sem, 1)
            for h in range(self.H):
                g.wait_ge(self.r_done.sem, self.r_done.at(it, h + 1))
                n = 3 if self.causal is not None else 2
                w = self.width()
                p = self.Pr[:, h % 4, 0:w].rearrange("p (a b) -> p a b", a=n)
                g.tensor_tensor(p, p, self.ri[:, h, 0:n].unsqueeze(2).to_broadcast([P, n, w // n]), ALU.mult)\
                    .then_inc(self.pn_done.sem, 1)


class Experts:

    ITERS, TOK, NT = 2, 512, 4

    def __init__(self, c, n_routed, full, rest, wgu, wrest, wdown, wdrest, router, iota, gated, tiny):
        self.c, self.E, self.full, self.rest = c, n_routed, full, rest
        self.wgu, self.wrest, self.wdown, self.wdrest, self.router = wgu, wrest, wdown, wdrest, router
        self.iota, self.gated, self.tiny = iota, gated, tiny
        self.NE = n_routed + 1
        self.blocks = full + (1 if rest else 0)
        self.cols = 8 + (1 if gated else 0)
        self.x_ready = c.x_ready
        s = c.sig
        n = self.NE * self.blocks
        self.logits_done = s("logits_done", 1, 1)
        self.shift_ready = s("shift_ready", 1, 1)
        self.exp_ready = s("exp_ready", 1, 1)
        self.gu_done = s("gu_done", n, 2)
        self.silu_done = s("silu_done", n, 2)
        self.h_ready = s("h_ready", n, 2)
        self.eo_done = s("eo_done", self.NE, 2)
        self.add_done = s("add_done", self.NE, 2)
        self.z_ready = self.add_done
        t = c.take
        self.SL = t(0, 2, 512)
        self.Hd = t(1024, 3, 512)
        self.lg = t(2560, T, 9)
        self.mx = t(2640, T)
        self.sm = t(2650, T)
        self.pr = t(2660, T, 8)
        self.top = t(2724, T, 8)
        self.idx = t(2788, T, 8).bitcast(mybir.dt.uint32)
        self.idf = t(2852, T, 8)
        self.dn = t(2916, T)
        self.wt = t(2930, T, 2)
        self.eq = t(2950, T, 8)
        self.eq2 = t(3014, T, 8)
        self.comb = t(3078, T, 9)

    def tensor(self, pe):
        c, PS = self.c, self.c.PS
        pe.wait_ge(self.x_ready.sem, self.x_ready.at(0, 2))
        for n in range(T):
            ins = pe.matmul(PS[:, 6, n * self.cols:(n + 1) * self.cols], c.XT[:, n * P:(n + 1) * P], self.router,
                            start=True, stop=True, skip_group_check=True)
        ins.then_inc(self.logits_done.sem, 1)
        with pe.Fori(0, self.ITERS) as it:
            x = c.XT[:, bass.ds(it * self.TOK, self.TOK)]

            def gate_up(j):
                e, f = divmod(j, self.blocks)
                if j >= 2:
                    pe.wait_ge(self.h_ready.sem, self.h_ready.at(it, j - 1))
                if f < self.full:
                    w = self.wgu[:, e * self.full + f, :]
                    pe.matmul(PS[:, j % 2, :], w[:, 0:P], x, start=True, stop=True)
                    pe.matmul(PS[:, 2 + j % 2, :], w[:, P:2 * P], x, start=True, stop=True)\
                        .then_inc(self.gu_done.sem, 1)
                else:
                    pe.matmul(PS[0:64 + self.rest, j % 2, :], self.wrest[:, e, :], x, start=True, stop=True)\
                        .then_inc(self.gu_done.sem, 1)

            def down(j):
                e, f = divmod(j, self.blocks)
                pe.wait_ge(self.h_ready.sem, self.h_ready.at(it, j + 1))
                if f == 0 and e >= 2:
                    pe.wait_ge(self.add_done.sem, self.add_done.at(it, e - 1))
                rows = P if f < self.full else self.rest
                w = self.wdown[:, e * self.full + f, :] if f < self.full else self.wdrest[:, e, :]
                for t in range(self.NT):
                    ins = pe.matmul(PS[:, 4 + e % 2, t * P:(t + 1) * P], self.Hd[0:rows, j % 3, t * P:(t + 1) * P], w,
                                    start=(f == 0 and t == 0), stop=(f == self.blocks - 1), skip_group_check=True)
                if f == self.blocks - 1:
                    ins.then_inc(self.eo_done.sem, 1)

            n = self.NE * self.blocks
            for j in range(n + 1):
                if j < n:
                    gate_up(j)
                if j >= 1:
                    down(j - 1)

    def scalar(self, a):
        c, PS = self.c, self.c.PS
        a.wait_ge(self.shift_ready.sem, self.shift_ready.at(0, 1))
        a.activation(self.lg[:, :, 0:self.cols], self.lg[:, :, 0:self.cols], ACT.Exp).then_inc(self.exp_ready.sem, 1)
        with a.Fori(0, self.ITERS) as it:
            for j in range(self.NE * self.blocks):
                f = j % self.blocks
                a.wait_ge(self.gu_done.sem, self.gu_done.at(it, j + 1))
                if f < self.full:
                    ins = a.activation(self.SL[:, j % 2, :], PS[:, j % 2, :], ACT.Silu)
                else:
                    ins = a.activation(self.SL[64:64 + self.rest, j % 2, :], PS[0:self.rest, j % 2, :], ACT.Silu)
                ins.then_inc(self.silu_done.sem, 1)

    def vector(self, v):
        c, PS = self.c, self.c.PS
        E, cols = self.E, self.cols

        def link(ins):
            c.dve.link(v, ins)

        def each(ap, n):
            return ap.unsqueeze(2).to_broadcast([P, T, n])

        v.wait_ge(self.logits_done.sem, self.logits_done.at(0, 1))
        lgp = PS[:, 6, 0:T * cols].rearrange("p (t e) -> p t e", t=T)
        link(v.tensor_copy(self.lg[:, :, 0:cols], lgp))
        if E < 8:
            link(v.memset(self.lg[:, :, E:8], NEG))
        link(v.tensor_reduce(self.mx, self.lg[:, :, 0:8], AX.X, ALU.max))
        if self.gated:
            link(v.tensor_scalar(self.lg[:, :, 8:9], self.lg[:, :, 8:9], -1.0, None, ALU.mult))
        v.tensor_tensor(self.lg[:, :, 0:8], self.lg[:, :, 0:8], each(self.mx, 8), ALU.subtract)\
            .then_inc(self.shift_ready.sem, 1)
        v.wait_ge(self.exp_ready.sem, self.exp_ready.at(0, 1))
        link(v.tensor_reduce(self.sm, self.lg[:, :, 0:8], AX.X, ALU.add))
        link(v.reciprocal(self.sm, self.sm))
        link(v.tensor_tensor(self.pr, self.lg[:, :, 0:8], each(self.sm, 8), ALU.mult))
        for n in range(T):
            ins = v.max(self.top[:, n, :], self.pr[:, n, :])
        link(ins)
        for n in range(T):
            ins = v.max_index(self.idx[:, n, :], self.top[:, n, :], self.pr[:, n, :])
        link(ins)
        link(v.tensor_copy(self.idf, self.idx))
        link(v.tensor_reduce(self.dn, self.top[:, :, 0:2], AX.X, ALU.add))
        if self.tiny:
            link(v.tensor_scalar(self.dn, self.dn, self.tiny, None, ALU.add))
        link(v.reciprocal(self.dn, self.dn))
        link(v.tensor_tensor(self.wt, self.top[:, :, 0:2], each(self.dn, 2), ALU.mult))
        iota = self.iota.unsqueeze(1).to_broadcast([P, T, 8])
        for i, eq in enumerate((self.eq, self.eq2)):
            link(v.tensor_tensor(eq, iota, each(self.idf[:, :, i], 8), ALU.is_equal))
            link(v.tensor_tensor(eq, eq, each(self.wt[:, :, i], 8), ALU.mult))
        link(v.tensor_tensor(self.comb[:, :, 0:8], self.eq, self.eq2, ALU.add))
        if self.gated:
            link(v.tensor_scalar(self.comb[:, :, E:E + 1], self.lg[:, :, 8:9], 1.0, None, ALU.add))
            link(v.reciprocal(self.comb[:, :, E:E + 1], self.comb[:, :, E:E + 1]))
        else:
            link(v.memset(self.comb[:, :, E:E + 1], 1.0))
        with v.Fori(0, self.ITERS) as it:
            def hidden(j):
                f = j % self.blocks
                v.wait_ge(self.silu_done.sem, self.silu_done.at(it, j + 1))
                if f < self.full:
                    ins = v.tensor_tensor(self.Hd[:, j % 3, :], self.SL[:, j % 2, :], PS[:, 2 + j % 2, :], ALU.mult)
                else:
                    r = slice(64, 64 + self.rest)
                    ins = v.tensor_tensor(self.Hd[0:self.rest, j % 3, :], self.SL[r, j % 2, :], PS[r, j % 2, :],
                                          ALU.mult)
                ins.then_inc(self.h_ready.sem, 1)

            def add(e):
                v.wait_ge(self.eo_done.sem, self.eo_done.at(it, e + 1))
                if e >= 1:
                    v.wait_ge(self.add_done.sem, self.add_done.at(it, e))
                for t in range(self.NT):
                    n = it * self.NT + t
                    z = c.Z[:, bass.ds(n, 1), :]
                    r = c.X[:, bass.ds(n, 1), :] if e == 0 else z
                    ins = v.scalar_tensor_tensor(z, PS[:, 4 + e % 2, t * P:(t + 1) * P].unsqueeze(1),
                                                 self.comb[:, bass.ds(n, 1), e], r, ALU.mult, ALU.add)
                ins.then_inc(self.add_done.sem, 1)

            n = self.NE * self.blocks
            for j in range(n):
                hidden(j)
                if j % self.blocks == min(1, self.blocks - 1) and j >= self.blocks:
                    add(j // self.blocks - 1)
            add(self.NE - 1)
        v.wait_ge(self.add_done.sem, self.add_done.at(self.ITERS - 1, self.NE))

    def gpsimd(self, g):
        pass


MAGIC = 1.5 * 2.0 ** 23


class BitLinear:

    def __init__(self, c, w1, w2, cw, cb):
        self.c, self.w1, self.w2, self.cw, self.cb = c, w1, w2, cw, cb
        self.x_ready = c.x_ready
        s = c.sig
        self.abs_ready = s("abs_ready", 1, 1)
        self.tot_done = s("tot_done", 1, 1)
        self.w_ready = s("w_ready", 1, 1)
        self.xq_ready = s("xq_ready", 2)
        self.xt_done = s("xt_done", 1)
        self.xt_ev = s("xt_ev", 1)
        self.h_done = s("h_done", 4)
        self.h_ev = s("h_ev", 4)
        self.cv_ready = s("cv_ready", 4)
        self.sl_ready = s("sl_ready", 4)
        self.ht_done = s("ht_done", 2)
        self.hq_ready = s("hq_ready", 2)
        self.hqt_done = s("hqt_done", 2)
        self.hqt_ev = s("hqt_ev", 2)
        self.y_done = s("y_done", 1)
        self.z_ready = s("z_ready", 1)
        t = c.take
        self.W1 = t(0, 512)
        self.W2 = t(512, 4, 128)
        self.ab = t(1024, 2)
        self.sc = t(1030, 2)
        self.isc = t(1034, 2)
        self.tmp = t(1040, 512)
        self.am = t(1560, 2)
        self.s1 = t(1564, 2)
        self.i1 = t(1568, 2)
        self.xq = t(1600, 2, 128)
        self.xqt = t(1856, 256)
        self.hp = t(2112, 4, 258)
        self.cv = t(3160, 4, 256)
        self.sl = t(4200, 4, 256)
        self.hq = t(5300, 2, 512)
        self.hqt = t(6400, 2, 512)
        self.am2 = t(7500, 2)
        self.s2 = t(7504, 2)
        self.i2 = t(7508, 2)

    def tensor(self, pe):
        c, PS = self.c, self.c.PS
        pe.wait_ge(self.abs_ready.sem, self.abs_ready.at(0, 1))
        pe.matmul(PS[:, 7, 0:2], c.one.to_broadcast([P, P]), self.ab, start=True, stop=True).then_inc(self.tot_done.sem, 1)
        pe.wait_ge(self.w_ready.sem, self.w_ready.at(0, 1))
        with pe.Fori(0, B) as it:
            for t in range(2):
                pe.wait_ge(self.xq_ready.sem, self.xq_ready.at(it, t + 1))
                ins = pe.transpose(PS[:, 6, t * P:(t + 1) * P], self.xq[:, t, :], c.ident)
            ins.then_inc(self.xt_done.sem, 1)
            pe.wait_ge(self.xt_ev.sem, self.xt_ev.at(it, 1))
            for f in range(4):
                if f >= 2:
                    pe.wait_ge(self.h_ev.sem, self.h_ev.at(it, f - 1))
                pe.matmul(PS[:, f % 2, 0:256], self.W1[:, f * P:(f + 1) * P], self.xqt, start=True, stop=True)\
                    .then_inc(self.h_done.sem, 1)
            for t in range(2):
                for f in range(4):
                    pe.wait_ge(self.sl_ready.sem, self.sl_ready.at(it, f + 1))
                    ins = pe.transpose(PS[:, 2 + t, f * P:(f + 1) * P], self.sl[:, f, t * P:(t + 1) * P], c.ident)
                ins.then_inc(self.ht_done.sem, 1)
            for t in range(2):
                pe.wait_ge(self.hq_ready.sem, self.hq_ready.at(it, t + 1))
                for f in range(4):
                    ins = pe.transpose(PS[:, 4 + t, f * P:(f + 1) * P], self.hq[:, t, f * P:(f + 1) * P], c.ident)
                ins.then_inc(self.hqt_done.sem, 1)
            for t in range(2):
                pe.wait_ge(self.hqt_ev.sem, self.hqt_ev.at(it, t + 1))
                for f in range(4):
                    ins = pe.matmul(PS[:, 7, t * P:(t + 1) * P], self.hqt[:, t, f * P:(f + 1) * P], self.W2[:, f, :],
                                    start=(f == 0), stop=(f == 3))
            ins.then_inc(self.y_done.sem, 1)

    def scalar(self, a):
        c, PS = self.c, self.c.PS
        c.act.link(a, a.activation(self.tmp, self.w1, ACT.Abs, accum_out=self.ab[:, 0:1]))
        a.activation(self.tmp, self.w2.rearrange("p a b -> p (a b)"), ACT.Abs, accum_out=self.ab[:, 1:2])\
            .then_inc(self.abs_ready.sem, 1)
        with a.Fori(0, B) as it:
            a.wait_ge(self.xt_done.sem, self.xt_done.at(it, 1))
            a.activation(self.xqt, PS[:, 6, 0:256], ACT.Copy).then_inc(self.xt_ev.sem, 1)
            for f in range(4):
                a.wait_ge(self.h_done.sem, self.h_done.at(it, f + 1))
                a.activation(self.hp[:, f, 1:257], PS[:, f % 2, 0:256], ACT.Copy).then_inc(self.h_ev.sem, 1)
            for f in range(4):
                a.wait_ge(self.cv_ready.sem, self.cv_ready.at(it, f + 1))
                a.activation(self.sl[:, f, :], self.cv[:, f, :], ACT.Silu).then_inc(self.sl_ready.sem, 1)
            for t in range(2):
                a.wait_ge(self.hqt_done.sem, self.hqt_done.at(it, t + 1))
                a.activation(self.hqt[:, t, :], PS[:, 4 + t, :], ACT.Copy).then_inc(self.hqt_ev.sem, 1)

    def vector(self, v):
        c, PS = self.c, self.c.PS

        def link(ins):
            c.dve.link(v, ins)

        link(v.memset(self.hp, 0.0))
        v.wait_ge(self.tot_done.sem, self.tot_done.at(0, 1))
        link(v.tensor_scalar(self.isc, PS[:, 7, 0:2], 1.0 / 65536.0, 1e-5, ALU.mult, ALU.max))
        link(v.reciprocal(self.sc, self.isc))
        w1, w2 = self.w1, self.w2.rearrange("p a b -> p (a b)")
        W2 = self.W2.rearrange("p a b -> p (a b)")
        for i, (src, dst) in enumerate(((w1, self.W1), (w2, W2))):
            link(v.tensor_scalar(dst, src, self.sc[:, i:i + 1], MAGIC, ALU.mult, ALU.add))
            link(v.tensor_scalar(dst, dst, MAGIC, 1.0, ALU.subtract, ALU.min))
            link(v.tensor_scalar(dst, dst, -1.0, self.isc[:, i:i + 1], ALU.max, ALU.mult))
        v.tensor_copy(self.ab, self.sc).then_inc(self.w_ready.sem, 1)
        v.wait_ge(self.x_ready.sem, self.x_ready.at(0, 2))

        def scales(am, s, i):
            link(v.tensor_scalar(i, am, 1e-5, None, ALU.max))
            link(v.reciprocal(s, i))
            v.tensor_scalar(s, s, 127.0, None, ALU.mult)
            link(v.tensor_scalar(i, i, 1.0 / 127.0, None, ALU.mult))

        def quantise(dst, src, s, i, ready):
            link(v.tensor_scalar(dst, src, s, MAGIC, ALU.mult, ALU.add))
            link(v.tensor_scalar(dst, dst, MAGIC, 127.0, ALU.subtract, ALU.min))
            v.tensor_scalar(dst, dst, -128.0, i, ALU.max, ALU.mult).then_inc(ready.sem, 1)

        with v.Fori(0, B) as it:
            c.dve.enter(it)
            x = c.X[:, bass.ds(it * 2, 2), :]
            link(v.tensor_reduce(self.am, x, AX.X, ALU.max, apply_absolute_value=True))
            scales(self.am, self.s1, self.i1)
            for t in range(2):
                quantise(self.xq[:, t:t + 1, :], c.X[:, bass.ds(it * 2 + t, 1), :], self.s1[:, t:t + 1],
                         self.i1[:, t:t + 1], self.xq_ready)
            for f in range(4):
                v.wait_ge(self.h_ev.sem, self.h_ev.at(it, f + 1))
                h, cv = self.hp[:, f, :], self.cv[:, f, :]
                link(v.tensor_scalar(cv, h[:, 1:257], self.cw[:, f, 1:2], self.cb[:, f:f + 1], ALU.mult, ALU.add))
                link(v.scalar_tensor_tensor(cv, h[:, 0:256], self.cw[:, f, 0:1], cv, ALU.mult, ALU.add))
                v.scalar_tensor_tensor(cv, h[:, 2:258], self.cw[:, f, 2:3], cv, ALU.mult, ALU.add)\
                    .then_inc(self.cv_ready.sem, 1)
            for t in range(2):
                v.wait_ge(self.ht_done.sem, self.ht_done.at(it, t + 1))
                h, u = PS[:, 2 + t, :], slice(t, t + 1)
                link(v.tensor_reduce(self.am2[:, u], h, AX.X, ALU.max, apply_absolute_value=True))
                scales(self.am2[:, u], self.s2[:, u], self.i2[:, u])
                quantise(self.hq[:, t, :], h, self.s2[:, u], self.i2[:, u], self.hq_ready)
            v.wait_ge(self.y_done.sem, self.y_done.at(it, 1))
            v.tensor_tensor(c.Z[:, bass.ds(it * 2, 2), :], two(PS[:, 7, 0:256]), x, ALU.add)\
                .then_inc(self.z_ready.sem, 1)
        c.dve.leave(B)
        v.wait_ge(self.z_ready.sem, self.z_ready.at(B - 1, 1))

    def gpsimd(self, g):
        pass


class TwoWay:

    def __init__(self, c, w, bq, bk, bv, wg, nbg):
        self.c, self.w, self.bq, self.bk, self.bv, self.wg, self.nbg = c, w, bq, bk, bv, wg, nbg
        self.x_ready = c.x_ready
        s = c.sig
        self.src_ready = s("src_ready", 1)
        self.qk_done = s("p_done", 4)
        self.q_ev = s("q_ev", 2)
        self.k_ev = s("k_ev", 2)
        self.v_done = s("vp_done", 2)
        self.v_ev = s("v_ev", 2)
        self.s_done = s("s_done", 2)
        self.mx_done = s("mx_done", 2)
        self.e_done = s("e_done", 2)
        self.pn_done = s("pn_done", 2)
        self.t_done = s("t_done", 2)
        self.pt_ev = s("pt_ev", 2)
        self.o_done = s("o_done", 2)
        self.o_ev = s("o_ev", 2)
        self.g_done = s("g_done", 1)
        self.g_exp = s("g_exp", 1)
        self.y_ready = s("y_ready", 1)
        self.y_done = s("y_done", 1)
        self.z_ready = s("z_ready", 1)
        t = c.take
        self.XB, self.CB = t(0, 256), t(256, 256)
        self.Q, self.K = t(512, 2, 256), t(1024, 2, 256)
        self.V = t(1536, 2, 2, 128)
        self.Pr, self.PT = t(2048, 2, 512), t(3072, 2, 512)
        self.O = t(4096, 2, 256)
        self.G, self.D, self.Y = t(4608, 256), t(4864, 256), t(5120, 256)
        self.nm, self.ss, self.ri = t(5400, 2, 2), t(5404, 2, 2), t(5408, 2, 2)
        self.nb = t(5412, 1)

    def tensor(self, pe):
        c, PS = self.c, self.c.PS
        with pe.Fori(0, B) as it:
            pe.wait_ge(self.src_ready.sem, self.src_ready.at(it, 1))
            for i in range(2):
                qs, ks = (self.XB, self.CB) if i == 0 else (self.CB, self.XB)
                pe.matmul(PS[:, 2 * i, 0:256], self.w[:, 3 * i, :], qs, start=True, stop=True)\
                    .then_inc(self.qk_done.sem, 1)
                pe.matmul(PS[:, 2 * i + 1, 0:256], self.w[:, 3 * i + 1, :], ks, start=True, stop=True)\
                    .then_inc(self.qk_done.sem, 1)
            for i in range(2):
                ks = self.CB if i == 0 else self.XB
                for t in range(2):
                    ins = pe.matmul(PS[:, 4 + i, t * P:(t + 1) * P], ks[:, t * P:(t + 1) * P], self.w[:, 3 * i + 2, :],
                                    start=True, stop=True)
                ins.then_inc(self.v_done.sem, 1)
            for i in range(2):
                pe.wait_ge(self.q_ev.sem, self.q_ev.at(it, i + 1))
                pe.wait_ge(self.k_ev.sem, self.k_ev.at(it, i + 1))
                for t in range(2):
                    ins = pe.matmul(PS[:, 6 + i, t * 256:t * 256 + 256], self.Q[:, i, t * P:(t + 1) * P],
                                    self.K[:, i, :], start=True, stop=True)
                ins.then_inc(self.s_done.sem, 1)
            for i in range(2):
                pe.wait_ge(self.pn_done.sem, self.pn_done.at(it, i + 1))
                for a, b in [(0, 0), (256, 128), (128, 256), (384, 384)]:
                    ins = pe.transpose(PS[:, i, b:b + P], self.Pr[:, i, a:a + P], c.ident)
                ins.then_inc(self.t_done.sem, 1)
            for i in range(2):
                pe.wait_ge(self.pt_ev.sem, self.pt_ev.at(it, i + 1))
                if i == 0:
                    pe.wait_ge(self.v_ev.sem, self.v_ev.at(it, 2))
                for kt in range(2):
                    ins = pe.matmul(PS[:, 2 + i, 0:256], self.V[:, i, kt, :], self.PT[:, i, kt * 256:kt * 256 + 256],
                                    start=(kt == 0), stop=(kt == 1))
                ins.then_inc(self.o_done.sem, 1)
            for i in range(2):
                pe.wait_ge(self.o_ev.sem, self.o_ev.at(it, i + 1))
                ins = pe.matmul(PS[:, 4, 0:256], self.wg[:, i, :], self.O[:, i, :], start=(i == 0), stop=(i == 1))
            ins.then_inc(self.g_done.sem, 1)
            pe.wait_ge(self.y_ready.sem, self.y_ready.at(it, 1))
            for t in range(2):
                ins = pe.transpose(PS[:, 7, t * P:(t + 1) * P], self.Y[:, t * P:(t + 1) * P], c.ident)
            ins.then_inc(self.y_done.sem, 1)

    def scalar(self, a):
        c, PS = self.c, self.c.PS
        a.wait_ge(self.x_ready.sem, self.x_ready.at(0, 2))
        with a.Fori(0, B) as it:
            a.activation(self.CB, c.CT[:, bass.ds(it * S, S)], ACT.Copy)
            a.activation(self.XB, c.XT[:, bass.ds(it * S, S)], ACT.Copy).then_inc(self.src_ready.sem, 1)
            for i in range(2):
                a.wait_ge(self.qk_done.sem, self.qk_done.at(it, 2 * i + 2))
                a.activation(self.K[:, i, :], PS[:, 2 * i + 1, 0:256], ACT.Identity, bias=self.bk[:, i:i + 1],
                             scale=1.0).then_inc(self.k_ev.sem, 1)
            for i in range(2):
                a.wait_ge(self.mx_done.sem, self.mx_done.at(it, i + 1))
                for t in range(2):
                    ins = a.activation(self.Pr[:, i, t * 256:t * 256 + 256], PS[:, 6 + i, t * 256:t * 256 + 256],
                                       ACT.Exp, bias=self.nm[:, i, t:t + 1], scale=1.0,
                                       accum_out=self.ss[:, i, t:t + 1])
                ins.then_inc(self.e_done.sem, 1)
            for i in range(2):
                a.wait_ge(self.o_done.sem, self.o_done.at(it, i + 1))
                a.activation(self.O[:, i, :], PS[:, 2 + i, 0:256], ACT.Copy).then_inc(self.o_ev.sem, 1)
            a.wait_ge(self.g_done.sem, self.g_done.at(it, 1))
            a.activation(self.G, PS[:, 4, 0:256], ACT.Exp, bias=self.nb, scale=-1.0).then_inc(self.g_exp.sem, 1)

    def vector(self, v):
        c, PS = self.c, self.c.PS

        def link(ins):
            c.dve.link(v, ins)

        link(v.tensor_scalar(self.nb, self.nbg, -1.0, None, ALU.mult))
        v.wait_ge(self.x_ready.sem, self.x_ready.at(0, 2))
        with v.Fori(0, B) as it:
            c.dve.enter(it)
            for i in range(2):
                v.wait_ge(self.qk_done.sem, self.qk_done.at(it, 2 * i + 1))
                v.tensor_scalar(self.Q[:, i, :], PS[:, 2 * i, 0:256], self.bq[:, i:i + 1], float(P) ** -0.5,
                                ALU.add, ALU.mult).then_inc(self.q_ev.sem, 1)
            for i in range(2):
                v.wait_ge(self.v_done.sem, self.v_done.at(it, i + 1))
                v.tensor_tensor(self.V[:, i, :, :], two(PS[:, 4 + i, 0:256]),
                                self.bv[:, i, :].unsqueeze(1).to_broadcast([P, 2, P]), ALU.add)\
                    .then_inc(self.v_ev.sem, 1)
            for i in range(2):
                v.wait_ge(self.s_done.sem, self.s_done.at(it, i + 1))
                v.tensor_reduce(self.nm[:, i, :], two(PS[:, 6 + i, :]), AX.X, ALU.max, negate=True)\
                    .then_inc(self.mx_done.sem, 1)
            for i in range(2):
                v.wait_ge(self.e_done.sem, self.e_done.at(it, i + 1))
                link(v.reciprocal(self.ri[:, i, :], self.ss[:, i, :]))
                p = two(self.Pr[:, i, :])
                v.tensor_tensor(p, p, self.ri[:, i, :].unsqueeze(2).to_broadcast([P, 2, 256]), ALU.mult)\
                    .then_inc(self.pn_done.sem, 1)
            for i in range(2):
                v.wait_ge(self.t_done.sem, self.t_done.at(it, i + 1))
                v.tensor_copy(self.PT[:, i, :], PS[:, i, :]).then_inc(self.pt_ev.sem, 1)
            v.wait_ge(self.o_ev.sem, self.o_ev.at(it, 2))
            link(v.tensor_tensor(self.D, self.O[:, 0, :], self.O[:, 1, :], ALU.subtract))
            v.wait_ge(self.g_exp.sem, self.g_exp.at(it, 1))
            link(v.tensor_scalar(self.G, self.G, 1.0, None, ALU.add))
            link(v.reciprocal(self.G, self.G))
            link(v.tensor_tensor(self.D, self.D, self.G, ALU.mult))
            v.tensor_tensor(self.Y, self.D, self.O[:, 1, :], ALU.add).then_inc(self.y_ready.sem, 1)
            v.wait_ge(self.y_done.sem, self.y_done.at(it, 1))
            v.tensor_tensor(c.Z[:, bass.ds(it * 2, 2), :], two(PS[:, 7, 0:256]), c.X[:, bass.ds(it * 2, 2), :],
                            ALU.add).then_inc(self.z_ready.sem, 1)
        c.dve.leave(B)
        v.wait_ge(self.z_ready.sem, self.z_ready.at(B - 1, 1))

    def gpsimd(self, g):
        pass


WIN_Q, WINDOWS = 96, ((0, 0), (96, 80), (160, 128))


def window_tables():
    i, j = np.arange(WIN_Q)[:, None], np.arange(P)[None, :]
    rel = np.stack([(q0 + i) - (k0 + j) for q0, k0 in WINDOWS], 1).astype(np.float32)
    return rel, np.where(np.abs(rel) <= 16, 0.0, NEG).astype(np.float32)


class BandedAttention:

    H = 16

    def __init__(self, c, wq, wk, wv, wo, slopes, rel, band, headmask):
        self.c, self.wq, self.wk, self.wv, self.wo = c, wq, wk, wv, wo
        self.slopes, self.rel, self.band, self.headmask = slopes, rel, band, headmask
        self.x_ready = c.x_ready
        s = c.sig
        self.src_ready = s("src_ready", 1)
        self.k_done, self.k_ev = s("kp_done", 1), s("k_ev", 1)
        self.q_done, self.q_ev = s("qp_done", 1), s("q_ev", 1)
        self.qz_ready = s("qz_ready", 4)
        self.v_done, self.v_ev = s("vp_done", 1), s("v_ev", 1)
        self.s_done = s("s_done", 16)
        self.sb_done = s("sb_done", 16)
        self.mx_done = s("mx_done", 16)
        self.e_done = s("e_done", 16)
        self.r_done = s("r_done", 16)
        self.pn_done = s("pn_done", 16)
        self.t_done = s("t_done", 16)
        self.pt_ev = s("pt_ev", 16)
        self.o_done = s("o_done", 4)
        self.o_ev = s("o_ev", 4)
        self.y_done = s("y_done", 1)
        self.z_ready = s("z_ready", 1)
        t = c.take
        self.XB, self.KT, self.QB = t(0, 256), t(256, 256), t(512, 256)
        self.QZ = t(768, 16, 256)
        self.V = t(4864, 3, 512)
        self.bias = t(6400, 16, 384)
        self.Sb = t(12544, 2, 384)
        self.Pr = t(13312, 4, 384)
        self.PT = t(14848, 6, 288)
        self.OT = t(16576, 4, 256).rearrange("p a b -> p (a b)")
        self.nm, self.ss, self.ri = c.small[:, 0:48], c.small[:, 48:96], c.small[:, 96:144]
        self.nm, self.ss, self.ri = (a.rearrange("p (h w) -> p h w", w=3) for a in (self.nm, self.ss, self.ri))

    def tensor(self, pe):
        c, PS = self.c, self.c.PS
        with pe.Fori(0, B) as it:
            pe.wait_ge(self.src_ready.sem, self.src_ready.at(it, 1))
            pe.matmul(PS[:, 4, 0:256], self.wk, self.XB, start=True, stop=True).then_inc(self.k_done.sem, 1)
            pe.matmul(PS[:, 5, 0:256], self.wq, self.XB, start=True, stop=True).then_inc(self.q_done.sem, 1)
            pe.wait_ge(self.k_ev.sem, self.k_ev.at(it, 1))
            for w, (q0, k0) in enumerate(WINDOWS):
                ins = pe.matmul(PS[:, 4, w * P:(w + 1) * P], self.XB[:, k0:k0 + P], self.wv, start=True, stop=True)
            ins.then_inc(self.v_done.sem, 1)

            def scores(h):
                if h % 4 == 0:
                    pe.wait_ge(self.qz_ready.sem, self.qz_ready.at(it, h // 4 + 1))
                if h >= 2:
                    pe.wait_ge(self.sb_done.sem, self.sb_done.at(it, h - 1))
                for w, (q0, k0) in enumerate(WINDOWS):
                    ins = pe.matmul(PS[0:WIN_Q, h % 2, w * P:(w + 1) * P], self.QZ[:, h, q0:q0 + WIN_Q],
                                    self.KT[:, k0:k0 + P], start=True, stop=True)
                ins.then_inc(self.s_done.sem, 1)

            def transposes(h):
                pe.wait_ge(self.pn_done.sem, self.pn_done.at(it, h + 1))
                if h >= 2:
                    pe.wait_ge(self.pt_ev.sem, self.pt_ev.at(it, h - 1))
                for w in range(3):
                    ins = pe.transpose(PS[:, 2 + h % 2, w * WIN_Q:(w + 1) * WIN_Q],
                                       self.Pr[0:WIN_Q, h % 4, w * P:(w + 1) * P], c.ident[0:WIN_Q, 0:WIN_Q])
                ins.then_inc(self.t_done.sem, 1)

            def values(k):
                pe.wait_ge(self.pt_ev.sem, self.pt_ev.at(it, 4 * k + 4))
                if k == 0:
                    pe.wait_ge(self.v_ev.sem, self.v_ev.at(it, 1))
                if k >= 2:
                    pe.wait_ge(self.o_ev.sem, self.o_ev.at(it, k - 1))
                for w in (2, 1, 0):
                    q0 = WINDOWS[w][0]
                    for r in range(4):
                        h = 4 * k + r
                        ins = pe.matmul(PS[32 * r:32 * r + 32, 6 + k % 2, q0:q0 + WIN_Q],
                                        self.V[:, w, 32 * h:32 * h + 32], self.PT[:, h % 6, w * WIN_Q:(w + 1) * WIN_Q],
                                        start=True, stop=True, skip_group_check=True)
                ins.then_inc(self.o_done.sem, 1)

            for step in range(self.H + 6):
                if step < self.H:
                    scores(step)
                if 3 <= step < self.H + 3:
                    transposes(step - 3)
                h = step - 4
                if 0 <= h < self.H and h % 4 == 3:
                    values(h // 4)
            pe.wait_ge(self.o_ev.sem, self.o_ev.at(it, 4))
            for t in range(2):
                for k in range(4):
                    ins = pe.matmul(PS[:, 0, t * P:(t + 1) * P], self.OT[:, k * 256 + t * P:k * 256 + (t + 1) * P],
                                    self.wo[:, k, :], start=(k == 0), stop=(k == 3))
            ins.then_inc(self.y_done.sem, 1)

    def scalar(self, a):
        c, PS = self.c, self.c.PS
        a.wait_ge(self.x_ready.sem, self.x_ready.at(0, 2))
        with a.Fori(0, B) as it:
            a.activation(self.XB, c.XT[:, bass.ds(it * S, S)], ACT.Copy).then_inc(self.src_ready.sem, 1)
            a.wait_ge(self.k_done.sem, self.k_done.at(it, 1))
            a.activation(self.KT, PS[:, 4, 0:256], ACT.Copy).then_inc(self.k_ev.sem, 1)

            def exps(h):
                a.wait_ge(self.mx_done.sem, self.mx_done.at(it, h + 1))
                if h >= 4:
                    a.wait_ge(self.t_done.sem, self.t_done.at(it, h - 3))
                for w in range(3):
                    s = slice(w * P, (w + 1) * P)
                    ins = a.activation(self.Pr[0:WIN_Q, h % 4, s], self.Sb[0:WIN_Q, h % 2, s], ACT.Exp,
                                       bias=self.nm[0:WIN_Q, h, w:w + 1], scale=1.0,
                                       accum_out=self.ss[0:WIN_Q, h, w:w + 1])
                ins.then_inc(self.e_done.sem, 1)

            def spread(h):
                a.wait_ge(self.t_done.sem, self.t_done.at(it, h + 1))
                if h >= 6:
                    a.wait_ge(self.o_done.sem, self.o_done.at(it, (h - 6) // 4 + 1))
                a.activation(self.PT[:, h % 6, :], PS[:, 2 + h % 2, 0:288], ACT.Copy).then_inc(self.pt_ev.sem, 1)

            for step in range(self.H + 6):
                if step < self.H:
                    exps(step)
                if 3 <= step < self.H + 3:
                    spread(step - 3)

    def vector(self, v):
        c, PS = self.c, self.c.PS
        ins = v.memset(self.V, 0.0)
        c.dve.link(v, ins)
        for h in range(self.H):
            ins = v.scalar_tensor_tensor(self.bias[0:WIN_Q, h, :], self.rel, self.slopes[0:WIN_Q, h:h + 1], self.band,
                                         ALU.mult, ALU.add)
        c.dve.link(v, ins)
        v.wait_ge(self.x_ready.sem, self.x_ready.at(0, 2))
        with v.Fori(0, B) as it:
            c.dve.enter(it)
            v.wait_ge(self.q_done.sem, self.q_done.at(it, 1))
            v.tensor_scalar(self.QB, PS[:, 5, 0:256], 8.0 ** -0.5, None, ALU.mult).then_inc(self.q_ev.sem, 1)
            v.wait_ge(self.v_done.sem, self.v_done.at(it, 1))
            for w in range(3):
                dst = self.V[:, w, :].rearrange("p (h e) -> p h e", e=32)[:, :, 0:8]
                ins = v.tensor_copy(dst, PS[:, 4, w * P:(w + 1) * P].rearrange("p (h e) -> p h e", e=8))
            ins.then_inc(self.v_ev.sem, 1)

            def maxima(h):
                v.wait_ge(self.s_done.sem, self.s_done.at(it, h + 1))
                if h >= 2:
                    v.wait_ge(self.e_done.sem, self.e_done.at(it, h - 1))
                v.tensor_tensor(self.Sb[0:WIN_Q, h % 2, :], PS[0:WIN_Q, h % 2, 0:384], self.bias[0:WIN_Q, h, :],
                                ALU.add).then_inc(self.sb_done.sem, 1)
                v.wait_ge(self.sb_done.sem, self.sb_done.at(it, h + 1))
                v.tensor_reduce(self.nm[0:WIN_Q, h, :], self.Sb[0:WIN_Q, h % 2, :].rearrange("p (w k) -> p w k", w=3),
                                AX.X, ALU.max, negate=True).then_inc(self.mx_done.sem, 1)

            def reciprocals(h):
                v.wait_ge(self.e_done.sem, self.e_done.at(it, h + 1))
                v.reciprocal(self.ri[0:WIN_Q, h, :], self.ss[0:WIN_Q, h, :]).then_inc(self.r_done.sem, 1)

            def out(k):
                v.wait_ge(self.o_done.sem, self.o_done.at(it, k + 1))
                v.tensor_copy(self.OT[:, k * 256:k * 256 + 256], PS[:, 6 + k % 2, 0:256]).then_inc(self.o_ev.sem, 1)

            for step in range(self.H + 6):
                if step < self.H:
                    maxima(step)
                if 1 <= step < self.H + 1:
                    reciprocals(step - 1)
                h = step - 5
                if 0 <= h < self.H and h % 4 == 3:
                    out(h // 4)
            v.wait_ge(self.y_done.sem, self.y_done.at(it, 1))
            v.tensor_tensor(c.Z[:, bass.ds(it * 2, 2), :], two(PS[:, 0, 0:256]), c.X[:, bass.ds(it * 2, 2), :],
                            ALU.add).then_inc(self.z_ready.sem, 1)
        c.dve.leave(B)
        v.wait_ge(self.z_ready.sem, self.z_ready.at(B - 1, 1))

    def gpsimd(self, g):
        with g.Fori(0, B) as it:
            g.wait_ge(self.q_ev.sem, self.q_ev.at(it, 1))
            for k in range(4):
                g.tensor_tensor(self.QZ[:, 4 * k:4 * k + 4, :], self.QB.unsqueeze(1).to_broadcast([P, 4, 256]),
                                self.headmask[:, 4 * k:4 * k + 4].unsqueeze(2).to_broadcast([P, 4, 256]),
                                ALU.mult).then_inc(self.qz_ready.sem, 1)
            for h in range(self.H):
                g.wait_ge(self.r_done.sem, self.r_done.at(it, h + 1))
                p = self.Pr[0:WIN_Q, h % 4, :].rearrange("p (w k) -> p w k", w=3)
                g.tensor_tensor(p, p, self.ri[0:WIN_Q, h, :].unsqueeze(2).to_broadcast([WIN_Q, 3, P]), ALU.mult)\
                    .then_inc(self.pn_done.sem, 1)


class FourTokenAttention:

    def __init__(self, c, win, bin_, relk, wout, bout):
        self.c, self.win, self.bin, self.relk, self.wout, self.bout = c, win, bin_, relk, wout, bout
        self.x_ready = c.x_ready
        s = c.sig
        self.p_done = s("p_done", T, 1)
        self.p_ev = s("p_ev", T, 1)
        self.kk_ready = s("kk_ready", 8, 1)
        self.kk_used = s("kk_used", 8, 1)
        self.sh_ready = s("sh_ready", 1, 1)
        self.e_ready = s("e_ready", 1, 1)
        self.ao_ready = s("ao_ready", T, 1)
        self.at_done = s("at_done", 2, 1)
        self.at_ev = s("at_ev", 2, 1)
        self.y_done = s("y_done", 2, 1)
        self.z_ready = s("z_ready", 1, 1)
        t = c.take
        self.QKV = t(0, T, 384)
        self.KK = t(3072, 2, 512)
        self.PD = t(4096, 2, 512)
        self.sc = t(5120, T, 64)
        self.mx = t(5632, T, 16)
        self.AO = t(5760, T, 128)
        self.AT = t(6784, 1024)
        self.order = [(tq, u) for tq in range(4) for u in range(2)]

    def tensor(self, pe):
        c, PS = self.c, self.c.PS
        pe.wait_ge(self.x_ready.sem, self.x_ready.at(0, 2))
        for n in range(T):
            if n >= 4:
                pe.wait_ge(self.p_ev.sem, self.p_ev.at(0, n - 3))
            pe.matmul(PS[:, 2 + n % 4, 0:384], c.XT[:, n * P:(n + 1) * P], self.win, start=True, stop=True)\
                .then_inc(self.p_done.sem, 1)
        for n in range(T):
            pe.wait_ge(self.ao_ready.sem, self.ao_ready.at(0, n + 1))
            ins = pe.transpose(PS[:, n // 4, (n % 4) * P:(n % 4) * P + P], self.AO[:, n, :], c.ident)
            if n % 4 == 3:
                ins.then_inc(self.at_done.sem, 1)
        for n in range(T):
            if n % 4 == 0:
                pe.wait_ge(self.at_ev.sem, self.at_ev.at(0, n // 4 + 1))
            ins = pe.matmul(PS[:, 6 + n // 4, (n % 4) * P:(n % 4) * P + P], self.AT[:, n * P:(n + 1) * P], self.wout,
                            start=True, stop=True)
            if n % 4 == 3:
                ins.then_inc(self.y_done.sem, 1)

    def scalar(self, a):
        c, PS = self.c, self.c.PS
        a.wait_ge(self.sh_ready.sem, self.sh_ready.at(0, 1))
        a.activation(self.sc, self.sc, ACT.Exp).then_inc(self.e_ready.sem, 1)
        for i in range(2):
            a.wait_ge(self.at_done.sem, self.at_done.at(0, i + 1))
            a.activation(self.AT[:, i * 512:(i + 1) * 512], PS[:, i, :], ACT.Copy).then_inc(self.at_ev.sem, 1)

    def gpsimd(self, g):
        g.wait_ge(self.p_ev.sem, self.p_ev.at(0, T))
        for i, (tq, u) in enumerate(self.order):
            if i >= 2:
                g.wait_ge(self.kk_used.sem, self.kk_used.at(0, i - 1))
            g.tensor_tensor(self.KK[:, i % 2, :].rearrange("p (s f) -> p s f", s=4), self.QKV[:, u:T:2, 128:256],
                            self.relk[:, 3 - tq:7 - tq, :], ALU.add).then_inc(self.kk_ready.sem, 1)

    def vector(self, v):
        c, PS = self.c, self.c.PS

        def link(ins):
            c.dve.link(v, ins)

        for n in range(T):
            v.wait_ge(self.p_done.sem, self.p_done.at(0, n + 1))
            v.tensor_tensor(self.QKV[:, n, :], PS[:, 2 + n % 4, 0:384], self.bin, ALU.add).then_inc(self.p_ev.sem, 1)
        v.wait_ge(self.p_ev.sem, self.p_ev.at(0, T))
        link(v.tensor_scalar(self.QKV[:, :, 0:128], self.QKV[:, :, 0:128], 8.0 ** -0.5, None, ALU.mult))
        for i, (tq, u) in enumerate(self.order):
            n = 2 * tq + u
            v.wait_ge(self.kk_ready.sem, self.kk_ready.at(0, i + 1))
            q = self.QKV[:, n, 0:128].unsqueeze(1).to_broadcast([P, 4, P])
            pd = self.PD[:, i % 2, :]
            v.tensor_tensor(pd.rearrange("p (s f) -> p s f", s=4), self.KK[:, i % 2, :].rearrange("p (s f) -> p s f", s=4),
                            q, ALU.mult).then_inc(self.kk_used.sem, 1)
            v.wait_ge(self.kk_used.sem, self.kk_used.at(0, i + 1))
            ins = v.tensor_reduce(self.sc[:, n, :], pd.rearrange("p (g d) -> p g d", d=8), AX.X, ALU.add)
            if i % 2:
                link(ins)
        by_head = self.sc.rearrange("p n (s h) -> p n h s", s=4)
        by_key = self.sc.rearrange("p n (s h) -> p n s h", s=4)
        link(v.tensor_reduce(self.mx, by_head, AX.X, ALU.max))
        for n in range(T):
            ins = v.tensor_tensor(by_key[:, n], by_key[:, n], self.mx[:, n, :].unsqueeze(1).to_broadcast([P, 4, 16]),
                                  ALU.subtract)
        ins.then_inc(self.sh_ready.sem, 1)
        v.wait_ge(self.e_ready.sem, self.e_ready.at(0, 1))
        link(v.tensor_reduce(self.mx, by_head, AX.X, ALU.add))
        link(v.reciprocal(self.mx, self.mx))
        for n in range(T):
            ins = v.tensor_tensor(by_key[:, n], by_key[:, n], self.mx[:, n, :].unsqueeze(1).to_broadcast([P, 4, 16]),
                                  ALU.mult)
        link(ins)
        for n in range(T):
            pd = self.PD[:, n % 2, :].rearrange("p (s h d) -> p s h d", s=4, h=16)
            for s in range(4):
                val = self.QKV[:, 2 * s + n % 2, 256:384].rearrange("p (h d) -> p h d", d=8)
                p = by_key[:, n, s, :].unsqueeze(2).to_broadcast([P, 16, 8])
                ins = v.tensor_tensor(pd[:, s], val, p, ALU.mult)
            link(ins)
            v.tensor_reduce(self.AO[:, n, :], self.PD[:, n % 2, :].rearrange("p (s f) -> p f s", s=4), AX.X, ALU.add)\
                .then_inc(self.ao_ready.sem, 1)
            if n >= 1:
                v.wait_ge(self.ao_ready.sem, self.ao_ready.at(0, n))
        for i in range(2):
            v.wait_ge(self.y_done.sem, self.y_done.at(0, i + 1))
            z = c.Z[:, 4 * i:4 * i + 4, :]
            y = PS[:, 6 + i, :].rearrange("p (t f) -> p t f", t=4)
            link(v.tensor_tensor(z, y, c.X[:, 4 * i:4 * i + 4, :], ALU.add))
            ins = v.tensor_tensor(z, z, self.bout.unsqueeze(1).to_broadcast([P, 4, P]), ALU.add)
        ins.then_inc(self.z_ready.sem, 1)
        v.wait_ge(self.z_ready.sem, self.z_ready.at(0, 1))


class Mamba:

    N = 16

    def __init__(self, c, g, b, win, cw, cb, wdt_in, wbc, wdt, bdt, alog, Dv, wout, onehot):
        self.c, self.g, self.b, self.win, self.cw, self.cb = c, g, b, win, cw, cb
        self.wdt_in, self.wbc, self.wdt, self.bdt, self.alog, self.Dv = wdt_in, wbc, wdt, bdt, alog, Dv
        self.wout, self.onehot = wout, onehot
        self.x_ready = c.x_ready
        s = c.sig
        N = self.N
        self.var_ready, self.sd_ready = s("var_ready", 1, 1), s("sd_ready", 1, 1)
        self.xn_ready = s("xn_ready", T, 1)
        self.xn_done = s("xn_done", 2, 1)
        self.xn_ev = s("xn_ev", 2, 1)
        self.a_ready = s("a_ready", 1, 1)
        self.uz_done = s("uz_done", 4)
        self.u_ev = s("u_ev", 2)
        self.z_ev = s("z_ev", 1)
        self.uc_ready = s("uc_ready", 2)
        self.us_ready = s("us_ready", 2)
        self.dbc_done = s("dbc_done", 2)
        self.dti_ev = s("dti_ev", 1)
        self.bc_ready = s("bc_ready", 1)
        self.dt_done = s("dt_done", 2)
        self.dtx_ready = s("dtx_ready", 2)
        self.sp_ready = s("sp_ready", 1)
        self.dt_ready = s("dt_ready", 1)
        self.da_ready = s("da_ready", N)
        self.b_done = s("b_done", N)
        self.c_done = s("c_done", N)
        self.db_ready = s("db_ready", N)
        self.sc_ready = s("sc_ready", N)
        self.hc_ready = s("hc_ready", N)
        self.acc_ready = s("acc_ready", N)
        self.yg_ready = s("yg_ready", 1)
        self.y_done = s("y_done", 1)
        self.z_ready = s("z_ready", 1)
        t = c.take
        self.XN = t(0, T, P)
        self.XNT = t(1024, 1024)
        self.A = t(2048, 32)
        self.up = t(2080, 2, 259)
        self.uc = t(2600, 2, 256)
        self.u = t(3112, 2, 256)
        self.sz = t(3624, 2, 256)
        self.dti = t(4136, 256)
        self.r = t(4392, 256)
        self.BC = t(4648, 128).bitcast(BF16)
        self.dx = t(4776, 2, 256)
        self.ab = t(5288, 2, 256)
        self.dt = t(5800, 2, 256)
        self.dtu = t(6312, 2, 256)
        self.dA = t(6824, 3, 512)
        self.dB = t(8360, 2, 512)
        self.h = t(9384, 2, 512)
        self.hC = t(10408, 3, 512)
        self.acc = t(11944, 2, 256)
        self.y = t(12456, 2, 256)
        self.yD = t(12968, 2, 256)
        self.e1 = t(13480, 2, 256)
        self.lw = t(13992, 2, 256)

    def tensor(self, pe):
        c, PS = self.c, self.c.PS
        pe.wait_ge(self.x_ready.sem, self.x_ready.at(0, 2))
        for n in range(T):
            pe.wait_ge(self.xn_ready.sem, self.xn_ready.at(0, n + 1))
            ins = pe.transpose(PS[:, n // 4, (n % 4) * P:(n % 4) * P + P], self.XN[:, n, :], c.ident)
            if n % 4 == 3:
                ins.then_inc(self.xn_done.sem, 1)
        pe.wait_ge(self.xn_ev.sem, self.xn_ev.at(0, 2))
        with pe.Fori(0, B) as it:
            x = self.XNT[:, bass.ds(it * S, S)]
            for j in range(4):
                if j == 3:
                    pe.wait_ge(self.u_ev.sem, self.u_ev.at(it, 1))
                dst = PS[:, min(j, 2), (256 if j == 3 else 0):(512 if j == 3 else 256)]
                pe.matmul(dst, self.win[:, j * P:(j + 1) * P], x, start=True, stop=True, skip_group_check=True)\
                    .then_inc(self.uz_done.sem, 1)
            for j in range(2):
                pe.wait_ge(self.us_ready.sem, self.us_ready.at(it, j + 1))
                ins = pe.matmul(PS[0:8, 3, 0:256], self.wdt_in[:, j, :], self.u[:, j, :], start=(j == 0), stop=(j == 1))
            ins.then_inc(self.dbc_done.sem, 1)
            for j in range(2):
                ins = pe.matmul(PS[0:96, 4, 0:256], self.wbc[:, j, :], self.u[:, j, :], start=(j == 0), stop=(j == 1))
            ins.then_inc(self.dbc_done.sem, 1)
            pe.wait_ge(self.dti_ev.sem, self.dti_ev.at(it, 1))
            for j in range(2):
                pe.matmul(PS[:, j, 0:256], self.wdt[0:8, j * P:(j + 1) * P], self.dti[0:8, :], start=True, stop=True)\
                    .then_inc(self.dt_done.sem, 1)
            pe.wait_ge(self.bc_ready.sem, self.bc_ready.at(it, 1))
            for n in range(self.N):
                if n >= 2:
                    pe.wait_ge(self.db_ready.sem, self.db_ready.at(it, n - 1))
                pe.matmul(PS[:, 4 + n % 2, 0:256], self.onehot[0:96, n:n + 1].to_broadcast([96, P]), self.BC[0:96, :],
                          start=True, stop=True).then_inc(self.b_done.sem, 1)
                if n >= 2:
                    pe.wait_ge(self.hc_ready.sem, self.hc_ready.at(it, n - 1))
                pe.matmul(PS[:, 6 + n % 2, 0:256], self.onehot[0:96, 16 + n:17 + n].to_broadcast([96, P]),
                          self.BC[0:96, :], start=True, stop=True).then_inc(self.c_done.sem, 1)
            pe.wait_ge(self.yg_ready.sem, self.yg_ready.at(it, 1))
            for t in range(2):
                for j in range(2):
                    ins = pe.matmul(PS[:, 3, t * P:(t + 1) * P], self.y[:, j, t * P:(t + 1) * P], self.wout[:, j, :],
                                    start=(j == 0), stop=(j == 1))
            ins.then_inc(self.y_done.sem, 1)

    def scalar(self, a):
        c, PS = self.c, self.c.PS

        def link(ins):
            c.act.link(a, ins)

        a.activation(self.A, self.alog, ACT.Exp).then_inc(self.a_ready.sem, 1)
        a.wait_ge(self.var_ready.sem, self.var_ready.at(0, 1))
        a.activation(c.sd[:, :], c.mv[:, :, 1], ACT.Sqrt, bias=c.eps, scale=1.0).then_inc(self.sd_ready.sem, 1)
        for i in range(2):
            a.wait_ge(self.xn_done.sem, self.xn_done.at(0, i + 1))
            a.activation(self.XNT[:, i * 512:(i + 1) * 512], PS[:, i, :], ACT.Identity, bias=self.b, scale=self.g)\
                .then_inc(self.xn_ev.sem, 1)
        with a.Fori(0, B) as it:
            c.act.enter(it)
            for j in range(2):
                a.wait_ge(self.uz_done.sem, self.uz_done.at(it, j + 1))
                a.activation(self.up[:, j, 3:259], PS[:, j, 0:256], ACT.Copy).then_inc(self.u_ev.sem, 1)
            a.wait_ge(self.uz_done.sem, self.uz_done.at(it, 4))
            a.activation(self.sz, two(PS[:, 2, :]), ACT.Silu).then_inc(self.z_ev.sem, 1)
            for j in range(2):
                a.wait_ge(self.uc_ready.sem, self.uc_ready.at(it, j + 1))
                a.activation(self.u[:, j, :], self.uc[:, j, :], ACT.Silu).then_inc(self.us_ready.sem, 1)
            a.wait_ge(self.dbc_done.sem, self.dbc_done.at(it, 1))
            a.activation(self.dti[0:8, :], PS[0:8, 3, 0:256], ACT.Copy).then_inc(self.dti_ev.sem, 1)
            a.wait_ge(self.dtx_ready.sem, self.dtx_ready.at(it, 2))
            link(a.activation(self.ab, self.dx, ACT.Abs))
            link(a.activation(self.ab, self.ab, ACT.Exp, scale=-1.0))
            link(a.activation(self.e1, self.ab, ACT.Identity, bias=self.c.one, scale=1.0))
            a.activation(self.lw, self.e1, ACT.Ln).then_inc(self.sp_ready.sem, 1)
            a.wait_ge(self.dt_ready.sem, self.dt_ready.at(it, 1))
            for n in range(self.N):
                if n >= 3:
                    a.wait_ge(self.sc_ready.sem, self.sc_ready.at(it, n - 2))
                d = two(self.dA[:, n % 3, :])
                for j in range(2):
                    ins = a.activation(d[:, j, 1:256], self.dt[:, j, 1:256], ACT.Exp,
                                       scale=self.A[:, j * 16 + n:j * 16 + n + 1])
                ins.then_inc(self.da_ready.sem, 1)
        c.act.leave(B)

    def vector(self, v):
        c, PS = self.c, self.c.PS

        def link(ins):
            c.dve.link(v, ins)

        v.memset(self.dA, 0.0)
        link(v.memset(self.up, 0.0))
        v.wait_ge(self.a_ready.sem, self.a_ready.at(0, 1))
        link(v.tensor_scalar(self.A, self.A, -1.0, None, ALU.mult))
        for n in range(T):
            ins = v.bn_stats(c.bn[:, n, :], c.X[:, n, :])
        link(ins)
        for n in range(T):
            ins = v.bn_aggr(c.mv[:, n, :], c.bn[:, n, :])
        ins.then_inc(self.var_ready.sem, 1)
        v.wait_ge(self.sd_ready.sem, self.sd_ready.at(0, 1))
        link(v.reciprocal(c.rs[:, :], c.sd[:, :]))
        refine(link, v, c.rs[:, :], c.mv[:, :, 1], EPS, c.rt[:, :])
        for n in range(T):
            v.tensor_scalar(self.XN[:, n, :], c.X[:, n, :], c.mv[:, n, 0:1], c.rs[:, n:n + 1],
                            ALU.subtract, ALU.mult).then_inc(self.xn_ready.sem, 1)
        with v.Fori(0, B) as it:
            c.dve.enter(it)
            for j in range(2):
                v.wait_ge(self.u_ev.sem, self.u_ev.at(it, j + 1))
                up, uc = self.up[:, j, :], self.uc[:, j, :]
                link(v.tensor_scalar(uc, up[:, 0:256], self.cw[:, j, 0:1], self.cb[:, j:j + 1], ALU.mult, ALU.add))
                for k in range(1, 4):
                    ins = v.scalar_tensor_tensor(uc, up[:, k:k + 256], self.cw[:, j, k:k + 1], uc, ALU.mult, ALU.add)
                    if k < 3:
                        link(ins)
                ins.then_inc(self.uc_ready.sem, 1)
            v.wait_ge(self.dbc_done.sem, self.dbc_done.at(it, 2))
            bc = PS[:, 4, 0:256]
            link(v.tensor_copy(self.BC[0:96, :], bc[0:96]))
            for k in (1, 2):
                s = slice(32 * k, 32 * k + 32)
                link(v.tensor_tensor(self.r[s, :], bc[s], self.BC[s, :], ALU.subtract))
                link(v.tensor_copy(self.BC[s, :], self.r[s, :]))
            s = slice(64, 96)
            link(v.tensor_tensor(self.r[s, :], self.r[s, :], self.BC[s, :], ALU.subtract))
            v.tensor_copy(self.BC[s, :], self.r[s, :]).then_inc(self.bc_ready.sem, 1)
            for j in range(2):
                v.wait_ge(self.dt_done.sem, self.dt_done.at(it, j + 1))
                v.tensor_scalar(self.dx[:, j, :], PS[:, j, 0:256], self.bdt[:, j:j + 1], None, ALU.add)\
                    .then_inc(self.dtx_ready.sem, 1)
            v.wait_ge(self.sp_ready.sem, self.sp_ready.at(it, 1))
            link(v.tensor_scalar(self.e1, self.e1, 1.0, None, ALU.subtract))
            link(v.tensor_tensor(self.e1, self.ab, self.e1, ALU.subtract))
            link(v.tensor_tensor(self.e1, self.lw, self.e1, ALU.add))
            v.scalar_tensor_tensor(self.dt, self.dx, 0.0, self.e1, ALU.max, ALU.add).then_inc(self.dt_ready.sem, 1)
            v.wait_ge(self.dt_ready.sem, self.dt_ready.at(it, 1))
            v.tensor_tensor(self.dtu, self.dt, self.u, ALU.mult)
            for j in range(2):
                ins = v.tensor_scalar(self.yD[:, j, :], self.u[:, j, :], self.Dv[:, j:j + 1], None, ALU.mult)
            link(ins)

            def inputs(n):
                v.wait_ge(self.b_done.sem, self.b_done.at(it, n + 1))
                b = PS[:, 4 + n % 2, 0:256].unsqueeze(1).to_broadcast([P, 2, 256])
                v.tensor_tensor(two(self.dB[:, n % 2, :]), self.dtu, b, ALU.mult).then_inc(self.db_ready.sem, 1)

            def scan(n):
                v.wait_ge(self.da_ready.sem, self.da_ready.at(it, n + 1))
                v.wait_ge(self.db_ready.sem, self.db_ready.at(it, n + 1))
                v.tensor_tensor_scan(self.h[:, n % 2, :], self.dA[:, n % 3, :], self.dB[:, n % 2, :], 0.0,
                                     ALU.mult, ALU.add).then_inc(self.sc_ready.sem, 1)

            def outputs(n):
                v.wait_ge(self.sc_ready.sem, self.sc_ready.at(it, n + 1))
                v.wait_ge(self.c_done.sem, self.c_done.at(it, n + 1))
                if n >= 3:
                    v.wait_ge(self.acc_ready.sem, self.acc_ready.at(it, n - 2))
                cc = PS[:, 6 + n % 2, 0:256].unsqueeze(1).to_broadcast([P, 2, 256])
                v.tensor_tensor(two(self.hC[:, n % 3, :]), two(self.h[:, n % 2, :]), cc, ALU.mult)\
                    .then_inc(self.hc_ready.sem, 1)

            for n in range(self.N + 1):
                if n < self.N:
                    inputs(n)
                    scan(n)
                if n >= 1:
                    outputs(n - 1)
            v.wait_ge(self.acc_ready.sem, self.acc_ready.at(it, self.N))
            v.wait_ge(self.z_ev.sem, self.z_ev.at(it, 1))
            v.tensor_tensor(self.y, self.acc, self.sz, ALU.mult).then_inc(self.yg_ready.sem, 1)
            v.wait_ge(self.y_done.sem, self.y_done.at(it, 1))
            z, x = c.Z[:, bass.ds(it * 2, 2), :], c.X[:, bass.ds(it * 2, 2), :]
            link(v.tensor_tensor(z, two(PS[:, 3, 0:256]), x, ALU.add))
            v.tensor_tensor(z, z, x, ALU.add).then_inc(self.z_ready.sem, 1)
        c.dve.leave(B)
        v.wait_ge(self.z_ready.sem, self.z_ready.at(B - 1, 1))

    def gpsimd(self, g):
        with g.Fori(0, B) as it:
            for n in range(self.N):
                g.wait_ge(self.hc_ready.sem, self.hc_ready.at(it, n + 1))
                acc, hc = self.acc.rearrange("p a b -> p (a b)"), self.hC[:, n % 3, :]
                if n == 0:
                    ins = g.tensor_tensor(acc, hc, self.yD.rearrange("p a b -> p (a b)"), ALU.add)
                else:
                    g.wait_ge(self.acc_ready.sem, self.acc_ready.at(it, n))
                    ins = g.tensor_tensor(acc, acc, hc, ALU.add)
                ins.then_inc(self.acc_ready.sem, 1)


def rotary_tables():
    f = np.float32
    half = np.arange(0, 64, 2, dtype=f)
    inv = (f(1.0) / f(10000.0) ** (half / f(64))).astype(f)
    t = np.arange(S, dtype=f)
    fr = t[:, None] * inv[None, :]
    fr = np.concatenate([fr, fr], -1).astype(f)
    base = ((half + f(0.4 * 64)) / f(1.4 * 64)).astype(f)
    power = ((t - S // 2) / f(32.0)).astype(f)
    scale = (base[None, :] ** power[:, None]).astype(f)
    scale = np.concatenate([scale, scale], -1)
    cos, sin = np.cos(fr).astype(f), np.sin(fr).astype(f)
    sin[:, 0:32] *= -1
    return np.stack([cos * scale * 8, sin * scale * 8, cos / scale, sin / scale], 1).astype(f)


def local_masks():
    i, j = np.arange(64)[:, None], np.arange(P)[None, :]
    first = np.where(j <= i, 0.0, NEG)
    later = np.where((j <= i + 64) & (j >= i), 0.0, NEG)
    m = np.stack([first, later, later, later], 1)
    return np.concatenate([m, m], 0).astype(np.float32)


class LocalLayer:

    KEYS = (0, 0, 64, 128)
    HID = (P, P, 85)

    def __init__(self, c, depth, wqkv, qs, ks, wo, lg, lb, w1, b1, w2, w2r, b2, tables, maskb):
        self.c, self.depth = c, depth
        self.wqkv, self.qs, self.ks, self.wo, self.lg, self.lb = wqkv, qs, ks, wo, lg, lb
        self.w1, self.b1, self.w2, self.w2r, self.b2, self.tables, self.maskb = w1, b1, w2, w2r, b2, tables, maskb
        self.x_ready = c.x_ready
        s = c.sig
        self.h_ready = s("h_ready", 1)
        self.mask_ready = s("mask_ready", 1, 1)
        self.p_done = s("p_done", 7)
        self.sq_done = s("sq_done", 4)
        self.ab_done = s("ab_done", 4)
        self.qk_sum = s("qk_sum", 4)
        self.ssq_used = s("ssq_used", 4)
        self.sum_ready = s("sum_ready", 1)
        self.nrm_ready = s("nrm_ready", 1)
        self.inv_ready = s("inv_ready", 1)
        self.qk_ready = s("qk_ready", 4)
        self.v_ev = s("v_ev", 3)
        self.tr_done = s("tr_done", 4)
        self.tr_ev = s("tr_ev", 4)
        self.s_done = s("s_done", 4)
        self.mx_done = s("mx_done", 4)
        self.e_done = s("e_done", 4)
        self.r_done = s("r_done", 4)
        self.pn_done = s("pn_done", 4)
        self.t_done = s("t_done", 4)
        self.pt_ev = s("pt_ev", 4)
        self.o_done = s("o_done", 4)
        self.o_ev = s("o_ev", 4)
        self.y_done = s("y_done", 1)
        self.x1_ready = s("x1_ready", 1)
        self.x1t_done = s("x1t_done", 1)
        self.h2_ready = s("h2_ready", 1)
        self.h2_done = s("h2_done", 1)
        self.var_ready = s("var_ready", 1)
        self.sd_ready = s("sd_ready", 1)
        self.n_ready = s("n_ready", 1)
        self.n_done = s("n_done", 1)
        self.n_ev = s("n_ev", 1)
        self.ag_done = s("ag_done", 6)
        self.g_ready = s("g_ready", 3)
        self.hid_ready = s("hid_ready", 3)
        self.f_done = s("f_done", 1)
        self.z_ready = s("z_ready" if depth else "x2_ready", 1)
        self.x2t_done = None if depth else s("x2t_done", 1)
        self.out_ready = None if depth else s("out_ready", 1)
        t = c.take
        self.XI, self.XIT = t(0, T, P), t(1024, 1024)
        self.Hs = t(2048, 256)
        self.tab = t(2304, 2, 256)
        self.SQ = t(2816, 512)
        self.ssq = t(3328, 4, 8)
        self.inv = t(3360, 4, 8)
        self.nrm = c.small[:, 96:128].rearrange("p (i h) -> p i h", h=8)
        self.nrt = c.small[:, 128:160].rearrange("p (i h) -> p i h", h=8)
        self.QA = t(3400, 4, 512)
        self.QB = t(5448, 2, 512)
        self.QZ = t(6472, 8, 256)
        self.KT = t(8520, 4, 256)
        self.V = t(9544, 3, 512)
        self.Pr = t(11080, 2, 512)
        self.PT = t(12104, 2, 512)
        self.OT = t(13128, 4, 256)
        self.X1 = t(14152, 2, 128)
        self.H2 = t(14408, 256)
        self.HN = t(14664, 2, 128)
        self.HNT = t(14920, 256)
        self.GE = t(15176, 2, 256)
        self.HD = t(15688, 3, 256)
        self.MBK = t(16456, 256).bitcast(BF16)
        self.nm, self.ss, self.ri = (c.small[:, 16 * i:16 * i + 16].rearrange("p (c w) -> p c w", w=4) for i in range(3))
        self.st, self.mv2, self.sd2, self.rs2 = c.small[:, 64:76], c.small[:, 80:84], c.small[:, 84:86], c.small[:, 86:88]

    def source(self, it):
        c = self.c
        if self.depth == 0:
            return c.X[:, bass.ds(it * 2, 2), :], c.XT
        return self.XI[:, bass.ds(it * 2, 2), :], self.XIT

    def tensor(self, pe):
        c, PS = self.c, self.c.PS
        pe.wait_ge(self.mask_ready.sem, self.mask_ready.at(0, 1))
        with pe.Fori(0, B) as it:
            pe.wait_ge(self.h_ready.sem, self.h_ready.at(it, 1))
            for t in range(2):
                for j in range(2):
                    pe.matmul(PS[:, 2 * t + j, :], self.Hs[:, t * P:(t + 1) * P], self.wqkv[:, j * 512:(j + 1) * 512],
                              start=True, stop=True).then_inc(self.p_done.sem, 1)
            if self.depth:
                pe.wait_ge(self.z_ready.sem, self.z_ready.at(it, 0))
            for w, k0 in enumerate((0, 64, 128)):
                pe.matmul(PS[:, 4 + w, :], self.Hs[:, k0:k0 + P], self.wqkv[:, 1024:1536], start=True, stop=True)\
                    .then_inc(self.p_done.sem, 1)
            pe.wait_ge(self.v_ev.sem, self.v_ev.at(it, 3))
            for i in range(4):
                pe.wait_ge(self.qk_ready.sem, self.qk_ready.at(it, i + 1))
                for k in range(4):
                    ins = pe.transpose(PS[:, 4 + i, k * P:(k + 1) * P], self.QA[:, i, k * P:(k + 1) * P], c.ident)
                ins.then_inc(self.tr_done.sem, 1)
            pe.wait_ge(self.tr_ev.sem, self.tr_ev.at(it, 4))

            def scores(k):
                if k >= 2:
                    pe.wait_ge(self.e_done.sem, self.e_done.at(it, k - 1))
                pe.matmul(PS[:, k % 2, :], c.IDB[:, :], self.MBK, start=True, stop=False, skip_group_check=True)
                for w in range(4):
                    for r in range(2):
                        ins = pe.matmul(PS[64 * r:64 * r + 64, k % 2, w * P:(w + 1) * P],
                                        self.QZ[:, 2 * k + r, w * 64:w * 64 + 64],
                                        self.KT[:, k, self.KEYS[w]:self.KEYS[w] + P],
                                        start=False, stop=True, skip_group_check=True)
                ins.then_inc(self.s_done.sem, 1)

            def transposes(k):
                pe.wait_ge(self.pn_done.sem, self.pn_done.at(it, k + 1))
                if k >= 2:
                    pe.wait_ge(self.pt_ev.sem, self.pt_ev.at(it, k - 1))
                for w in range(4):
                    ins = pe.transpose(PS[:, 2 + k % 2, w * P:(w + 1) * P], self.Pr[:, k % 2, w * P:(w + 1) * P], c.ident)
                ins.then_inc(self.t_done.sem, 1)

            def values(k):
                pe.wait_ge(self.pt_ev.sem, self.pt_ev.at(it, k + 1))
                if k >= 2:
                    pe.wait_ge(self.o_ev.sem, self.o_ev.at(it, k - 1))
                for w in range(4):
                    ins = pe.matmul(PS[:, 4 + k % 2, w * P:(w + 1) * P], self.V[:, self.KEYS[w] // 64, k * P:(k + 1) * P],
                                    self.PT[:, k % 2, w * P:(w + 1) * P], start=True, stop=True)
                ins.then_inc(self.o_done.sem, 1)

            for step in range(7):
                if step < 4:
                    scores(step)
                if 1 <= step < 5:
                    transposes(step - 1)
                if 2 <= step < 6:
                    values(step - 2)
            pe.wait_ge(self.o_ev.sem, self.o_ev.at(it, 4))
            for t in range(2):
                for k in range(4):
                    ins = pe.matmul(PS[:, 6, t * P:(t + 1) * P], self.OT[:, k, t * P:(t + 1) * P], self.wo[:, k, :],
                                    start=(k == 0), stop=(k == 3))
            ins.then_inc(self.y_done.sem, 1)
            pe.wait_ge(self.x1_ready.sem, self.x1_ready.at(it, 1))
            for t in range(2):
                ins = pe.transpose(PS[:, 7, t * P:(t + 1) * P], self.X1[:, t, :], c.ident)
            ins.then_inc(self.x1t_done.sem, 1)
            pe.wait_ge(self.h2_ready.sem, self.h2_ready.at(it, 1))
            for t in range(2):
                ins = pe.transpose(PS[:, 6, t * P:(t + 1) * P], self.H2[:, t * P:(t + 1) * P], c.ident)
            ins.then_inc(self.h2_done.sem, 1)
            pe.wait_ge(self.n_ready.sem, self.n_ready.at(it, 1))
            for t in range(2):
                ins = pe.transpose(PS[:, 7, t * P:(t + 1) * P], self.HN[:, t, :], c.ident)
            ins.then_inc(self.n_done.sem, 1)
            pe.wait_ge(self.n_ev.sem, self.n_ev.at(it, 1))
            at = 0
            for f, m in enumerate(self.HID):
                if f == 2:
                    pe.wait_ge(self.hid_ready.sem, self.hid_ready.at(it, 1))
                pe.matmul(PS[0:m, f % 2, 0:256], self.w1[:, at:at + m], self.HNT, start=True, stop=True)\
                    .then_inc(self.ag_done.sem, 1)
                pe.matmul(PS[0:m, 2 + f % 2, 0:256], self.w1[:, 341 + at:341 + at + m], self.HNT, start=True, stop=True)\
                    .then_inc(self.ag_done.sem, 1)
                at += m
            for f, m in enumerate(self.HID):
                pe.wait_ge(self.hid_ready.sem, self.hid_ready.at(it, f + 1))
                w = self.w2[:, f, :] if f < 2 else self.w2r[0:m, :]
                for t in range(2):
                    ins = pe.matmul(PS[:, 4, t * P:(t + 1) * P], self.HD[0:m, f, t * P:(t + 1) * P], w,
                                    start=(f == 0 and t == 0), stop=(f == 2), skip_group_check=True)
            ins.then_inc(self.f_done.sem, 1)
            if self.depth == 0:
                pe.wait_ge(self.z_ready.sem, self.z_ready.at(it, 1))
                for t in range(2):
                    ins = pe.transpose(PS[:, 5, t * P:(t + 1) * P], self.HN[:, t, :], c.ident)
                ins.then_inc(self.x2t_done.sem, 1)

    def scalar(self, a):
        c, PS = self.c, self.c.PS
        a.wait_ge(self.x_ready.sem, self.x_ready.at(0, 2))
        if self.depth:
            a.wait_ge(self.prev_out.sem, self.prev_out.at(B - 1, 1))
        with a.Fori(0, B) as it:
            c.act.enter(it)
            _, XT = self.source(it)
            a.activation(self.Hs[64:128, 1:256], XT[64:128, bass.ds(it * S, S - 1)], ACT.Copy)
            a.activation(self.Hs[0:64, :], XT[0:64, bass.ds(it * S, S)], ACT.Copy).then_inc(self.h_ready.sem, 1)
            for i in range(4):
                a.wait_ge(self.ab_done.sem, self.ab_done.at(it, i + 1))
                if i:
                    a.wait_ge(self.ssq_used.sem, self.ssq_used.at(it, i))
                a.activation(self.SQ, PS[:, i, :], ACT.Square).then_inc(self.sq_done.sem, 1)
            for w in range(3):
                a.wait_ge(self.p_done.sem, self.p_done.at(it, 5 + w))
                a.activation(self.V[:, w, :], PS[:, 4 + w, :], ACT.Copy).then_inc(self.v_ev.sem, 1)
            a.wait_ge(self.sum_ready.sem, self.sum_ready.at(it, 1))
            a.activation(self.nrm, self.ssq, ACT.Sqrt).then_inc(self.nrm_ready.sem, 1)

            def exps(k):
                a.wait_ge(self.mx_done.sem, self.mx_done.at(it, k + 1))
                if k >= 2:
                    a.wait_ge(self.t_done.sem, self.t_done.at(it, k - 1))
                for w in range(4):
                    s = slice(w * P, (w + 1) * P)
                    ins = a.activation(self.Pr[:, k % 2, s], PS[:, k % 2, s], ACT.Exp, bias=self.nm[:, k, w:w + 1],
                                       scale=1.0, accum_out=self.ss[:, k, w:w + 1])
                ins.then_inc(self.e_done.sem, 1)

            def out(k):
                a.wait_ge(self.o_done.sem, self.o_done.at(it, k + 1))
                for r in range(2):
                    s = slice(64 * r, 64 * r + 64)
                    src = PS[s, 4 + k % 2, :].rearrange("p (w q) -> p w q", w=4)[:, :, s]
                    ins = a.activation(self.OT[s, k, :].rearrange("p (w q) -> p w q", w=4), src, ACT.Copy)
                ins.then_inc(self.o_ev.sem, 1)

            for step in range(7):
                if step < 4:
                    exps(step)
                if 2 <= step < 6:
                    out(step - 2)
            a.wait_ge(self.x1t_done.sem, self.x1t_done.at(it, 1))
            a.activation(self.H2[64:128, 1:256], PS[64:128, 7, 0:255], ACT.Copy)
            a.activation(self.H2[0:64, :], PS[0:64, 7, 0:256], ACT.Copy).then_inc(self.h2_ready.sem, 1)
            a.wait_ge(self.var_ready.sem, self.var_ready.at(it, 1))
            a.activation(self.sd2, self.mv2.rearrange("p (t k) -> p t k", k=2)[:, :, 1], ACT.Sqrt, bias=c.eps, scale=1.0)\
                .then_inc(self.sd_ready.sem, 1)
            a.wait_ge(self.n_done.sem, self.n_done.at(it, 1))
            a.activation(self.HNT, PS[:, 7, 0:256], ACT.Identity, bias=self.lb, scale=self.lg).then_inc(self.n_ev.sem, 1)
            for f, m in enumerate(self.HID):
                a.wait_ge(self.ag_done.sem, self.ag_done.at(it, 2 * f + 2))
                if f == 2:
                    a.wait_ge(self.hid_ready.sem, self.hid_ready.at(it, 1))
                a.activation(self.GE[0:m, f % 2, :], PS[0:m, 2 + f % 2, 0:256], ACT.Gelu, bias=self.b1[0:m, 3 + f:4 + f],
                             scale=1.0).then_inc(self.g_ready.sem, 1)
            if self.depth == 0:
                a.wait_ge(self.x2t_done.sem, self.x2t_done.at(it, 1))
                a.activation(self.XIT[:, bass.ds(it * S, S)], PS[:, 5, 0:256], ACT.Copy).then_inc(self.out_ready.sem, 1)
        c.act.leave(B)

    def vector(self, v):
        c, PS = self.c, self.c.PS

        def link(ins):
            c.dve.link(v, ins)

        v.wait_ge(self.x_ready.sem, self.x_ready.at(0, 2))
        if self.depth:
            v.wait_ge(self.prev_out.sem, self.prev_out.at(B - 1, 1))
        v.memset(self.Hs[64:128, 0:1], 0.0)
        v.memset(self.H2[64:128, 0:1], 0.0)
        v.memset(self.QZ[0:64, 1:8:2, :], 0.0)
        v.memset(self.QZ[64:128, 0:8:2, :], 0.0)
        for t in range(2):
            for i, sc in enumerate((self.qs, self.ks)):
                cos = self.tables[:, t, 2 * i, :]
                sin = self.tables[:, t, 2 * i + 1, :]
                o = self.tab[:, t, i * 128:(i + 1) * 128]
                v.tensor_tensor(o[:, 0:64], cos, sc, ALU.mult)
                v.tensor_tensor(o[:, 64:96], sin[:, 0:32], sc[:, 32:64], ALU.mult)
                v.tensor_tensor(o[:, 96:128], sin[:, 32:64], sc[:, 0:32], ALU.mult)
        link(v.tensor_copy(self.MBK, self.maskb))
        v.memset(self.nm, 0.0).then_inc(self.mask_ready.sem, 1)
        v.wait_ge(self.mask_ready.sem, self.mask_ready.at(0, 1))
        with v.Fori(0, B) as it:
            c.dve.enter(it)
            xin, _ = self.source(it)

            def rotate(i):
                t, j = divmod(i, 2)
                v.wait_ge(self.p_done.sem, self.p_done.at(it, i + 1))
                if i >= 2:
                    v.wait_ge(self.qk_sum.sem, self.qk_sum.at(it, i - 1))
                tab = self.tab[:, t, j * 128:(j + 1) * 128]
                q = PS[:, i, :].rearrange("p (h d) -> p h d", h=8)
                qa = self.QA[:, i, :].rearrange("p (h d) -> p h d", h=8)
                qb = self.QB[:, i % 2, :].rearrange("p (h d) -> p h d", h=8)

                def tb(a, b):
                    return tab[:, a:b].unsqueeze(1).to_broadcast([P, 8, b - a])

                v.tensor_tensor(qa, q, tb(0, 64), ALU.mult)
                v.tensor_tensor(qb[:, :, 0:32], q[:, :, 32:64], tb(64, 96), ALU.mult)
                v.tensor_tensor(qb[:, :, 32:64], q[:, :, 0:32], tb(96, 128), ALU.mult).then_inc(self.ab_done.sem, 1)

            def norms(i):
                v.wait_ge(self.sq_done.sem, self.sq_done.at(it, i + 1))
                v.tensor_reduce(self.ssq[:, i, :], self.SQ.rearrange("p (h d) -> p h d", h=8), AX.X, ALU.add)\
                    .then_inc(self.ssq_used.sem, 1)

            for i in range(5):
                if i < 4:
                    rotate(i)
                if i >= 1:
                    norms(i - 1)
            v.wait_ge(self.ssq_used.sem, self.ssq_used.at(it, 4))
            v.tensor_scalar(self.ssq, self.ssq, 1e-24, None, ALU.max).then_inc(self.sum_ready.sem, 1)
            v.wait_ge(self.nrm_ready.sem, self.nrm_ready.at(it, 1))
            link(v.reciprocal(self.inv, self.nrm))
            refine(link, v, self.inv, self.ssq, 0.0, self.nrt)
            v.tensor_scalar(self.inv, self.inv, 1.0, None, ALU.mult).then_inc(self.inv_ready.sem, 1)
            for i in range(4):
                v.wait_ge(self.tr_done.sem, self.tr_done.at(it, i + 1))
                t, j = divmod(i, 2)
                src = PS[:, 4 + i, :].rearrange("p (k q) -> p k q", k=4)
                if j == 0:
                    v.tensor_copy(self.QZ[0:64, 0:8:2, t * P:(t + 1) * P], src[0:64])
                    ins = v.tensor_copy(self.QZ[64:128, 1:8:2, t * P:(t + 1) * P], src[64:128])
                else:
                    ins = v.tensor_copy(self.KT[:, :, t * P:(t + 1) * P], src)
                ins.then_inc(self.tr_ev.sem, 1)

            def maxima(k):
                v.wait_ge(self.s_done.sem, self.s_done.at(it, k + 1))
                v.tensor_reduce(self.nm[:, k, :], PS[:, k % 2, :].rearrange("p (w j) -> p w j", w=4), AX.X, ALU.max,
                                negate=True).then_inc(self.mx_done.sem, 1)

            def reciprocals(k):
                v.wait_ge(self.e_done.sem, self.e_done.at(it, k + 1))
                v.reciprocal(self.ri[:, k, :], self.ss[:, k, :]).then_inc(self.r_done.sem, 1)

            def spread(k):
                v.wait_ge(self.t_done.sem, self.t_done.at(it, k + 1))
                if k >= 2:
                    v.wait_ge(self.o_done.sem, self.o_done.at(it, k - 1))
                v.tensor_copy(self.PT[:, k % 2, :], PS[:, 2 + k % 2, :]).then_inc(self.pt_ev.sem, 1)

            for step in range(7):
                if step < 4:
                    maxima(step)
                if 0 <= step < 4:
                    reciprocals(step)
                if 1 <= step < 5:
                    spread(step - 1)
            v.wait_ge(self.y_done.sem, self.y_done.at(it, 1))
            v.tensor_tensor(self.X1, two(PS[:, 6, 0:256]), xin, ALU.add).then_inc(self.x1_ready.sem, 1)
            v.wait_ge(self.h2_done.sem, self.h2_done.at(it, 1))
            for t in range(2):
                ins = v.bn_stats(self.st[:, 6 * t:6 * t + 6], PS[:, 6, t * P:(t + 1) * P])
            link(ins)
            v.tensor_tensor(self.X1, self.X1, self.b2.unsqueeze(1).to_broadcast([P, 2, P]), ALU.add)
            for t in range(2):
                ins = v.bn_aggr(self.mv2[:, 2 * t:2 * t + 2], self.st[:, 6 * t:6 * t + 6])
            ins.then_inc(self.var_ready.sem, 1)
            v.wait_ge(self.sd_ready.sem, self.sd_ready.at(it, 1))
            link(v.reciprocal(self.rs2, self.sd2))
            refine(link, v, self.rs2, self.mv2.rearrange("p (t k) -> p t k", k=2)[:, :, 1], EPS, c.rt[:, 0:2])
            for t in range(2):
                ins = v.tensor_scalar(self.HN[:, t, :], PS[:, 6, t * P:(t + 1) * P], self.mv2[:, 2 * t:2 * t + 1],
                                      self.rs2[:, t:t + 1], ALU.subtract, ALU.mult)
            ins.then_inc(self.n_ready.sem, 1)
            for f, m in enumerate(self.HID):
                v.wait_ge(self.g_ready.sem, self.g_ready.at(it, f + 1))
                v.scalar_tensor_tensor(self.HD[0:m, f, :], PS[0:m, f % 2, 0:256], self.b1[0:m, f:f + 1],
                                       self.GE[0:m, f % 2, :], ALU.add, ALU.mult).then_inc(self.hid_ready.sem, 1)
            v.wait_ge(self.f_done.sem, self.f_done.at(it, 1))
            y = two(PS[:, 4, 0:256])
            if self.depth == 0:
                v.tensor_tensor(self.XI[:, bass.ds(it * 2, 2), :], self.X1, y, ALU.add)
                v.tensor_tensor(self.HN, self.X1, y, ALU.add).then_inc(self.z_ready.sem, 1)
                v.wait_ge(self.x2t_done.sem, self.x2t_done.at(it, 1))
            else:
                link(v.tensor_tensor(self.X1, self.X1, y, ALU.add))
                v.tensor_tensor(c.Z[:, bass.ds(it * 2, 2), :], self.X1, c.X[:, bass.ds(it * 2, 2), :], ALU.add)\
                    .then_inc(self.z_ready.sem, 1)
        c.dve.leave(B)
        v.wait_ge(self.z_ready.sem, self.z_ready.at(B - 1, 1))

    def gpsimd(self, g):
        c = self.c
        with g.Fori(0, B) as it:
            for i in range(4):
                g.wait_ge(self.ab_done.sem, self.ab_done.at(it, i + 1))
                g.tensor_tensor(self.QA[:, i, :], self.QA[:, i, :], self.QB[:, i % 2, :], ALU.add)\
                    .then_inc(self.qk_sum.sem, 1)
            g.wait_ge(self.inv_ready.sem, self.inv_ready.at(it, 1))
            g.wait_ge(self.qk_sum.sem, self.qk_sum.at(it, 4))
            for i in range(4):
                q = self.QA[:, i, :].rearrange("p (h d) -> p h d", h=8)
                g.tensor_tensor(q, q, self.inv[:, i, :].unsqueeze(2).to_broadcast([P, 8, 64]), ALU.mult)\
                    .then_inc(self.qk_ready.sem, 1)
            for k in range(4):
                g.wait_ge(self.r_done.sem, self.r_done.at(it, k + 1))
                p = self.Pr[:, k % 2, :].rearrange("p (w j) -> p w j", w=4)
                g.tensor_tensor(p, p, self.ri[:, k, :].unsqueeze(2).to_broadcast([P, 4, P]), ALU.mult)\
                    .then_inc(self.pn_done.sem, 1)


def chunks(w):
    return w.reshape(-1, P, w.shape[-1]).transpose(1, 0, 2)


def head_rows(w):
    out = np.zeros((4, 4, 32, w.shape[-1]), w.dtype)
    out[:, :, 0:8] = w.reshape(4, 4, 8, -1)
    return out.reshape(4, P, -1).transpose(1, 0, 2)


def over(b):
    return np.broadcast_to(b.reshape(1, -1), (P, b.size))


def constants():
    i = np.arange(P)
    f = np.float32
    headmask = (i[:, None] // 8 == np.arange(16)[None, :]).astype(f)
    rel, band = (t.reshape(WIN_Q, -1) for t in window_tables())
    return [("ident", np.eye(P, dtype=f)), ("headmask", headmask),
            ("eps", np.full((P, 1), EPS, f)), ("rel", rel), ("one", np.ones((P, 1), f)),
            ("onehot", (i[:, None] % 32 == np.arange(32)[None, :]).astype(f)), ("band", band),
            ("iota8", np.broadcast_to(np.arange(8, dtype=f), (P, 8)))]


def weights(w):
    i = np.arange(P)
    l0a = [("causal", np.where(i[None, :] <= i[:, None], 0.0, NEG).astype(np.float32)), ("L0a_wlat", w["L0_attn_w_kv_down"]), ("L0a_wkv", w["L0_attn_w_kv_up"]), ("L0a_wq", w["L0_attn_w_q"]),
           ("L0a_wo", chunks(w["L0_attn_w_out"]))]
    l1x = [("L1x_wq", w["L1_xattn_W_q"].T), ("L1x_wk", w["L1_xattn_W_k"].T), ("L1x_wv", w["L1_xattn_W_v"].T),
           ("L1x_wo", head_rows(w["L1_xattn_W_out"].T)), ("L1x_bq", w["L1_xattn_b_q"][:, None]),
           ("L1x_bk", w["L1_xattn_b_k"][:, None]), ("L1x_bv", over(w["L1_xattn_b_v"])),
           ("L1x_bo", over(w["L1_xattn_b_out"]))]
    l2x = [("L2x_wq", w["L2_xattn_wq"].T), ("L2x_wk", w["L2_xattn_wk"].T),
           ("L2x_wo", head_rows(w["L2_xattn_wo"].T)), ("L2x_bq", w["L2_xattn_bq"][:, None]),
           ("L2x_bk", w["L2_xattn_bk"][:, None]), ("L2x_bv", over(w["L2_xattn_bk"])),
           ("L2x_bo", over(w["L2_xattn_bo"]))]
    l3x = [("L3x_wq", w["L3_xattn_Wq"]), ("L3x_wk", w["L3_xattn_Wk"]), ("L3x_wv", w["L3_xattn_Wv"]),
           ("L3x_wo", chunks(w["L3_xattn_Wo"])), ("L3x_bo", over(w["L3_xattn_bo"]))]
    names = ("Wq_c", "Wk_s", "Wv_s", "Wq_s", "Wk_c", "Wv_c")
    l0x = [("L0x_w", np.stack([w["L0_xattn_" + n].T for n in names], 1)),
           ("L0x_bq", np.stack([w["L0_xattn_bq_c"], w["L0_xattn_bq_s"]], 1)),
           ("L0x_bk", np.stack([w["L0_xattn_bk_s"], w["L0_xattn_bk_c"]], 1)),
           ("L0x_bv", np.stack([over(w["L0_xattn_bv_s"]), over(w["L0_xattn_bv_c"])], 1)),
           ("L0x_wg", chunks(w["L0_xattn_Wg"].T)), ("L0x_bg", w["L0_xattn_bg"][:, None])]
    l1f = [("L1f_w1", w["L1_ffn_w1"].T), ("L1f_w2", chunks(w["L1_ffn_w2"].T)),
           ("L1f_cw", chunks(w["L1_ffn_conv_w"][:, 0, :])), ("L1f_cb", chunks(w["L1_ffn_conv_b"][:, None])[:, :, 0])]
    up = np.concatenate([w["L2_ffn_w_up"], w["L2_ffn_sw_up"][None]], 0).transpose(1, 0, 2)
    gate = np.concatenate([w["L2_ffn_w_gate"], w["L2_ffn_sw_gate"][None]], 0).transpose(1, 0, 2)
    down = np.concatenate([w["L2_ffn_w_down"], w["L2_ffn_sw_down"][None]], 0).transpose(1, 0, 2)
    gap = np.zeros((P, up.shape[1], 64 - (up.shape[2] - P)), up.dtype)
    l2f = [("L2f_gu", np.concatenate([gate[:, :, :P], up[:, :, :P]], 2)),
           ("L2f_rest", np.concatenate([gate[:, :, P:], gap, up[:, :, P:]], 2)),
           ("L2f_down", down[:P]), ("L2f_drest", down[P:]),
           ("L2f_router", np.concatenate([w["L2_ffn_gate_w"], w["L2_ffn_shared_gate_w"]], 0).T)]
    up = np.concatenate([w["L3_ffn_routed_up"], w["L3_ffn_shared_up"][None]], 0).transpose(2, 0, 1)
    gate = np.concatenate([w["L3_ffn_routed_gate"], w["L3_ffn_shared_gate"][None]], 0).transpose(2, 0, 1)
    down = np.concatenate([w["L3_ffn_routed_down"], w["L3_ffn_shared_down"][None]], 0)
    n = up.shape[1] * 4
    l3f = [("L3f_gu", np.concatenate([gate.reshape(P, n, P), up.reshape(P, n, P)], 2)),
           ("L3f_down", down.transpose(0, 2, 1).reshape(-1, 4, P, P).transpose(2, 0, 1, 3).reshape(P, n, P))]
    router = np.zeros((P, 8), np.float32)
    router[:, 0:7] = w["L3_ffn_router_w"].T
    l3r = [("L3f_router", router)]
    rel = w["L2_attn_rel_pos_keys"][13:20, 0:8]
    l2a = [("L2a_win", w["L2_attn_in_proj_weight"].T), ("L2a_bin", over(w["L2_attn_in_proj_bias"])),
           ("L2a_rel", np.broadcast_to(np.tile(rel, (1, 16)), (P, 7, P))), ("L2a_wout", w["L2_attn_out_w"].T),
           ("L2a_bout", over(w["L2_attn_out_b"]))]
    wx = w["L1_attn_W_x"].T
    l1a = [("L1a_g", w["L1_attn_ln_g"][:, None]), ("L1a_b", w["L1_attn_ln_b"][:, None]), ("L1a_win", w["L1_attn_W_in"].T),
           ("L1a_cw", chunks(w["L1_attn_conv_w"])), ("L1a_cb", chunks(w["L1_attn_conv_b"][:, None])[:, :, 0]),
           ("L1a_wdti", chunks(wx[:, 0:8])), ("L1a_wbc", chunks(np.tile(wx[:, 8:40], (1, 3)))),
           ("L1a_wdt", w["L1_attn_W_dt"].T), ("L1a_bdt", chunks(w["L1_attn_dt_bias"][:, None])[:, :, 0]),
           ("L1a_alog", chunks(w["L1_attn_A_log"]).reshape(P, 32)), ("L1a_D", chunks(w["L1_attn_D"][:, None])[:, :, 0]),
           ("L1a_wout", chunks(w["L1_attn_W_out"].T))]
    l0f = [("rotary", rotary_tables().reshape(2, P, 4, 64).transpose(1, 0, 2, 3)),
           ("local", local_masks().reshape(P, 512))]
    for d in range(2):
        b1 = np.zeros((2, 384), np.float32)
        b1[:, 0:341] = w["L0_ffn_b1"][d].reshape(2, 341)
        l0f += [(f"L0f{d}_wqkv", w["L0_ffn_wqkv"][d]), (f"L0f{d}_qs", over(w["L0_ffn_q_scale"][d])),
                (f"L0f{d}_ks", over(w["L0_ffn_k_scale"][d])), (f"L0f{d}_wo", chunks(w["L0_ffn_wo"][d])),
                (f"L0f{d}_lg", w["L0_ffn_ln_g"][d][:, None]), (f"L0f{d}_lb", w["L0_ffn_ln_b"][d][:, None]),
                (f"L0f{d}_w1", w["L0_ffn_w1"][d]), (f"L0f{d}_b1", b1.reshape(6, P).T),
                (f"L0f{d}_w2", chunks(w["L0_ffn_w2"][d][0:256])), (f"L0f{d}_w2r", w["L0_ffn_w2"][d][256:341]),
                (f"L0f{d}_b2", over(w["L0_ffn_b2"][d]))]
    l3a = [("L3a_wq", w["L3_attn_Wq"].T), ("L3a_wk", w["L3_attn_Wk"].T), ("L3a_wv", w["L3_attn_Wv"].T),
           ("L3a_wo", head_rows(w["L3_attn_Wo"].T)), ("L3a_slopes", over(w["L3_attn_slopes"]))]
    return {"first": l0a + l0x + l0f, "rest": l1a + l1x + l1f + l2a + l2x + l2f + l3a, "last": l3x + l3r + l3f}


def pack(pieces):
    table, at = {}, 0
    for name, a in pieces:
        n = int(np.prod(a.shape[1:]))
        table[name] = (at, a.shape)
        at += n
    out = np.zeros((P, at), np.float32)
    for name, a in pieces:
        o, shape = table[name]
        out[0:shape[0], o:o + int(np.prod(shape[1:]))] = a.reshape(shape[0], -1)
    return out, table


def build(nc, dram, tables, totals, names):
    with ExitStack() as ctx:
        c = Core(ctx, nc, totals)
        packs = {k: c.sb(f"w_{k}", [P, dram[k].shape[1]]) for k in tables if k != "first"}
        packs["first"] = packs["last"][:, 0:dram["first"].shape[1]]
        mask = c.sb("mask", [P, T, S], U8)
        loaded = {k: ctx.enter_context(nc.semaphore(f"loaded_{k}")) for k in list(tables) + ["x", "ctx", "mask"]}
        stored = ctx.enter_context(nc.semaphore("stored"))
        x_loaded_tr = c.sig("x_loaded_tr", 2, 1)
        start_x = c.x_ready

        def W(name):
            for k, table in tables.items():
                if name in table:
                    o, shape = table[name]
                    ap = packs[k][0:shape[0], o:o + int(np.prod(shape[1:]))]
                    if len(shape) == 3:
                        ap = ap.rearrange("p (a b) -> p a b", a=shape[1])
                    if len(shape) == 4:
                        ap = ap.rearrange("p (a b c) -> p a b c", a=shape[1], b=shape[2])
                    return ap

        c.W = W
        c.ident, c.eps, c.one = W("ident"), W("eps"), W("one")
        onehot = c.sb("onehot", [P, 32], BF16)

        def wait_weights(eng, stage):
            eng.wait_ge(loaded["ctx"], 16)
            eng.wait_ge(loaded["mask"], 16)
            eng.wait_ge(loaded[stage.region], 16)
        c.wait_weights = wait_weights

        def local(d):
            w = [W(f"L0f{d}_{n}") for n in ("wqkv", "qs", "ks", "wo", "lg", "lb", "w1", "b1", "w2", "w2r", "b2")]
            return LocalLayer(c, d, *w, W("rotary"), W("local"))

        makers = {
            "L1a": lambda: Mamba(c, *(W(f"L1a_{n}") for n in ("g", "b", "win", "cw", "cb", "wdti", "wbc", "wdt", "bdt",
                                                             "alog", "D", "wout")), onehot),
            "L0a": lambda: Attention(c, 64, W("L0a_wq"), W("L0a_wkv")[:, 0:1024], W("L0a_wkv")[:, 1024:2048],
                                     W("L0a_wo"), "x", wlat=W("L0a_wlat"), causal=W("causal")),
            "L0x": lambda: TwoWay(c, W("L0x_w"), W("L0x_bq"), W("L0x_bk"), W("L0x_bv"), W("L0x_wg"), W("L0x_bg")),
            "L1f": lambda: BitLinear(c, W("L1f_w1"), W("L1f_w2"), W("L1f_cw"), W("L1f_cb")),
            "L2a": lambda: FourTokenAttention(c, W("L2a_win"), W("L2a_bin"), W("L2a_rel"), W("L2a_wout"), W("L2a_bout")),
            "L3a": lambda: BandedAttention(c, W("L3a_wq"), W("L3a_wk"), W("L3a_wv"), W("L3a_wo"), W("L3a_slopes"),
                                           W("rel"), W("band"), W("headmask")),
            "L2f": lambda: Experts(c, 8, 1, 48, W("L2f_gu"), W("L2f_rest"), W("L2f_down"), W("L2f_drest"),
                                   W("L2f_router"), W("iota8"), True, 0.0),
            "L3f": lambda: Experts(c, 7, 4, 0, W("L3f_gu"), None, W("L3f_down"), None,
                                   W("L3f_router"), W("iota8"), False, 1e-9),
            "L1x": lambda: Attention(c, 8, W("L1x_wq"), W("L1x_wk"), W("L1x_wv"), W("L1x_wo"), "ctx",
                                     bq=W("L1x_bq"), bk=W("L1x_bk"), bv=W("L1x_bv"), bo=W("L1x_bo"),
                                     headmask=W("headmask")),
            "L2x": lambda: Attention(c, 8, W("L2x_wq"), W("L2x_wk"), W("L2x_wk"), W("L2x_wo"), "ctx",
                                     bq=W("L2x_bq"), bk=W("L2x_bk"), bv=W("L2x_bv"), bo=W("L2x_bo"),
                                     headmask=W("headmask")),
            "L3x": lambda: Attention(c, 64, W("L3x_wq"), W("L3x_wk"), W("L3x_wv"), W("L3x_wo"), "ctx",
                                     mask=mask, bo=W("L3x_bo")),
        }
        regions = {"L0a": "first", "L0x": "first", "L0f": "first", "L3x": "last", "L3f": "last"}
        stages = []
        for i, n in enumerate(names):
            if n == "L0f":
                first = local(0)
                first.region = "first"
                stages.append(first)
                s = local(1)
                s.prev_out = first.out_ready
            else:
                s = makers[n]()
            s.region = regions.get(n, "rest")
            if s.region == "first":
                last_first = s.z_ready
            stages += [s, LayerEnd(c, s.z_ready, last=i == len(names) - 1)]
        last_x = stages[-1].x_tile
        block = ctx.enter_context(nc.Block())

        @block.sync
        def _(sp):
            sp.dma_start(packs["consts"][:, :], dram["consts"]).then_inc(loaded["consts"], 16)
            sp.dma_start(c.X[:, :, :], dram["x"].rearrange("(t p) d -> p t d", p=P)).then_inc(loaded["x"], 16)
            if "L0" in names[0]:
                sp.dma_start(packs["first"], dram["first"]).then_inc(loaded["first"], 16)
            sp.dma_start(mask[:, :, :], dram["mask"].rearrange("(t p) k -> p t k", p=P)).then_inc(loaded["mask"], 16)
            sp.dma_start(c.CT[:, :], dram["ctxT"]).then_inc(loaded["ctx"], 16)
            sp.dma_start(packs["rest"][:, :], dram["rest"]).then_inc(loaded["rest"], 16)
            if "L3" in names[-1]:
                if "L0" in names[0]:
                    sp.wait_ge(last_first.sem, last_first.at(B - 1, 1))
                sp.dma_start(packs["last"][:, :], dram["last"]).then_inc(loaded["last"], 16)
            sp.wait_ge(last_x.sem, last_x.at(0, T))
            sp.dma_start(dram["out"].rearrange("(t p) d -> p t d", p=P), c.X[:, :, :]).then_inc(stored, 16)
            sp.wait_ge(stored, 16)

        @block.tensor
        def _(pe):
            pe.wait_ge(loaded["consts"], 16)
            pe.wait_ge(loaded["x"], 16)
            for n in range(T):
                ins = pe.transpose(c.PS[:, n // 4, (n % 4) * P:(n % 4) * P + P], c.X[:, n, :], c.ident)
                if n % 4 == 3:
                    ins.then_inc(x_loaded_tr.sem, 1)
            for s in stages:
                if isinstance(s, LayerEnd) is False:
                    wait_weights(pe, s)
                s.tensor(pe)

        @block.vector
        def _(v):
            v.wait_ge(loaded["consts"], 16)
            v.tensor_copy(c.IDB[:, :], c.ident)
            v.tensor_copy(onehot[:, :], W("onehot"))
            v.wait_ge(x_loaded_tr.sem, 1)
            v.tensor_copy(c.XT[:, 0:512], c.PS[:, 0, :]).then_inc(start_x.sem, 1)
            for s in stages:
                if not isinstance(s, LayerEnd):
                    wait_weights(v, s)
                s.vector(v)

        @block.scalar
        def _(a):
            a.wait_ge(x_loaded_tr.sem, 2)
            a.activation(c.XT[:, 512:1024], c.PS[:, 1, :], ACT.Copy).then_inc(start_x.sem, 1)
            for s in stages:
                if not isinstance(s, LayerEnd):
                    wait_weights(a, s)
                s.scalar(a)

        @block.gpsimd
        def _(g):
            for s in stages:
                if not isinstance(s, LayerEnd):
                    wait_weights(g, s)
                s.gpsimd(g)


def lay_out(w):
    arrays = {"x": np.ascontiguousarray(w["x"]).reshape(B * S, P),
              "ctxT": np.ascontiguousarray(w["ctx_1024"].reshape(B * S, P).T),
              "mask": np.ascontiguousarray(w["mask_BxSxS2_bk1"]).reshape(B * S, S)}
    tables = {}
    arrays["consts"], tables["consts"] = pack(constants())
    for k, pieces in weights(w).items():
        arrays[k], tables[k] = pack(pieces)
    return arrays, tables


def program(nc, arrays, tables, totals, names):
    dram = {k: nc.dram_tensor(f"in_{k}", a.shape, mybir.dt.from_np(a.dtype), kind="ExternalInput").ap()
            for k, a in arrays.items()}
    dram["out"] = nc.dram_tensor("out_0", (B * S, P), F32, kind="ExternalOutput").ap()
    build(nc, dram, tables, totals, names)


ORDER = ["L0a", "L0x", "L0f", "L1a", "L1x", "L1f", "L2a", "L2x", "L2f", "L3a", "L3x", "L3f"]


def kernel(**inputs):
    import concourse.bacc as bacc
    from concourse.bass_utils import run_bass_kernel_spmd as run

    w = {k: np.asarray(v) for k, v in inputs.items()}
    arrays, tables = lay_out(w)
    totals = {}
    for _ in range(2):
        nc = bacc.Bacc("TRN2", target_bir_lowering=False, num_devices=1)
        program(nc, arrays, tables, totals, ORDER)
    r = run(nc, [{f"in_{k}": a for k, a in arrays.items()}], core_ids=[0])
    return r.results[0]["out_0"].reshape(B, S, P)
```

```python
import numpy as np
import concourse.bass as bass
from concourse import mybir
from contextlib import ExitStack

F32 = mybir.dt.float32
BF16 = mybir.dt.bfloat16
U8 = mybir.dt.uint8
ALU = mybir.AluOpType
ACT = mybir.ActivationFunctionType
AX = mybir.AxisListType

P = 128
B, S = 4, 256
T = B * S // P
NEG = -(2.0 ** 127)
EPS = 1e-5


class Signal:

    def __init__(self, sem, before, per):
        self.sem, self.before, self.per = sem, before, per

    def at(self, it, k, ahead=0):
        return it * self.per + (self.before + ahead * self.per + k)


class Signals:

    def __init__(self, ctx, nc):
        self.ctx, self.nc, self.sems, self.total = ctx, nc, {}, {}

    def __call__(self, name, per=1, iters=B):
        if name not in self.sems:
            self.sems[name] = self.ctx.enter_context(self.nc.semaphore(name))
            self.total[name] = 0
        before = self.total[name]
        self.total[name] += per * iters
        return Signal(self.sems[name], before, per)


class Steps:

    def __init__(self, sem, totals, name):
        self.sem, self.totals, self.name = sem, totals, name
        self.before, self.k, self.it, self.loops, self.per = 0, 0, None, 0, 0

    def enter(self, it):
        self.before += self.k
        self.it, self.k = it, 0
        self.per = self.totals.get((self.name, self.loops), 1)

    def leave(self, iters, first=0):
        self.totals[(self.name, self.loops)] = self.k
        self.totals[(self.name, self.loops, "first")] = first
        self.loops += 1
        self.before += iters * self.k
        self.it, self.k = None, 0

    def value(self):
        if self.it is None:
            return self.before + self.k
        skipped = self.totals.get((self.name, self.loops, "first"), 0) * self.per
        return self.it * self.per + (self.before + self.k - skipped)

    def link(self, eng, ins):
        ins.then_inc(self.sem, 1)
        self.k += 1
        eng.wait_ge(self.sem, self.value())


def two(ap):
    return ap.rearrange("p (a b) -> p a b", a=2)


class Core:

    def __init__(self, ctx, nc, totals):
        self.nc = nc
        self.sig = Signals(ctx, nc)

        def sb(name, shape, dt=F32):
            return ctx.enter_context(nc.sbuf_tensor(name, shape, dt))

        self.sb = sb
        self.X = sb("X", [P, T, P])
        self.XT = sb("XT", [P, B * S])
        self.CT = sb("CT", [P, B * S])
        self.Z = sb("Z", [P, T, P])
        self.PS = ctx.enter_context(nc.psum_tensor("PS", [P, 8, 512], F32))
        self.bn = sb("bn", [P, T, 6])
        self.mv = sb("mv", [P, T, 2])
        self.sd = sb("sd", [P, T])
        self.rs = sb("rs", [P, T])
        self.rt = sb("rt", [P, T])
        self.IDB = sb("IDB", [P, P], BF16)
        self.CMB = sb("CMB", [P, P], BF16)
        self.arena = sb("arena", [P, 17600])
        self.small = sb("small", [P, 256])
        sems = {n: ctx.enter_context(nc.semaphore(n)) for n in ("dve_step", "act_step", "pool_step")}
        self.dve = Steps(sems["dve_step"], totals, "dve")
        self.act = Steps(sems["act_step"], totals, "act")
        self.pool = Steps(sems["pool_step"], totals, "pool")
        self.x_ready = self.sig("x_ready", 2, 1)

    def take(self, start, *shape):
        n = int(np.prod(shape))
        ap = self.arena[:, start:start + n]
        assert start + n <= 17600
        if len(shape) == 2:
            ap = ap.rearrange("p (a b) -> p a b", a=shape[0])
        if len(shape) == 3:
            ap = ap.rearrange("p (a b c) -> p a b c", a=shape[0], b=shape[1])
        return ap


def refine(link, v, r, a, eps, tmp):
    link(v.scalar_tensor_tensor(tmp, a, eps, r, ALU.add, ALU.mult))
    link(v.scalar_tensor_tensor(tmp, tmp, -0.5, r, ALU.mult, ALU.mult))
    link(v.scalar_tensor_tensor(r, tmp, 1.5, r, ALU.add, ALU.mult))


class LayerEnd:

    def __init__(self, c, z_ready, last=False, early=False, counted=0):
        self.c, self.z_ready, self.last = c, z_ready, last
        self.groups = [(0, T - 2), (T - 2, T)] if early else [(0, T)]
        self.counted = counted
        if counted:
            self.bn_ready = c.sig("bn_ready", counted, 1)
        self.var_ready = c.sig("var_ready", len(self.groups), 1)
        self.sd_ready = c.sig("sd_ready", len(self.groups), 1)
        self.x_tile = c.sig("x_tile", T, 1)
        self.xt_ps = c.sig("xt_ps", 2, 1)
        if not last:
            self.x_next = c.sig("x_ready", 2, 1)
        c.x_ready = None if last else self.x_next

    def count(self, v, first, n):
        for t in range(n):
            z = self.c.Z[:, bass.ds(first + t, 1), :].rearrange("p a f -> p (a f)")
            ins = v.bn_stats(self.c.bn[:, bass.ds(first + t, 1), :].rearrange("p a f -> p (a f)"), z)
        ins.then_inc(self.bn_ready.sem, 1)

    def stats(self, v, g):
        c, (a, b) = self.c, self.groups[g]
        if self.counted:
            v.wait_ge(self.bn_ready.sem, self.bn_ready.at(0, self.counted))
        else:
            for n in range(a, b):
                ins = v.bn_stats(c.bn[:, n, :], c.Z[:, n, :])
            c.dve.link(v, ins)
        for n in range(a, b):
            ins = v.bn_aggr(c.mv[:, n, :], c.bn[:, n, :])
        ins.then_inc(self.var_ready.sem, 1)

    def tiles(self, v, g):
        c, (a, b) = self.c, self.groups[g]
        v.wait_ge(self.sd_ready.sem, self.sd_ready.at(0, g + 1))
        c.dve.link(v, v.reciprocal(c.rs[:, a:b], c.sd[:, a:b]))
        refine(lambda ins: c.dve.link(v, ins), v, c.rs[:, a:b], c.mv[:, a:b, 1], EPS, c.rt[:, a:b])
        for n in range(a, b):
            v.tensor_scalar(c.X[:, n, :], c.Z[:, n, :], c.mv[:, n, 0:1], c.rs[:, n:n + 1],
                            ALU.subtract, ALU.mult).then_inc(self.x_tile.sem, 1)

    def root(self, a, g):
        c, (i, j) = self.c, self.groups[g]
        a.wait_ge(self.var_ready.sem, self.var_ready.at(0, g + 1))
        a.activation(c.sd[:, i:j], c.mv[:, i:j, 1], ACT.Sqrt, bias=c.eps, scale=1.0)\
            .then_inc(self.sd_ready.sem, 1)

    def transposes(self, pe, g):
        c = self.c
        for n in range(*self.groups[g]) if not self.last else ():
            pe.wait_ge(self.x_tile.sem, self.x_tile.at(0, n + 1))
            ins = pe.transpose(c.PS[:, n // 4, (n % 4) * P:(n % 4) * P + P], c.X[:, n, :], c.ident)
            if n % 4 == 3:
                ins.then_inc(self.xt_ps.sem, 1)

    def early_stats(self, v):
        v.wait_ge(self.z_ready.sem, self.z_ready.at(B - 2, 1))
        self.stats(v, 0)

    def vector(self, v):
        c, g = self.c, len(self.groups) - 1
        self.stats(v, g)
        self.tiles(v, g)
        if not self.last and g == 0:
            v.wait_ge(self.xt_ps.sem, self.xt_ps.at(0, 1))
            v.tensor_copy(c.XT[:, 0:512], c.PS[:, 0, :]).then_inc(self.x_next.sem, 1)

    def scalar(self, a):
        c, g = self.c, len(self.groups) - 1
        if g == 1 and not self.last:
            a.wait_ge(self.xt_ps.sem, self.xt_ps.at(0, 1))
            a.activation(c.XT[:, 0:512], c.PS[:, 0, :], ACT.Copy).then_inc(self.x_next.sem, 1)
        self.root(a, g)
        if not self.last:
            a.wait_ge(self.xt_ps.sem, self.xt_ps.at(0, 2))
            a.activation(c.XT[:, 512:1024], c.PS[:, 1, :], ACT.Copy).then_inc(self.x_next.sem, 1)

    def tensor(self, pe):
        if not self.last:
            self.transposes(pe, len(self.groups) - 1)

    def gpsimd(self, g):
        pass


class Attention:

    H = 16

    def __init__(self, c, D, wq, wk, wv, wo, kv, wlat=None, causal=None, mask=None,
                 bq=None, bk=None, bv=None, bo=None, headmask=None):
        self.c, self.D, self.kv, self.causal, self.mask = c, D, kv, causal, mask
        self.wq, self.wk, self.wv, self.wo, self.wlat = wq, wk, wv, wo, wlat
        self.bq, self.bk, self.bv, self.bo, self.headmask = bq, bk, bv, bo, headmask
        self.hpc = 2 if D == 64 else 4
        self.M = P // self.hpc
        self.NC = self.H // self.hpc
        self.scale = float(D) ** -0.5
        self.qk_jobs = 8 if D == 64 else 1
        self.v_jobs = 4 if D == 64 else 1
        self.NPT = 4 if D == 64 else 8
        self.ybank = 5 if D == 64 else 6
        self.lag = 5 if D == 64 else 4
        self.x_ready = c.x_ready
        s = c.sig
        self.src_ready = s("src_ready", 1)
        if wlat is not None:
            self.lat_done = s("lat_done", 1)
            self.lat_ev = s("lat_ev", 1)
        self.kp_done = s("kp_done", self.qk_jobs)
        self.qp_done = s("qp_done", self.qk_jobs)
        self.vp_done = s("vp_done", self.v_jobs)
        self.k_ev = s("k_ev", self.qk_jobs)
        self.q_ev = s("q_ev", self.qk_jobs if D == 64 else self.H)
        self.q_dve = s("q_dve", 8, 1) if D == 8 else None
        self.v_ev = s("v_ev", self.v_jobs)
        self.zeros = s("zeros", 1, 1) if D == 64 else None
        self.mask_ready = s("mask_ready", 1) if mask is not None else None
        self.qm_ready = s("qm_ready", 1, 1) if D == 8 else None
        self.s_done = s("s_done", 16)
        self.mx_done = s("mx_done", 16)
        self.e_done = s("e_done", 16)
        self.r_done = s("r_done", 16)
        self.pn_done = s("pn_done", 16)
        self.t_done = s("t_done", 16)
        self.pt_ev = s("pt_ev", 16)
        self.o_done = s("o_done", self.NC)
        self.o_ev = s("o_ev", self.NC)
        self.y_done = s("y_done", 1)
        self.z_ready = s("z_ready", 1)
        t = c.take
        self.XB, self.CB, self.LT = t(0, 256), t(256, 256), t(512, 256)
        self.MB = t(768, 256).bitcast(BF16).rearrange("p (a b) -> p a b", a=2)
        self.QZ = t(1024, 16, 256)
        self.V = t(5120, 2, 1024)
        self.Pr = t(7168, 4, 512)
        self.OT = t(9216, 8, 256)
        self.nm = t(11264, 16, 2)
        self.ss = t(11296, 16, 2)
        self.ri = t(11328, 16, 3)
        self.qm, self.qb = t(11376, 16), t(11392, 16)
        if D == 64:
            self.KT = t(11408, 8, 256)
            self.PT = t(13456, 4, 512)
        else:
            self.KT = t(11408, 1, 256)
            self.PT = t(11664, 8, 512)

    def spans(self):
        if self.causal is not None:
            return [(0, 0, 128), (128, 1, 256)]
        return [(0, 0, 256), (256, 1, 256)]

    def width(self):
        return 384 if self.causal is not None else 512

    def pt_blocks(self):
        if self.causal is not None:
            return [(0, 0), (128, 128), (256, 256)]
        return [(0, 0), (256, 128), (128, 256), (384, 384)]

    def chunk_after(self, s, lag):
        h = s - lag
        return h // self.hpc if h % self.hpc == self.hpc - 1 else None

    def parts(self, eng, part, steps=None):
        part(0, False, True, True)
        with eng.Fori(1, B - 1) as it:
            if steps:
                steps.enter(it)
            part(it, True, True, True)
        if steps:
            steps.leave(B - 2, 1)
        part(B - 1, True, True, False)
        part(B, True, False, False)

    def tensor(self, pe):
        c, PS = self.c, self.c.PS
        pe.wait_ge(self.x_ready.sem, self.x_ready.at(0, 2))
        src = self.LT if self.wlat is not None else self.XB if self.kv == "x" else self.CB

        def latent(it, d):
            pe.wait_ge(self.src_ready.sem, self.src_ready.at(it, 1, d))
            pe.matmul(PS[:, 4, 0:256], self.wlat, self.XB, start=True, stop=True).then_inc(self.lat_done.sem, 1)
            pe.wait_ge(self.lat_ev.sem, self.lat_ev.at(it, 1, d))

        def keys(it, d, q, bank):
            pe.matmul(PS[:, bank, 0:256], self.wk[:, q * P:(q + 1) * P], src, start=True, stop=True)\
                .then_inc(self.kp_done.sem, 1)

        def queries(it, d, q, bank):
            pe.matmul(PS[:, bank, 0:256], self.wq[:, q * P:(q + 1) * P], self.XB, start=True, stop=True)\
                .then_inc(self.qp_done.sem, 1)

        def values_of(it, d, n, bank):
            h, t = divmod(n, 2)
            pe.matmul(PS[:, bank, :], src[:, t * P:(t + 1) * P], self.wv[:, h * 512:(h + 1) * 512],
                      start=True, stop=True).then_inc(self.vp_done.sem, 1)

        def small_values():
            pe.matmul(PS[:, 4, 256:384], src[:, 0:P], self.wv, start=True, stop=True, skip_group_check=True)
            pe.matmul(PS[:, 4, 384:512], src[:, P:2 * P], self.wv, start=True, stop=True, skip_group_check=True)\
                .then_inc(self.vp_done.sem, 1)

        def scores(it, h, prev):
            if self.D == 64:
                if h % 2 == 0:
                    pe.wait_ge(self.k_ev.sem, self.k_ev.at(it, h // 2 + 1))
                    pe.wait_ge(self.q_ev.sem, self.q_ev.at(it, h // 2 + 1))
                keys = self.KT[:, h // 2, :]
            else:
                if h == 0:
                    pe.wait_ge(self.k_ev.sem, self.k_ev.at(it, 1))
                if prev:
                    pe.wait_ge(self.q_ev.sem, self.q_ev.at(it, h + 1))
                elif h < 8:
                    pe.wait_ge(self.q_ev.sem, self.q_ev.at(0, 2 * h + 2))
                else:
                    pe.wait_ge(self.q_dve.sem, self.q_dve.at(0, h - 7))
                keys = self.KT[:, 0, :]
            if h == 0 and self.mask is not None:
                pe.wait_ge(self.mask_ready.sem, self.mask_ready.at(it, 1))
            for col, t, n in self.spans():
                masked = self.causal is not None or self.mask is not None
                ins = pe.matmul(PS[:, h % 2, col:col + n], self.QZ[:, h, t * P:(t + 1) * P], keys[:, 0:n],
                                start=True, stop=not masked, skip_group_check=True)
                if self.causal is not None:
                    ins = pe.matmul(PS[:, h % 2, col + n - P:col + n], c.IDB[:, :], c.CMB[:, :],
                                    start=False, stop=True, skip_group_check=True)
                if self.mask is not None:
                    ins = pe.matmul(PS[:, h % 2, col:col + n], c.IDB[:, :], self.MB[:, t, :],
                                    start=False, stop=True, skip_group_check=True)
            ins.then_inc(self.s_done.sem, 1)

        def transposes(it, h):
            pe.wait_ge(self.pn_done.sem, self.pn_done.at(it, h + 1))
            for a, b in self.pt_blocks():
                ins = pe.transpose(PS[:, 2 + h % 2, b:b + P], self.Pr[:, h % 4, a:a + P], c.ident)
            ins.then_inc(self.t_done.sem, 1)

        def values(it, k):
            pe.wait_ge(self.pt_ev.sem, self.pt_ev.at(it, (k + 1) * self.hpc))
            for kt in range(2):
                for r in range(self.hpc):
                    h = (k * self.hpc + r) % self.H
                    o = PS[r * self.M:(r + 1) * self.M, 6 + k % 2, 0:256]
                    pt = self.PT[:, h % self.NPT, kt * 256:kt * 256 + 256]
                    if self.causal is not None and kt == 1:
                        o, pt = o[:, 128:256], pt[:, 0:128]
                    ins = pe.matmul(o, self.V[:, kt, h * self.M:(h + 1) * self.M], pt,
                                    start=(kt == 0), stop=(kt == 1), skip_group_check=True)
            ins.then_inc(self.o_done.sem, 1)

        def output(it):
            pe.wait_ge(self.o_ev.sem, self.o_ev.at(it, 0))
            for t in range(2):
                for k in range(self.NC):
                    ins = pe.matmul(PS[:, self.ybank, t * P:(t + 1) * P], self.OT[:, k, t * P:(t + 1) * P],
                                    self.wo[:, k, :], start=(k == 0), stop=(k == self.NC - 1))
            ins.then_inc(self.y_done.sem, 1)

        def part(it, prev, cur, nxt):
            for s in range(16):
                if not cur and s == 7:
                    self.end.transposes(pe, 0)
                if cur:
                    if prev or s >= 2:
                        pe.wait_ge(self.e_done.sem, self.e_done.at(it, s - 1))
                    scores(it, s, prev)
                h = s - 3
                if (h < 0 and prev) or (h >= 0 and cur):
                    if prev or h >= 2:
                        pe.wait_ge(self.pt_ev.sem, self.pt_ev.at(it, h - 1))
                    transposes(it, h)
                k = self.chunk_after(s, self.lag)
                if k is not None and ((k < 0 and prev) or (k >= 0 and cur)):
                    if self.D == 8 and k == 0 and prev:
                        pe.wait_ge(self.z_ready.sem, self.z_ready.at(it, 0))
                    if self.D == 8 and k == 0:
                        pe.wait_ge(self.v_ev.sem, self.v_ev.at(it, 1))
                    if self.D == 64 and k in (0, 4):
                        pe.wait_ge(self.v_ev.sem, self.v_ev.at(it, 2 if k == 0 else 4))
                    if prev or k >= 2:
                        pe.wait_ge(self.o_ev.sem, self.o_ev.at(it, k - 1))
                    values(it, k)
                if self.D == 64:
                    if cur and s == 4:
                        pe.wait_ge(self.k_ev.sem, self.k_ev.at(it, 8))
                        values_of(it, 0, 2, 4)
                    if cur and s == 5:
                        pe.wait_ge(self.q_ev.sem, self.q_ev.at(it, 8))
                        values_of(it, 0, 3, 5)
                    if prev and s == 6:
                        if cur:
                            pe.wait_ge(self.v_ev.sem, self.v_ev.at(it, 4))
                        output(it)
                    if nxt:
                        if s == 6:
                            pe.wait_ge(self.v_ev.sem, self.v_ev.at(it, 3))
                        if s == 6 and self.wlat is not None:
                            latent(it, 1)
                        q = s - 8
                        if q == 0:
                            pe.wait_ge(self.v_ev.sem, self.v_ev.at(it, 4))
                            pe.wait_ge(self.src_ready.sem, self.src_ready.at(it, 1, 1))
                            if prev:
                                pe.wait_ge(self.z_ready.sem, self.z_ready.at(it, 0))
                        if q >= 0:
                            if q >= 1:
                                pe.wait_ge(self.k_ev.sem, self.k_ev.at(it, q, 1))
                            if q == 5:
                                pe.wait_ge(self.v_ev.sem, self.v_ev.at(it, 1, 1))
                            keys(it, 1, q, 4)
                            if q >= 1:
                                pe.wait_ge(self.q_ev.sem, self.q_ev.at(it, q, 1))
                            if q == 7:
                                pe.wait_ge(self.v_ev.sem, self.v_ev.at(it, 2, 1))
                            queries(it, 1, q, 5)
                        if s == 12:
                            pe.wait_ge(self.k_ev.sem, self.k_ev.at(it, 5, 1))
                            values_of(it, 1, 0, 4)
                        if s == 14:
                            pe.wait_ge(self.q_ev.sem, self.q_ev.at(it, 7, 1))
                            values_of(it, 1, 1, 5)
                else:
                    if prev and s == 5:
                        output(it)
                    if nxt and s == 1:
                        pe.wait_ge(self.src_ready.sem, self.src_ready.at(it, 1, 1))
                        pe.wait_ge(self.q_ev.sem, self.q_ev.at(it, 16))
                        queries(it, 1, 0, 5)
                    if nxt and s == 6:
                        pe.wait_ge(self.v_ev.sem, self.v_ev.at(it, 1))
                        if not prev:
                            pe.wait_ge(self.q_dve.sem, self.q_dve.at(0, 8))
                        keys(it, 1, 0, 4)
                        small_values()

        if self.wlat is not None:
            latent(0, 0)
        else:
            pe.wait_ge(self.src_ready.sem, self.src_ready.at(0, 1))
        for q in range(self.qk_jobs):
            bank = 4 + 2 * (q % 2)
            if q >= 2:
                pe.wait_ge(self.k_ev.sem, self.k_ev.at(0, q - 1))
            keys(0, 0, q, bank)
            if self.D == 8:
                small_values()
            if q >= 2:
                pe.wait_ge(self.q_ev.sem, self.q_ev.at(0, q - 1))
            if self.D == 8:
                pe.matmul(PS[:, 7, 0:256], self.wq, self.XB, start=True, stop=True)
            queries(0, 0, q, bank + 1)
        if self.D == 64:
            pe.wait_ge(self.k_ev.sem, self.k_ev.at(0, 7))
            values_of(0, 0, 0, 4)
            pe.wait_ge(self.q_ev.sem, self.q_ev.at(0, 7))
            values_of(0, 0, 1, 5)
            pe.wait_ge(self.q_ev.sem, self.q_ev.at(0, 8))
            pe.wait_ge(self.zeros.sem, self.zeros.at(0, 1))
        self.parts(pe, part)

    def scalar(self, a):
        c, PS = self.c, self.c.PS
        a.wait_ge(self.x_ready.sem, self.x_ready.at(0, 2))

        def source(it, d):
            if self.kv == "ctx":
                a.activation(self.CB, c.CT[:, bass.ds(it * S + d * S, S)], ACT.Copy)
            a.activation(self.XB, c.XT[:, bass.ds(it * S + d * S, S)], ACT.Copy).then_inc(self.src_ready.sem, 1)

        def latent(it, d):
            a.wait_ge(self.lat_done.sem, self.lat_done.at(it, 1, d))
            a.activation(self.LT, PS[:, 4, 0:256], ACT.Copy).then_inc(self.lat_ev.sem, 1)

        def keys(it, d, q, bank):
            a.wait_ge(self.kp_done.sem, self.kp_done.at(it, q + 1, d))
            if self.D == 8:
                a.wait_ge(self.vp_done.sem, self.vp_done.at(it, 1, d))
            src = PS[:, bank, 0:256]
            if self.bk is None:
                ins = a.activation(self.KT[:, q, :], src, ACT.Copy)
            else:
                ins = a.activation(self.KT[:, q, :], src, ACT.Identity, bias=self.bk, scale=1.0)
            ins.then_inc(self.k_ev.sem, 1)

        def head_queries(h, inc=1):
            a.activation(self.QZ[:, h, :], PS[:, 5, 0:256], ACT.Identity, bias=self.qb[:, h:h + 1],
                         scale=self.qm[:, h:h + 1]).then_inc(self.q_ev.sem, inc)

        def exps(it, h):
            a.wait_ge(self.mx_done.sem, self.mx_done.at(it, h + 1))
            for col, t, n in self.spans():
                ins = a.activation(self.Pr[:, h % 4, col:col + n], PS[:, h % 2, col:col + n], ACT.Exp,
                                   bias=self.nm[:, h, t:t + 1], scale=1.0, accum_out=self.ss[:, h, t:t + 1])
            ins.then_inc(self.e_done.sem, 1)

        def part(it, prev, cur, nxt):
            if not cur:
                self.end.root(a, 0)
            for s in range(16):
                if cur:
                    if prev or s >= 4:
                        a.wait_ge(self.t_done.sem, self.t_done.at(it, s - 3))
                    exps(it, s)
                k = self.chunk_after(s, self.lag + 1)
                if k is not None and ((k < 0 and prev) or (k >= 0 and cur)):
                    a.wait_ge(self.o_done.sem, self.o_done.at(it, k + 1))
                    if k == 0 and prev:
                        a.wait_ge(self.y_done.sem, self.y_done.at(it, 0))
                    a.activation(self.OT[:, k % self.NC, :], PS[:, 6 + k % 2, 0:256], ACT.Copy)\
                        .then_inc(self.o_ev.sem, 1)
                if nxt and self.D == 64:
                    if s == 5:
                        a.wait_ge(self.vp_done.sem, self.vp_done.at(it, 4))
                        source(it, 1)
                    if s == 6 and self.wlat is not None:
                        latent(it, 1)
                    if s >= 8:
                        keys(it, 1, s - 8, 4)
                if nxt and self.D == 8:
                    if s == 0:
                        source(it, 1)
                    if s == 2:
                        a.wait_ge(self.qp_done.sem, self.qp_done.at(it, 1, 1))
                        head_queries(0)
                        head_queries(1)
                    if s >= 2:
                        head_queries(s)
                    if s == 15:
                        keys(it, 1, 0, 4)

        source(0, 0)
        if self.wlat is not None:
            latent(0, 0)
        for q in range(self.qk_jobs):
            keys(0, 0, q, 4 + 2 * (q % 2))
        if self.D == 8:
            a.wait_ge(self.qm_ready.sem, self.qm_ready.at(0, 1))
            a.wait_ge(self.qp_done.sem, self.qp_done.at(0, 1))
            for h in range(8):
                head_queries(h, 2)
        self.parts(a, part)

    def vector(self, v):
        c, PS = self.c, self.c.PS
        v.wait_ge(self.x_ready.sem, self.x_ready.at(0, 2))
        if self.causal is not None:
            v.tensor_copy(c.CMB[:, :], self.causal)
        if self.D == 8:
            c.dve.link(v, v.tensor_scalar(self.qm, self.headmask, self.scale, None, ALU.mult))
            v.tensor_scalar(self.qb, self.qm, self.bq, None, ALU.mult).then_inc(self.qm_ready.sem, 1)
            v.memset(self.V[:, :, :], 0.0)
            v.wait_ge(self.qm_ready.sem, self.qm_ready.at(0, 1))
            v.wait_ge(self.qp_done.sem, self.qp_done.at(0, 1))
            for h in range(8, 16):
                v.tensor_scalar(self.QZ[:, h, :], PS[:, 7, 0:256], self.qm[:, h:h + 1], self.qb[:, h:h + 1],
                                ALU.mult, ALU.add).then_inc(self.q_dve.sem, 1)
        c.dve.link(v, v.memset(self.nm[:, :, :], 0.0))

        def mask(it, d):
            v.tensor_scalar(self.MB, self.mask[:, bass.ds(it * 2 + 2 * d, 2), :], NEG, None, ALU.mult)\
                .then_inc(self.mask_ready.sem, 1)

        def queries(it, d, q, bank):
            v.wait_ge(self.qp_done.sem, self.qp_done.at(it, q + 1, d))
            src = PS[:, bank, 0:256]
            v.tensor_scalar(self.QZ[0:64, 2 * q, :], src[0:64], self.scale, None, ALU.mult)
            v.tensor_scalar(self.QZ[64:128, 2 * q + 1, :], src[64:128], self.scale, None, ALU.mult)\
                .then_inc(self.q_ev.sem, 1)

        def values_of(it, d, n, bank):
            v.wait_ge(self.vp_done.sem, self.vp_done.at(it, n + 1, d))
            h, t = divmod(n, 2)
            v.tensor_copy(self.V[:, t, h * 512:h * 512 + 512], PS[:, bank, :]).then_inc(self.v_ev.sem, 1)

        def small_values(it):
            v.wait_ge(self.vp_done.sem, self.vp_done.at(it, 1))
            for t in range(2):
                dst = self.V[:, t, 0:512].rearrange("p (h e) -> p h e", e=32)[:, :, 0:8]
                src = PS[:, 4, 256 + t * P:256 + (t + 1) * P].rearrange("p (h e) -> p h e", e=8)
                ins = v.tensor_tensor(dst, src, self.bv.rearrange("p (h e) -> p h e", e=8), ALU.add)
            ins.then_inc(self.v_ev.sem, 1)

        def maxima(it, h):
            v.wait_ge(self.s_done.sem, self.s_done.at(it, h + 1))
            if self.causal is not None:
                v.tensor_reduce(self.nm[:, h, 0:1], PS[:, h % 2, 0:128], AX.X, ALU.max, negate=True)
                ins = v.tensor_reduce(self.nm[:, h, 1:2], PS[:, h % 2, 128:384], AX.X, ALU.max, negate=True)
            else:
                ins = v.tensor_reduce(self.nm[:, h, :], two(PS[:, h % 2, :]), AX.X, ALU.max, negate=True)
            ins.then_inc(self.mx_done.sem, 1)

        def reciprocals(it, h):
            v.wait_ge(self.e_done.sem, self.e_done.at(it, h + 1))
            h %= self.H
            if self.causal is not None:
                v.reciprocal(self.ri[:, h, 0:2], self.ss[:, h, :])
                ins = v.reciprocal(self.ri[:, h, 2:3], self.ss[:, h, 1:2])
            else:
                ins = v.reciprocal(self.ri[:, h, 0:2], self.ss[:, h, :])
            ins.then_inc(self.r_done.sem, 1)

        def spread(it, h):
            v.wait_ge(self.t_done.sem, self.t_done.at(it, h + 1))
            w = self.width()
            v.tensor_copy(self.PT[:, h % self.NPT, 0:w], PS[:, 2 + h % 2, 0:w]).then_inc(self.pt_ev.sem, 1)

        def output(it):
            v.wait_ge(self.y_done.sem, self.y_done.at(it, 0))
            zt = c.Z[:, bass.ds(it * 2 - 2, 2), :]
            xt = c.X[:, bass.ds(it * 2 - 2, 2), :]
            y = two(PS[:, self.ybank, 0:256])
            if self.bo is None:
                v.tensor_tensor(zt, y, xt, ALU.add).then_inc(self.z_ready.sem, 1)
            else:
                c.dve.link(v, v.tensor_tensor(zt, y, xt, ALU.add))
                v.tensor_tensor(zt, zt, self.bo.unsqueeze(1).to_broadcast([P, 2, P]), ALU.add)\
                    .then_inc(self.z_ready.sem, 1)

        def part(it, prev, cur, nxt):
            def live(h):
                return (h < 0 and prev) or (h >= 0 and cur)

            for s in range(16):
                if cur:
                    maxima(it, s)
                if live(s - 1):
                    reciprocals(it, s - 1)
                h = s - 3
                if live(h):
                    if prev or h >= self.NPT:
                        v.wait_ge(self.o_done.sem, self.o_done.at(it, (h - self.NPT) // self.hpc + 1))
                    spread(it, h)
                if prev and not nxt and cur and s == 12:
                    self.end.early_stats(v)
                if not cur and s == 2:
                    self.end.tiles(v, 0)
                if self.D == 64:
                    if cur and s in (4, 5):
                        values_of(it, 0, s - 2, s)
                    if prev and s == 6:
                        output(it)
                    if nxt and s >= 8:
                        queries(it, 1, s - 8, 5)
                    if nxt and s in (12, 14):
                        values_of(it, 1, (s - 12) // 2, 4 + (s - 12) // 2)
                    if nxt and s == 15 and self.mask is not None:
                        mask(it, 1)
                else:
                    if cur and s == 4:
                        if prev:
                            v.wait_ge(self.o_done.sem, self.o_done.at(it, 0))
                        small_values(it)
                    if prev and s == 6:
                        output(it)

        if self.mask is not None:
            mask(0, 0)
        if self.D == 64:
            for q in range(8):
                queries(0, 0, q, 5 + 2 * (q % 2))
            values_of(0, 0, 0, 4)
            values_of(0, 0, 1, 5)
        self.parts(v, part, c.dve)
        v.wait_ge(self.z_ready.sem, self.z_ready.at(B - 1, 1))

    def gpsimd(self, g):
        if self.D == 64:
            g.wait_ge(self.x_ready.sem, self.x_ready.at(0, 2))
            g.memset(self.QZ[0:64, 1:16:2, :], 0.0)
            g.memset(self.QZ[64:128, 0:16:2, :], 0.0).then_inc(self.zeros.sem, 1)
        with g.Fori(0, B) as it:
            for h in range(self.H):
                g.wait_ge(self.r_done.sem, self.r_done.at(it, h + 1))
                n = 3 if self.causal is not None else 2
                w = self.width()
                p = self.Pr[:, h % 4, 0:w].rearrange("p (a b) -> p a b", a=n)
                g.tensor_tensor(p, p, self.ri[:, h, 0:n].unsqueeze(2).to_broadcast([P, n, w // n]), ALU.mult)\
                    .then_inc(self.pn_done.sem, 1)


class Experts:

    ITERS, TOK, NT = 2, 512, 4

    def __init__(self, c, n_routed, full, rest, wgu, wrest, wdown, wdrest, router, iota, gated, tiny):
        self.c, self.E, self.full, self.rest = c, n_routed, full, rest
        self.wgu, self.wrest, self.wdown, self.wdrest, self.router = wgu, wrest, wdown, wdrest, router
        self.iota, self.gated, self.tiny = iota, gated, tiny
        self.NE = n_routed + 1
        self.blocks = full + (1 if rest else 0)
        self.cols = 8 + (1 if gated else 0)
        self.x_ready = c.x_ready
        s = c.sig
        n = self.NE * self.blocks
        self.logits_done = s("logits_done", 1, 1)
        self.shift_ready = s("shift_ready", 1, 1)
        self.exp_ready = s("exp_ready", 1, 1)
        self.gu_done = s("gu_done", n, 2)
        self.silu_done = s("silu_done", n, 2)
        self.h_ready = s("h_ready", n, 2)
        self.eo_done = s("eo_done", self.NE, 2)
        self.add_done = s("add_done", self.NE, 2)
        self.z_ready = self.add_done
        t = c.take
        self.SL = t(0, 2, 512)
        self.Hd = t(1024, 3, 512)
        self.lg = t(2560, T, 9)
        self.mx = t(2640, T)
        self.sm = t(2650, T)
        self.pr = t(2660, T, 8)
        self.top = t(2724, T, 8)
        self.idx = t(2788, T, 8).bitcast(mybir.dt.uint32)
        self.idf = t(2852, T, 8)
        self.dn = t(2916, T)
        self.wt = t(2930, T, 2)
        self.eq = t(2950, T, 8)
        self.eq2 = t(3014, T, 8)
        self.comb = t(3078, T, 9)

    def tensor(self, pe):
        c, PS = self.c, self.c.PS
        pe.wait_ge(self.x_ready.sem, self.x_ready.at(0, 2))
        for n in range(T):
            ins = pe.matmul(PS[:, 6, n * self.cols:(n + 1) * self.cols], c.XT[:, n * P:(n + 1) * P], self.router,
                            start=True, stop=True, skip_group_check=True)
        ins.then_inc(self.logits_done.sem, 1)
        with pe.Fori(0, self.ITERS) as it:
            x = c.XT[:, bass.ds(it * self.TOK, self.TOK)]

            def gate_up(j):
                e, f = divmod(j, self.blocks)
                if j >= 2:
                    pe.wait_ge(self.h_ready.sem, self.h_ready.at(it, j - 1))
                if f < self.full:
                    w = self.wgu[:, e * self.full + f, :]
                    pe.matmul(PS[:, j % 2, :], w[:, 0:P], x, start=True, stop=True)
                    pe.matmul(PS[:, 2 + j % 2, :], w[:, P:2 * P], x, start=True, stop=True)\
                        .then_inc(self.gu_done.sem, 1)
                else:
                    pe.matmul(PS[0:64 + self.rest, j % 2, :], self.wrest[:, e, :], x, start=True, stop=True)\
                        .then_inc(self.gu_done.sem, 1)

            def down(j):
                e, f = divmod(j, self.blocks)
                pe.wait_ge(self.h_ready.sem, self.h_ready.at(it, j + 1))
                if f == 0 and e >= 2:
                    pe.wait_ge(self.add_done.sem, self.add_done.at(it, e - 1))
                rows = P if f < self.full else self.rest
                w = self.wdown[:, e * self.full + f, :] if f < self.full else self.wdrest[:, e, :]
                for t in range(self.NT):
                    ins = pe.matmul(PS[:, 4 + e % 2, t * P:(t + 1) * P], self.Hd[0:rows, j % 3, t * P:(t + 1) * P], w,
                                    start=(f == 0 and t == 0), stop=(f == self.blocks - 1), skip_group_check=True)
                if f == self.blocks - 1:
                    ins.then_inc(self.eo_done.sem, 1)

            n = self.NE * self.blocks
            for j in range(n + 1):
                if j < n:
                    gate_up(j)
                if j >= 1:
                    down(j - 1)

    def scalar(self, a):
        c, PS = self.c, self.c.PS
        a.wait_ge(self.shift_ready.sem, self.shift_ready.at(0, 1))
        a.activation(self.lg[:, :, 0:self.cols], self.lg[:, :, 0:self.cols], ACT.Exp).then_inc(self.exp_ready.sem, 1)
        with a.Fori(0, self.ITERS) as it:
            for j in range(self.NE * self.blocks):
                f = j % self.blocks
                a.wait_ge(self.gu_done.sem, self.gu_done.at(it, j + 1))
                if f < self.full:
                    ins = a.activation(self.SL[:, j % 2, :], PS[:, j % 2, :], ACT.Silu)
                else:
                    ins = a.activation(self.SL[64:64 + self.rest, j % 2, :], PS[0:self.rest, j % 2, :], ACT.Silu)
                ins.then_inc(self.silu_done.sem, 1)

    def vector(self, v):
        c, PS = self.c, self.c.PS
        E, cols = self.E, self.cols

        def link(ins):
            c.dve.link(v, ins)

        def each(ap, n):
            return ap.unsqueeze(2).to_broadcast([P, T, n])

        v.wait_ge(self.logits_done.sem, self.logits_done.at(0, 1))
        lgp = PS[:, 6, 0:T * cols].rearrange("p (t e) -> p t e", t=T)
        link(v.tensor_copy(self.lg[:, :, 0:cols], lgp))
        if E < 8:
            link(v.memset(self.lg[:, :, E:8], NEG))
        link(v.tensor_reduce(self.mx, self.lg[:, :, 0:8], AX.X, ALU.max))
        if self.gated:
            link(v.tensor_scalar(self.lg[:, :, 8:9], self.lg[:, :, 8:9], -1.0, None, ALU.mult))
        v.tensor_tensor(self.lg[:, :, 0:8], self.lg[:, :, 0:8], each(self.mx, 8), ALU.subtract)\
            .then_inc(self.shift_ready.sem, 1)

        def largest():
            v.wait_ge(self.exp_ready.sem, self.exp_ready.at(0, 1))
            link(v.tensor_reduce(self.sm, self.lg[:, :, 0:8], AX.X, ALU.add))
            link(v.reciprocal(self.sm, self.sm))
            link(v.tensor_tensor(self.pr, self.lg[:, :, 0:8], each(self.sm, 8), ALU.mult))
            for n in range(T):
                ins = v.max(self.top[:, n, :], self.pr[:, n, :])
            link(ins)
            for n in range(T):
                ins = v.max_index(self.idx[:, n, :], self.top[:, n, :], self.pr[:, n, :])
            link(ins)

        def weights():
            link(v.tensor_copy(self.idf, self.idx))
            link(v.tensor_reduce(self.dn, self.top[:, :, 0:2], AX.X, ALU.add))
            if self.tiny:
                link(v.tensor_scalar(self.dn, self.dn, self.tiny, None, ALU.add))
            link(v.reciprocal(self.dn, self.dn))
            link(v.tensor_tensor(self.wt, self.top[:, :, 0:2], each(self.dn, 2), ALU.mult))

        def shares():
            iota = self.iota.unsqueeze(1).to_broadcast([P, T, 8])
            for i, eq in enumerate((self.eq, self.eq2)):
                link(v.tensor_tensor(eq, iota, each(self.idf[:, :, i], 8), ALU.is_equal))
                link(v.tensor_tensor(eq, eq, each(self.wt[:, :, i], 8), ALU.mult))
            link(v.tensor_tensor(self.comb[:, :, 0:8], self.eq, self.eq2, ALU.add))
            if self.gated:
                link(v.tensor_scalar(self.comb[:, :, E:E + 1], self.lg[:, :, 8:9], 1.0, None, ALU.add))
                link(v.reciprocal(self.comb[:, :, E:E + 1], self.comb[:, :, E:E + 1]))
            else:
                link(v.memset(self.comb[:, :, E:E + 1], 1.0))

        def tokens(it, first):
            def hidden(j):
                f = j % self.blocks
                v.wait_ge(self.silu_done.sem, self.silu_done.at(it, j + 1))
                if f < self.full:
                    ins = v.tensor_tensor(self.Hd[:, j % 3, :], self.SL[:, j % 2, :], PS[:, 2 + j % 2, :], ALU.mult)
                else:
                    r = slice(64, 64 + self.rest)
                    ins = v.tensor_tensor(self.Hd[0:self.rest, j % 3, :], self.SL[r, j % 2, :], PS[r, j % 2, :],
                                          ALU.mult)
                ins.then_inc(self.h_ready.sem, 1)

            def add(e):
                v.wait_ge(self.eo_done.sem, self.eo_done.at(it, e + 1))
                if e >= 1:
                    v.wait_ge(self.add_done.sem, self.add_done.at(it, e))
                for t in range(self.NT):
                    n = it * self.NT + t
                    z = c.Z[:, bass.ds(n, 1), :]
                    r = c.X[:, bass.ds(n, 1), :] if e == 0 else z
                    ins = v.scalar_tensor_tensor(z, PS[:, 4 + e % 2, t * P:(t + 1) * P].unsqueeze(1),
                                                 self.comb[:, bass.ds(n, 1), e], r, ALU.mult, ALU.add)
                ins.then_inc(self.add_done.sem, 1)

            n = self.NE * self.blocks
            for j in range(n):
                hidden(j)
                if first and j < 2:
                    (weights, shares)[j]()
                if j % self.blocks == min(1, self.blocks - 1) and j >= self.blocks:
                    add(j // self.blocks - 1)
            add(self.NE - 1)
            v.wait_ge(self.add_done.sem, self.add_done.at(it, self.NE))
            self.end.count(v, it * self.NT, self.NT)

        largest()
        for i in range(self.ITERS):
            tokens(i, i == 0)
        v.wait_ge(self.add_done.sem, self.add_done.at(self.ITERS - 1, self.NE))

    def gpsimd(self, g):
        pass


MAGIC = 1.5 * 2.0 ** 23


class BitLinear:

    def __init__(self, c, w1, w2, cw, cb):
        self.c, self.w1, self.w2, self.cw, self.cb = c, w1, w2, cw, cb
        self.x_ready = c.x_ready
        s = c.sig
        self.abs_ready = s("abs_ready", 1, 1)
        self.tot_done = s("tot_done", 1, 1)
        self.w_ready = s("w_ready", 1, 1)
        self.xq_ready = s("xq_ready", T, 1)
        self.xt_done = s("xt_done", 2, 1)
        self.xt_ev = s("xt_ev", 2, 1)
        self.hp_zero = s("hp_zero", 1, 1)
        self.h_done = s("h_done", 4)
        self.h_ev = s("h_ev", 4)
        self.cv_ready = s("cv_ready", 4)
        self.sl_ready = s("sl_ready", 4)
        self.ht_done = s("ht_done", 2)
        self.hq_ready = s("hq_ready", 2)
        self.hqt_done = s("hqt_done", 2)
        self.hqt_ev = s("hqt_ev", 2)
        self.y_done = s("y_done", 1)
        self.z_ready = s("z_ready", 1)
        t = c.take
        self.W1 = t(0, 512)
        self.W2 = t(512, 4, 128)
        self.ab = t(1024, 2)
        self.sc = t(1030, 2)
        self.isc = t(1034, 2)
        self.tmp = t(1040, 512)
        self.am = t(1560, T)
        self.s1 = t(1568, T)
        self.i1 = t(1576, T)
        self.xq = t(8000, T, 128)
        self.xqt = t(9024, T * P)
        self.hp = t(2112, 4, 258)
        self.cv = t(3160, 4, 256)
        self.sl = t(4200, 4, 256)
        self.hq = t(5300, 2, 512)
        self.hqt = t(6400, 2, 512)
        self.am2 = t(7500, 2)
        self.s2 = t(7504, 2)
        self.i2 = t(7508, 2)

    def tensor(self, pe):
        c, PS = self.c, self.c.PS
        pe.wait_ge(self.abs_ready.sem, self.abs_ready.at(0, 1))
        pe.matmul(PS[:, 7, 0:2], c.one.to_broadcast([P, P]), self.ab, start=True, stop=True).then_inc(self.tot_done.sem, 1)
        pe.wait_ge(self.w_ready.sem, self.w_ready.at(0, 1))
        for n in range(T):
            pe.wait_ge(self.xq_ready.sem, self.xq_ready.at(0, n + 1))
            ins = pe.transpose(PS[:, 4 + n // 4, (n % 4) * P:(n % 4) * P + P], self.xq[:, n, :], c.ident)
            if n % 4 == 3:
                ins.then_inc(self.xt_done.sem, 1)
        pe.wait_ge(self.w_ready.sem, self.w_ready.at(0, 1))
        pe.wait_ge(self.xt_ev.sem, self.xt_ev.at(0, 2))

        def up(it, d, f, first):
            if f >= 2 or not first:
                pe.wait_ge(self.h_ev.sem, self.h_ev.at(it, f - 1, d))
            pe.matmul(PS[:, f % 2, 0:256], self.W1[:, f * P:(f + 1) * P], self.xqt[:, bass.ds(it * S + d * S, S)],
                      start=True, stop=True).then_inc(self.h_done.sem, 1)

        def batch(it, more):
            for t in range(2):
                for f in range(4):
                    pe.wait_ge(self.sl_ready.sem, self.sl_ready.at(it, f + 1))
                    ins = pe.transpose(PS[:, 2 + t, f * P:(f + 1) * P], self.sl[:, f, t * P:(t + 1) * P], c.ident)
                ins.then_inc(self.ht_done.sem, 1)
            if more:
                for f in range(4):
                    up(it, 1, f, False)
            for t in range(2):
                pe.wait_ge(self.hq_ready.sem, self.hq_ready.at(it, t + 1))
                for f in range(4):
                    ins = pe.transpose(PS[:, 4 + t, f * P:(f + 1) * P], self.hq[:, t, f * P:(f + 1) * P], c.ident)
                ins.then_inc(self.hqt_done.sem, 1)
            pe.wait_ge(self.z_ready.sem, self.z_ready.at(it, 0))
            for t in range(2):
                pe.wait_ge(self.hqt_ev.sem, self.hqt_ev.at(it, t + 1))
                for f in range(4):
                    ins = pe.matmul(PS[:, 7, t * P:(t + 1) * P], self.hqt[:, t, f * P:(f + 1) * P], self.W2[:, f, :],
                                    start=(f == 0), stop=(f == 3))
            ins.then_inc(self.y_done.sem, 1)

        for f in range(4):
            up(0, 0, f, True)
        with pe.Fori(0, B - 1) as it:
            batch(it, True)
        batch(B - 1, False)

    def scalar(self, a):
        c, PS = self.c, self.c.PS
        c.act.link(a, a.activation(self.tmp, self.w1, ACT.Abs, accum_out=self.ab[:, 0:1]))
        a.activation(self.tmp, self.w2.rearrange("p a b -> p (a b)"), ACT.Abs, accum_out=self.ab[:, 1:2])\
            .then_inc(self.abs_ready.sem, 1)
        for i in range(2):
            a.wait_ge(self.xt_done.sem, self.xt_done.at(0, i + 1))
            a.activation(self.xqt[:, i * 512:i * 512 + 512], PS[:, 4 + i, :], ACT.Copy).then_inc(self.xt_ev.sem, 1)

        def hidden(it, d, f):
            a.wait_ge(self.h_done.sem, self.h_done.at(it, f + 1, d))
            a.activation(self.hp[:, f, 1:257], PS[:, f % 2, 0:256], ACT.Copy)
            a.activation(self.cv[:, f, :], PS[:, f % 2, 0:256], ACT.Identity, bias=self.cb[:, f:f + 1],
                         scale=self.cw[:, f, 1:2]).then_inc(self.h_ev.sem, 1)

        def batch(it, more):
            for f in range(4):
                a.wait_ge(self.cv_ready.sem, self.cv_ready.at(it, f + 1))
                a.activation(self.sl[:, f, :], self.cv[:, f, :], ACT.Silu).then_inc(self.sl_ready.sem, 1)
            if more:
                for f in range(4):
                    hidden(it, 1, f)
            for t in range(2):
                a.wait_ge(self.hqt_done.sem, self.hqt_done.at(it, t + 1))
                a.activation(self.hqt[:, t, :], PS[:, 4 + t, :], ACT.Copy).then_inc(self.hqt_ev.sem, 1)

        a.wait_ge(self.hp_zero.sem, self.hp_zero.at(0, 1))
        for f in range(4):
            hidden(0, 0, f)
        with a.Fori(0, B - 1) as it:
            batch(it, True)
        batch(B - 1, False)

    def vector(self, v):
        c, PS = self.c, self.c.PS

        def link(ins):
            c.dve.link(v, ins)

        v.memset(self.hp, 0.0).then_inc(self.hp_zero.sem, 1)
        v.wait_ge(self.x_ready.sem, self.x_ready.at(0, 2))

        def scales(am, s, i):
            link(v.tensor_scalar(i, am, 1e-5, None, ALU.max))
            link(v.reciprocal(s, i))
            v.tensor_scalar(s, s, 127.0, None, ALU.mult)
            link(v.tensor_scalar(i, i, 1.0 / 127.0, None, ALU.mult))

        def quantise(dst, src, s, i, ready):
            link(v.tensor_scalar(dst, src, s, MAGIC, ALU.mult, ALU.add))
            link(v.tensor_scalar(dst, dst, MAGIC, 127.0, ALU.subtract, ALU.min))
            v.tensor_scalar(dst, dst, -128.0, i, ALU.max, ALU.mult).then_inc(ready.sem, 1)

        link(v.tensor_reduce(self.am, c.X[:, :, :], AX.X, ALU.max, apply_absolute_value=True))
        scales(self.am, self.s1, self.i1)
        for n in range(T):
            quantise(self.xq[:, n, :], c.X[:, n, :], self.s1[:, n:n + 1], self.i1[:, n:n + 1], self.xq_ready)
        v.wait_ge(self.tot_done.sem, self.tot_done.at(0, 1))
        link(v.tensor_scalar(self.isc, PS[:, 7, 0:2], 1.0 / 65536.0, 1e-5, ALU.mult, ALU.max))
        link(v.reciprocal(self.sc, self.isc))
        w1, w2 = self.w1, self.w2.rearrange("p a b -> p (a b)")
        W2 = self.W2.rearrange("p a b -> p (a b)")
        for i, (src, dst) in enumerate(((w1, self.W1), (w2, W2))):
            link(v.tensor_scalar(dst, src, self.sc[:, i:i + 1], MAGIC, ALU.mult, ALU.add))
            link(v.tensor_scalar(dst, dst, MAGIC, 1.0, ALU.subtract, ALU.min))
            link(v.tensor_scalar(dst, dst, -1.0, self.isc[:, i:i + 1], ALU.max, ALU.mult))
        v.tensor_copy(self.ab, self.sc).then_inc(self.w_ready.sem, 1)

        def convolve(it, d, f):
            v.wait_ge(self.h_ev.sem, self.h_ev.at(it, f + 1, d))
            h, cv = self.hp[:, f, :], self.cv[:, f, :]
            link(v.scalar_tensor_tensor(cv, h[:, 0:256], self.cw[:, f, 0:1], cv, ALU.mult, ALU.add))
            v.scalar_tensor_tensor(cv, h[:, 2:258], self.cw[:, f, 2:3], cv, ALU.mult, ALU.add)\
                .then_inc(self.cv_ready.sem, 1)

        def batch(it, more):
            for t in range(2):
                v.wait_ge(self.ht_done.sem, self.ht_done.at(it, t + 1))
                h, u = PS[:, 2 + t, :], slice(t, t + 1)
                link(v.tensor_reduce(self.am2[:, u], h, AX.X, ALU.max, apply_absolute_value=True))
                scales(self.am2[:, u], self.s2[:, u], self.i2[:, u])
                quantise(self.hq[:, t, :], h, self.s2[:, u], self.i2[:, u], self.hq_ready)
            if more:
                for f in range(4):
                    convolve(it, 1, f)
            v.wait_ge(self.y_done.sem, self.y_done.at(it, 1))
            v.tensor_tensor(c.Z[:, bass.ds(it * 2, 2), :], two(PS[:, 7, 0:256]), c.X[:, bass.ds(it * 2, 2), :],
                            ALU.add).then_inc(self.z_ready.sem, 1)

        for f in range(4):
            convolve(0, 0, f)
        with v.Fori(0, B - 1) as it:
            c.dve.enter(it)
            batch(it, True)
        c.dve.leave(B - 1)
        batch(B - 1, False)
        v.wait_ge(self.z_ready.sem, self.z_ready.at(B - 1, 1))

    def gpsimd(self, g):
        pass


class TwoWay:

    def __init__(self, c, w, bq, bk, bv, wg, nbg):
        self.c, self.w, self.bq, self.bk, self.bv, self.wg, self.nbg = c, w, bq, bk, bv, wg, nbg
        self.x_ready = c.x_ready
        s = c.sig
        self.src_ready = s("src_ready", 1)
        self.qk_done = s("p_done", 4)
        self.q_ev = s("q_ev", 2)
        self.k_ev = s("k_ev", 2)
        self.v_done = s("vp_done", 2)
        self.v_ev = s("v_ev", 2)
        self.s_done = s("s_done", 2)
        self.mx_done = s("mx_done", 2)
        self.e_done = s("e_done", 2)
        self.pn_done = s("pn_done", 2)
        self.t_done = s("t_done", 2)
        self.pt_ev = s("pt_ev", 2)
        self.o_done = s("o_done", 2)
        self.o_ev = s("o_ev", 2)
        self.g_done = s("g_done", 1)
        self.g_exp = s("g_exp", 1)
        self.y_ready = s("y_ready", 1)
        self.y_done = s("y_done", 1)
        self.z_ready = s("z_ready", 1)
        t = c.take
        self.XB, self.CB = t(0, 256), t(256, 256)
        self.Q, self.K = t(512, 2, 256), t(1024, 2, 256)
        self.V = t(1536, 2, 2, 128)
        self.Pr, self.PT = t(2048, 2, 512), t(3072, 2, 512)
        self.O = t(4096, 2, 256)
        self.G, self.D, self.Y = t(4608, 256), t(4864, 256), t(5120, 256)
        self.nm, self.ss, self.ri = t(5400, 2, 2), t(5404, 2, 2), t(5408, 2, 2)
        self.nb = t(5412, 1)

    def tensor(self, pe):
        c, PS = self.c, self.c.PS

        def queries_keys(it, d):
            pe.wait_ge(self.src_ready.sem, self.src_ready.at(it, 1, d))
            for i in range(2):
                qs, ks = (self.XB, self.CB) if i == 0 else (self.CB, self.XB)
                pe.matmul(PS[:, 2 * i, 0:256], self.w[:, 3 * i, :], qs, start=True, stop=True)\
                    .then_inc(self.qk_done.sem, 1)
                pe.matmul(PS[:, 2 * i + 1, 0:256], self.w[:, 3 * i + 1, :], ks, start=True, stop=True)\
                    .then_inc(self.qk_done.sem, 1)

        def values_of(bank):
            for i in range(2):
                ks = self.CB if i == 0 else self.XB
                for t in range(2):
                    ins = pe.matmul(PS[:, bank + i, t * P:(t + 1) * P], ks[:, t * P:(t + 1) * P],
                                    self.w[:, 3 * i + 2, :], start=True, stop=True)
                ins.then_inc(self.v_done.sem, 1)

        def scores(it, d):
            for i in range(2):
                pe.wait_ge(self.q_ev.sem, self.q_ev.at(it, i + 1, d))
                pe.wait_ge(self.k_ev.sem, self.k_ev.at(it, i + 1, d))
                for t in range(2):
                    ins = pe.matmul(PS[:, 6 + i, t * 256:t * 256 + 256], self.Q[:, i, t * P:(t + 1) * P],
                                    self.K[:, i, :], start=True, stop=True)
                ins.then_inc(self.s_done.sem, 1)

        def batch(it, more):
            pe.wait_ge(self.v_ev.sem, self.v_ev.at(it, 2))
            if more:
                queries_keys(it, 1)
            for i in range(2):
                pe.wait_ge(self.pn_done.sem, self.pn_done.at(it, i + 1))
                if more and i == 0:
                    pe.wait_ge(self.q_ev.sem, self.q_ev.at(it, 1, 1))
                if more and i == 1:
                    pe.wait_ge(self.k_ev.sem, self.k_ev.at(it, 1, 1))
                for a, b in [(0, 0), (256, 128), (128, 256), (384, 384)]:
                    ins = pe.transpose(PS[:, i, b:b + P], self.Pr[:, i, a:a + P], c.ident)
                ins.then_inc(self.t_done.sem, 1)
            for i in range(2):
                pe.wait_ge(self.pt_ev.sem, self.pt_ev.at(it, i + 1))
                if more and i == 0:
                    pe.wait_ge(self.q_ev.sem, self.q_ev.at(it, 2, 1))
                if more and i == 1:
                    pe.wait_ge(self.k_ev.sem, self.k_ev.at(it, 2, 1))
                for kt in range(2):
                    ins = pe.matmul(PS[:, 2 + i, 0:256], self.V[:, i, kt, :], self.PT[:, i, kt * 256:kt * 256 + 256],
                                    start=(kt == 0), stop=(kt == 1))
                ins.then_inc(self.o_done.sem, 1)
            if more:
                values_of(0)
                scores(it, 1)
            for i in range(2):
                pe.wait_ge(self.o_ev.sem, self.o_ev.at(it, i + 1))
                ins = pe.matmul(PS[:, 4, 0:256], self.wg[:, i, :], self.O[:, i, :], start=(i == 0), stop=(i == 1))
            ins.then_inc(self.g_done.sem, 1)
            pe.wait_ge(self.y_ready.sem, self.y_ready.at(it, 1))
            for t in range(2):
                ins = pe.transpose(PS[:, 5, t * P:(t + 1) * P], self.Y[:, t * P:(t + 1) * P], c.ident)
            ins.then_inc(self.y_done.sem, 1)

        queries_keys(0, 0)
        values_of(4)
        scores(0, 0)
        with pe.Fori(0, B - 1) as it:
            batch(it, True)
        batch(B - 1, False)

    def scalar(self, a):
        c, PS = self.c, self.c.PS
        a.wait_ge(self.x_ready.sem, self.x_ready.at(0, 2))

        def source(it, d):
            if d:
                a.wait_ge(self.v_done.sem, self.v_done.at(it, 2))
            a.activation(self.CB, c.CT[:, bass.ds(it * S + d * S, S)], ACT.Copy)
            a.activation(self.XB, c.XT[:, bass.ds(it * S + d * S, S)], ACT.Copy).then_inc(self.src_ready.sem, 1)

        def keys(it, d):
            for i in range(2):
                a.wait_ge(self.qk_done.sem, self.qk_done.at(it, 2 * i + 2, d))
                a.activation(self.K[:, i, :], PS[:, 2 * i + 1, 0:256], ACT.Identity, bias=self.bk[:, i:i + 1],
                             scale=1.0).then_inc(self.k_ev.sem, 1)

        def batch(it, more):
            if more:
                source(it, 1)
            for i in range(2):
                a.wait_ge(self.mx_done.sem, self.mx_done.at(it, i + 1))
                for t in range(2):
                    ins = a.activation(self.Pr[:, i, t * 256:t * 256 + 256], PS[:, 6 + i, t * 256:t * 256 + 256],
                                       ACT.Exp, bias=self.nm[:, i, t:t + 1], scale=1.0,
                                       accum_out=self.ss[:, i, t:t + 1])
                ins.then_inc(self.e_done.sem, 1)
            if more:
                keys(it, 1)
            for i in range(2):
                a.wait_ge(self.o_done.sem, self.o_done.at(it, i + 1))
                a.activation(self.O[:, i, :], PS[:, 2 + i, 0:256], ACT.Copy).then_inc(self.o_ev.sem, 1)
            a.wait_ge(self.g_done.sem, self.g_done.at(it, 1))
            a.activation(self.G, PS[:, 4, 0:256], ACT.Exp, bias=self.nb, scale=-1.0).then_inc(self.g_exp.sem, 1)

        source(0, 0)
        keys(0, 0)
        with a.Fori(0, B - 1) as it:
            batch(it, True)
        batch(B - 1, False)

    def vector(self, v):
        c, PS = self.c, self.c.PS

        def link(ins):
            c.dve.link(v, ins)

        link(v.tensor_scalar(self.nb, self.nbg, -1.0, None, ALU.mult))
        v.wait_ge(self.x_ready.sem, self.x_ready.at(0, 2))

        def queries(it, d):
            for i in range(2):
                v.wait_ge(self.qk_done.sem, self.qk_done.at(it, 2 * i + 1, d))
                v.tensor_scalar(self.Q[:, i, :], PS[:, 2 * i, 0:256], self.bq[:, i:i + 1], float(P) ** -0.5,
                                ALU.add, ALU.mult).then_inc(self.q_ev.sem, 1)

        def values_of(it, d, bank):
            for i in range(2):
                v.wait_ge(self.v_done.sem, self.v_done.at(it, i + 1, d))
                v.tensor_tensor(self.V[:, i, :, :], two(PS[:, bank + i, 0:256]),
                                self.bv[:, i, :].unsqueeze(1).to_broadcast([P, 2, P]), ALU.add)\
                    .then_inc(self.v_ev.sem, 1)

        def maxima(it, d):
            for i in range(2):
                v.wait_ge(self.s_done.sem, self.s_done.at(it, i + 1, d))
                v.tensor_reduce(self.nm[:, i, :], two(PS[:, 6 + i, :]), AX.X, ALU.max, negate=True)\
                    .then_inc(self.mx_done.sem, 1)

        def batch(it, more):
            if more:
                queries(it, 1)
            for i in range(2):
                v.wait_ge(self.e_done.sem, self.e_done.at(it, i + 1))
                link(v.reciprocal(self.ri[:, i, :], self.ss[:, i, :]))
                p = two(self.Pr[:, i, :])
                v.tensor_tensor(p, p, self.ri[:, i, :].unsqueeze(2).to_broadcast([P, 2, 256]), ALU.mult)\
                    .then_inc(self.pn_done.sem, 1)
            for i in range(2):
                v.wait_ge(self.t_done.sem, self.t_done.at(it, i + 1))
                v.tensor_copy(self.PT[:, i, :], PS[:, i, :]).then_inc(self.pt_ev.sem, 1)
            if more:
                values_of(it, 1, 0)
            v.wait_ge(self.o_ev.sem, self.o_ev.at(it, 2))
            link(v.tensor_tensor(self.D, self.O[:, 0, :], self.O[:, 1, :], ALU.subtract))
            if more:
                maxima(it, 1)
            v.wait_ge(self.g_exp.sem, self.g_exp.at(it, 1))
            link(v.tensor_scalar(self.G, self.G, 1.0, None, ALU.add))
            link(v.reciprocal(self.G, self.G))
            link(v.tensor_tensor(self.D, self.D, self.G, ALU.mult))
            v.tensor_tensor(self.Y, self.D, self.O[:, 1, :], ALU.add).then_inc(self.y_ready.sem, 1)
            v.wait_ge(self.y_done.sem, self.y_done.at(it, 1))
            v.tensor_tensor(c.Z[:, bass.ds(it * 2, 2), :], two(PS[:, 5, 0:256]), c.X[:, bass.ds(it * 2, 2), :],
                            ALU.add).then_inc(self.z_ready.sem, 1)

        queries(0, 0)
        values_of(0, 0, 4)
        maxima(0, 0)
        with v.Fori(0, B - 1) as it:
            c.dve.enter(it)
            batch(it, True)
        c.dve.leave(B - 1)
        batch(B - 1, False)
        v.wait_ge(self.z_ready.sem, self.z_ready.at(B - 1, 1))

    def gpsimd(self, g):
        pass


WIN_Q, WINDOWS = 96, ((0, 0), (96, 80), (160, 128))


def window_tables():
    i, j = np.arange(WIN_Q)[:, None], np.arange(P)[None, :]
    rel = np.stack([(q0 + i) - (k0 + j) for q0, k0 in WINDOWS], 1).astype(np.float32)
    return rel, np.where(np.abs(rel) <= 16, 0.0, NEG).astype(np.float32)


class BandedAttention(Attention):

    hpc, NC, NPT = 4, 4, 8

    def __init__(self, c, wq, wk, wv, wo, slopes, rel, band, headmask, spare):
        self.c, self.wq, self.wk, self.wv, self.wo = c, wq, wk, wv, wo
        self.slopes, self.rel, self.band, self.headmask = slopes, rel, band, headmask
        self.causal = None
        self.x_ready = c.x_ready
        s = c.sig
        self.src_ready = s("src_ready", 1)
        self.kp_done, self.k_ev = s("kp_done", 1), s("k_ev", 1)
        self.qp_done, self.qb_ready = s("qp_done", 1), s("qb_ready", 1)
        self.q_ev = s("q_ev", 8)
        self.vp_done, self.v_ev = s("vp_done", 1), s("v_ev", 1)
        self.s_done = s("s_done", 16)
        self.sb_done = s("sb_done", 16)
        self.mx_done = s("mx_done", 16)
        self.e_done = s("e_done", 16)
        self.r_done = s("r_done", 16)
        self.pn_done = s("pn_done", 16)
        self.t_done = s("t_done", 16)
        self.pt_ev = s("pt_ev", 16)
        self.o_done = s("o_done", 4)
        self.o_ev = s("o_ev", 4)
        self.y_done = s("y_done", 1)
        self.z_ready = s("z_ready", 1)
        t = c.take
        self.XB, self.KT, self.QB = t(0, 256), t(256, 256), t(512, 256)
        self.QZ = t(768, 16, 256)
        self.V = t(4864, 3, 512)
        self.bias = t(6400, 16, 384)
        self.Sb = t(12544, 2, 384)
        self.Pr = t(13312, 4, 384)
        self.OT = t(14848, 4, 256)
        self.PT = spare[:, 0:8 * 288].rearrange("p (a b) -> p a b", a=8)
        self.nm, self.ss, self.ri = c.small[:, 0:48], c.small[:, 48:96], c.small[:, 96:144]
        self.nm, self.ss, self.ri = (a.rearrange("p (h w) -> p h w", w=3) for a in (self.nm, self.ss, self.ri))

    def tensor(self, pe):
        c, PS = self.c, self.c.PS

        def keys_values(it, d):
            pe.wait_ge(self.qb_ready.sem, self.qb_ready.at(it, 1, d))
            pe.matmul(PS[:, 5, 256:512], self.wk, self.XB, start=True, stop=True, skip_group_check=True)\
                .then_inc(self.kp_done.sem, 1)
            for w, (q0, k0) in enumerate(WINDOWS):
                ins = pe.matmul(PS[:, 4, w * P:(w + 1) * P], self.XB[:, k0:k0 + P], self.wv, start=True, stop=True,
                                skip_group_check=True)
            ins.then_inc(self.vp_done.sem, 1)

        def queries(it, d):
            pe.wait_ge(self.src_ready.sem, self.src_ready.at(it, 1, d))
            pe.matmul(PS[:, 5, 0:256], self.wq, self.XB, start=True, stop=True, skip_group_check=True)\
                .then_inc(self.qp_done.sem, 1)

        def scores(it, h):
            if h == 0:
                pe.wait_ge(self.k_ev.sem, self.k_ev.at(it, 1))
            if h % 2 == 0:
                pe.wait_ge(self.q_ev.sem, self.q_ev.at(it, h // 2 + 1))
            for w, (q0, k0) in enumerate(WINDOWS):
                ins = pe.matmul(PS[0:WIN_Q, h % 2, w * P:(w + 1) * P], self.QZ[:, h, q0:q0 + WIN_Q],
                                self.KT[:, k0:k0 + P], start=True, stop=True)
            ins.then_inc(self.s_done.sem, 1)

        def transposes(it, h):
            pe.wait_ge(self.pn_done.sem, self.pn_done.at(it, h + 1))
            for w in range(3):
                ins = pe.transpose(PS[:, 2 + h % 2, w * WIN_Q:(w + 1) * WIN_Q],
                                   self.Pr[0:WIN_Q, h % 4, w * P:(w + 1) * P], c.ident[0:WIN_Q, 0:WIN_Q])
            ins.then_inc(self.t_done.sem, 1)

        def values(it, k):
            pe.wait_ge(self.pt_ev.sem, self.pt_ev.at(it, 4 * k + 4))
            for w in (2, 1, 0):
                q0 = WINDOWS[w][0]
                for r in range(4):
                    h = (4 * k + r) % self.H
                    ins = pe.matmul(PS[32 * r:32 * r + 32, 6 + k % 2, q0:q0 + WIN_Q],
                                    self.V[:, w, 32 * h:32 * h + 32], self.PT[:, h % 8, w * WIN_Q:(w + 1) * WIN_Q],
                                    start=True, stop=True, skip_group_check=True)
            ins.then_inc(self.o_done.sem, 1)

        def output(it):
            pe.wait_ge(self.o_ev.sem, self.o_ev.at(it, 0))
            for t in range(2):
                for k in range(4):
                    ins = pe.matmul(PS[:, 6, t * P:(t + 1) * P], self.OT[:, k, t * P:(t + 1) * P],
                                    self.wo[:, k, :], start=(k == 0), stop=(k == 3))
            ins.then_inc(self.y_done.sem, 1)

        def part(it, prev, cur, nxt):
            for s in range(16):
                if cur:
                    if prev or s >= 2:
                        pe.wait_ge(self.sb_done.sem, self.sb_done.at(it, s - 1))
                    scores(it, s)
                h = s - 3
                if (h < 0 and prev) or (h >= 0 and cur):
                    if prev or h >= 2:
                        pe.wait_ge(self.pt_ev.sem, self.pt_ev.at(it, h - 1))
                    transposes(it, h)
                k = self.chunk_after(s, 5)
                if k is not None and ((k < 0 and prev) or (k >= 0 and cur)):
                    if k == 0 and prev:
                        pe.wait_ge(self.z_ready.sem, self.z_ready.at(it, 0))
                    if k == 0:
                        pe.wait_ge(self.v_ev.sem, self.v_ev.at(it, 1))
                    if prev or k >= 2:
                        pe.wait_ge(self.o_ev.sem, self.o_ev.at(it, k - 1))
                    values(it, k)
                if prev and s == 6:
                    output(it)
                if not cur and s == 7:
                    self.end.transposes(pe, 0)
                if nxt and s == 3:
                    queries(it, 1)
                if nxt and s == 7:
                    pe.wait_ge(self.v_ev.sem, self.v_ev.at(it, 1))
                    keys_values(it, 1)

        queries(0, 0)
        keys_values(0, 0)
        self.parts(pe, part)

    def scalar(self, a):
        c, PS = self.c, self.c.PS
        a.wait_ge(self.x_ready.sem, self.x_ready.at(0, 2))

        def source(it, d):
            a.activation(self.XB, c.XT[:, bass.ds(it * S + d * S, S)], ACT.Copy).then_inc(self.src_ready.sem, 1)

        def keys(it, d):
            a.wait_ge(self.kp_done.sem, self.kp_done.at(it, 1, d))
            a.activation(self.KT, PS[:, 5, 256:512], ACT.Copy).then_inc(self.k_ev.sem, 1)

        def exps(it, h):
            a.wait_ge(self.mx_done.sem, self.mx_done.at(it, h + 1))
            for w in range(3):
                s = slice(w * P, (w + 1) * P)
                ins = a.activation(self.Pr[0:WIN_Q, h % 4, s], self.Sb[0:WIN_Q, h % 2, s], ACT.Exp,
                                   bias=self.nm[0:WIN_Q, h, w:w + 1], scale=1.0,
                                   accum_out=self.ss[0:WIN_Q, h, w:w + 1])
            ins.then_inc(self.e_done.sem, 1)

        def part(it, prev, cur, nxt):
            for s in range(16):
                if cur:
                    if prev or s >= 4:
                        a.wait_ge(self.t_done.sem, self.t_done.at(it, s - 3))
                    exps(it, s)
                h = s - 3
                if (h < 0 and prev) or (h >= 0 and cur):
                    a.wait_ge(self.t_done.sem, self.t_done.at(it, h + 1))
                    if prev or h >= 8:
                        a.wait_ge(self.o_done.sem, self.o_done.at(it, (h - 8) // 4 + 1))
                    a.activation(self.PT[:, h % 8, :], PS[:, 2 + h % 2, 0:288], ACT.Copy).then_inc(self.pt_ev.sem, 1)
                if not cur and s == 2:
                    self.end.root(a, 0)
                if nxt and s == 1:
                    source(it, 1)
                if nxt and s == 15:
                    keys(it, 1)

        source(0, 0)
        keys(0, 0)
        self.parts(a, part)

    def vector(self, v):
        c, PS = self.c, self.c.PS
        c.dve.link(v, v.memset(self.V, 0.0))
        for h in range(self.H):
            ins = v.scalar_tensor_tensor(self.bias[0:WIN_Q, h, :], self.rel, self.slopes[0:WIN_Q, h:h + 1], self.band,
                                         ALU.mult, ALU.add)
            if h == 0:
                v.wait_ge(self.qp_done.sem, self.qp_done.at(0, 1))
                v.tensor_scalar(self.QB, PS[:, 5, 0:256], 8.0 ** -0.5, None, ALU.mult).then_inc(self.qb_ready.sem, 1)
        c.dve.link(v, ins)
        v.wait_ge(self.x_ready.sem, self.x_ready.at(0, 2))

        def queries(it, d):
            v.wait_ge(self.qp_done.sem, self.qp_done.at(it, 1, d))
            v.wait_ge(self.q_ev.sem, self.q_ev.at(it, 8))
            v.tensor_scalar(self.QB, PS[:, 5, 0:256], 8.0 ** -0.5, None, ALU.mult).then_inc(self.qb_ready.sem, 1)

        def values_of(it):
            v.wait_ge(self.vp_done.sem, self.vp_done.at(it, 1))
            for w in range(3):
                dst = self.V[:, w, :].rearrange("p (h e) -> p h e", e=32)[:, :, 0:8]
                ins = v.tensor_copy(dst, PS[:, 4, w * P:(w + 1) * P].rearrange("p (h e) -> p h e", e=8))
            ins.then_inc(self.v_ev.sem, 1)

        def maxima(it, h):
            v.wait_ge(self.s_done.sem, self.s_done.at(it, h + 1))
            v.tensor_tensor(self.Sb[0:WIN_Q, h % 2, :], PS[0:WIN_Q, h % 2, 0:384], self.bias[0:WIN_Q, h, :],
                            ALU.add).then_inc(self.sb_done.sem, 1)
            v.wait_ge(self.sb_done.sem, self.sb_done.at(it, h + 1))
            v.tensor_reduce(self.nm[0:WIN_Q, h, :], self.Sb[0:WIN_Q, h % 2, :].rearrange("p (w k) -> p w k", w=3),
                            AX.X, ALU.max, negate=True).then_inc(self.mx_done.sem, 1)

        def part(it, prev, cur, nxt):
            for s in range(16):
                if cur:
                    if prev or s >= 2:
                        v.wait_ge(self.e_done.sem, self.e_done.at(it, s - 1))
                    maxima(it, s)
                h = s - 1
                if (h < 0 and prev) or (h >= 0 and cur):
                    v.wait_ge(self.e_done.sem, self.e_done.at(it, h + 1))
                    h %= 16
                    v.reciprocal(self.ri[0:WIN_Q, h, :], self.ss[0:WIN_Q, h, :]).then_inc(self.r_done.sem, 1)
                k = self.chunk_after(s, 6)
                if k is not None and ((k < 0 and prev) or (k >= 0 and cur)):
                    v.wait_ge(self.o_done.sem, self.o_done.at(it, k + 1))
                    if k == 0 and prev:
                        v.wait_ge(self.y_done.sem, self.y_done.at(it, 0))
                    v.tensor_copy(self.OT[:, k % 4, :], PS[:, 6 + k % 2, 0:256]).then_inc(self.o_ev.sem, 1)
                if cur and not nxt and s == 12:
                    self.end.early_stats(v)
                if not cur and s == 6:
                    self.end.tiles(v, 0)
                if cur and s == 5:
                    if prev:
                        v.wait_ge(self.o_done.sem, self.o_done.at(it, 0))
                    values_of(it)
                if prev and s == 7:
                    v.wait_ge(self.y_done.sem, self.y_done.at(it, 0))
                    v.tensor_tensor(c.Z[:, bass.ds(it * 2 - 2, 2), :], two(PS[:, 6, 0:256]),
                                    c.X[:, bass.ds(it * 2 - 2, 2), :], ALU.add).then_inc(self.z_ready.sem, 1)
                if nxt and s == 4:
                    queries(it, 1)

        self.parts(v, part)
        v.wait_ge(self.z_ready.sem, self.z_ready.at(B - 1, 1))

    def gpsimd(self, g):
        def pair(h):
            g.tensor_tensor(self.QZ[:, h:h + 2, :], self.QB.unsqueeze(1).to_broadcast([P, 2, 256]),
                            self.headmask[:, h:h + 2].unsqueeze(2).to_broadcast([P, 2, 256]),
                            ALU.mult).then_inc(self.q_ev.sem, 1)

        def part(it, nxt):
            for h in range(self.H):
                g.wait_ge(self.r_done.sem, self.r_done.at(it, h + 1))
                p = self.Pr[0:WIN_Q, h % 4, :].rearrange("p (w k) -> p w k", w=3)
                g.tensor_tensor(p, p, self.ri[0:WIN_Q, h, :].unsqueeze(2).to_broadcast([WIN_Q, 3, P]), ALU.mult)\
                    .then_inc(self.pn_done.sem, 1)
                if nxt and h == 5:
                    g.wait_ge(self.qb_ready.sem, self.qb_ready.at(it, 1, 1))
                if nxt and h >= 5:
                    for p in range(8):
                        if h == max(5 + p, 2 * p + 1):
                            pair(2 * p)

        g.wait_ge(self.qb_ready.sem, self.qb_ready.at(0, 1))
        for h in range(0, self.H, 2):
            pair(h)
        with g.Fori(0, B - 1) as it:
            part(it, True)
        part(B - 1, False)


class FourTokenAttention:

    def __init__(self, c, win, bin_, relk, wout, bout):
        self.c, self.win, self.bin, self.relk, self.wout, self.bout = c, win, bin_, relk, wout, bout
        self.x_ready = c.x_ready
        s = c.sig
        self.p_done = s("p_done", T, 1)
        self.p_ev = s("p_ev", T, 1)
        self.kk_ready = s("kk_ready", 8, 1)
        self.kk_used = s("kk_used", 8, 1)
        self.sh_ready = s("sh_ready", 1, 1)
        self.e_ready = s("e_ready", 1, 1)
        self.ao_ready = s("ao_ready", T, 1)
        self.at_done = s("at_done", 2, 1)
        self.at_ev = s("at_ev", 2, 1)
        self.y_done = s("y_done", 2, 1)
        self.z_ready = s("z_ready", 1, 1)
        t = c.take
        self.QKV = t(0, T, 384)
        self.KK = t(3072, 2, 512)
        self.PD = t(4096, 2, 512)
        self.sc = t(5120, T, 64)
        self.mx = t(5632, T, 16)
        self.AO = t(5760, T, 128)
        self.AT = t(6784, 1024)
        self.order = [(tq, u) for tq in range(4) for u in range(2)]

    def tensor(self, pe):
        c, PS = self.c, self.c.PS
        pe.wait_ge(self.x_ready.sem, self.x_ready.at(0, 2))
        for n in range(T):
            if n >= 4:
                pe.wait_ge(self.p_ev.sem, self.p_ev.at(0, n - 3))
            pe.matmul(PS[:, 2 + n % 4, 0:384], c.XT[:, n * P:(n + 1) * P], self.win, start=True, stop=True)\
                .then_inc(self.p_done.sem, 1)
        for n in range(T):
            pe.wait_ge(self.ao_ready.sem, self.ao_ready.at(0, n + 1))
            ins = pe.transpose(PS[:, n // 4, (n % 4) * P:(n % 4) * P + P], self.AO[:, n, :], c.ident)
            if n % 4 == 3:
                ins.then_inc(self.at_done.sem, 1)
        for n in range(T):
            if n % 4 == 0:
                pe.wait_ge(self.at_ev.sem, self.at_ev.at(0, n // 4 + 1))
            ins = pe.matmul(PS[:, 6 + n // 4, (n % 4) * P:(n % 4) * P + P], self.AT[:, n * P:(n + 1) * P], self.wout,
                            start=True, stop=True)
            if n % 4 == 3:
                ins.then_inc(self.y_done.sem, 1)

    def scalar(self, a):
        c, PS = self.c, self.c.PS
        a.wait_ge(self.sh_ready.sem, self.sh_ready.at(0, 1))
        a.activation(self.sc, self.sc, ACT.Exp).then_inc(self.e_ready.sem, 1)
        for i in range(2):
            a.wait_ge(self.at_done.sem, self.at_done.at(0, i + 1))
            a.activation(self.AT[:, i * 512:(i + 1) * 512], PS[:, i, :], ACT.Copy).then_inc(self.at_ev.sem, 1)

    def gpsimd(self, g):
        g.wait_ge(self.p_ev.sem, self.p_ev.at(0, T))
        for i, (tq, u) in enumerate(self.order):
            if i >= 2:
                g.wait_ge(self.kk_used.sem, self.kk_used.at(0, i - 1))
            g.tensor_tensor(self.KK[:, i % 2, :].rearrange("p (s f) -> p s f", s=4), self.QKV[:, u:T:2, 128:256],
                            self.relk[:, 3 - tq:7 - tq, :], ALU.add).then_inc(self.kk_ready.sem, 1)

    def vector(self, v):
        c, PS = self.c, self.c.PS

        def link(ins):
            c.dve.link(v, ins)

        for n in range(T):
            v.wait_ge(self.p_done.sem, self.p_done.at(0, n + 1))
            v.tensor_tensor(self.QKV[:, n, :], PS[:, 2 + n % 4, 0:384], self.bin, ALU.add).then_inc(self.p_ev.sem, 1)
        v.wait_ge(self.p_ev.sem, self.p_ev.at(0, T))
        link(v.tensor_scalar(self.QKV[:, :, 0:128], self.QKV[:, :, 0:128], 8.0 ** -0.5, None, ALU.mult))
        for i, (tq, u) in enumerate(self.order):
            n = 2 * tq + u
            v.wait_ge(self.kk_ready.sem, self.kk_ready.at(0, i + 1))
            q = self.QKV[:, n, 0:128].unsqueeze(1).to_broadcast([P, 4, P])
            pd = self.PD[:, i % 2, :]
            v.tensor_tensor(pd.rearrange("p (s f) -> p s f", s=4), self.KK[:, i % 2, :].rearrange("p (s f) -> p s f", s=4),
                            q, ALU.mult).then_inc(self.kk_used.sem, 1)
            v.wait_ge(self.kk_used.sem, self.kk_used.at(0, i + 1))
            ins = v.tensor_reduce(self.sc[:, n, :], pd.rearrange("p (g d) -> p g d", d=8), AX.X, ALU.add)
            if i % 2:
                link(ins)
        by_head = self.sc.rearrange("p n (s h) -> p n h s", s=4)
        by_key = self.sc.rearrange("p n (s h) -> p n s h", s=4)
        link(v.tensor_reduce(self.mx, by_head, AX.X, ALU.max))
        for n in range(T):
            ins = v.tensor_tensor(by_key[:, n], by_key[:, n], self.mx[:, n, :].unsqueeze(1).to_broadcast([P, 4, 16]),
                                  ALU.subtract)
        ins.then_inc(self.sh_ready.sem, 1)
        v.wait_ge(self.e_ready.sem, self.e_ready.at(0, 1))
        link(v.tensor_reduce(self.mx, by_head, AX.X, ALU.add))
        link(v.reciprocal(self.mx, self.mx))
        for n in range(T):
            ins = v.tensor_tensor(by_key[:, n], by_key[:, n], self.mx[:, n, :].unsqueeze(1).to_broadcast([P, 4, 16]),
                                  ALU.mult)
        link(ins)
        for n in range(T):
            pd = self.PD[:, n % 2, :].rearrange("p (s h d) -> p s h d", s=4, h=16)
            for s in range(4):
                val = self.QKV[:, 2 * s + n % 2, 256:384].rearrange("p (h d) -> p h d", d=8)
                p = by_key[:, n, s, :].unsqueeze(2).to_broadcast([P, 16, 8])
                ins = v.tensor_tensor(pd[:, s], val, p, ALU.mult)
            link(ins)
            v.tensor_reduce(self.AO[:, n, :], self.PD[:, n % 2, :].rearrange("p (s f) -> p f s", s=4), AX.X, ALU.add)\
                .then_inc(self.ao_ready.sem, 1)
            if n >= 1:
                v.wait_ge(self.ao_ready.sem, self.ao_ready.at(0, n))
        for i in range(2):
            v.wait_ge(self.y_done.sem, self.y_done.at(0, i + 1))
            z = c.Z[:, 4 * i:4 * i + 4, :]
            y = PS[:, 6 + i, :].rearrange("p (t f) -> p t f", t=4)
            link(v.tensor_tensor(z, y, c.X[:, 4 * i:4 * i + 4, :], ALU.add))
            ins = v.tensor_tensor(z, z, self.bout.unsqueeze(1).to_broadcast([P, 4, P]), ALU.add)
        ins.then_inc(self.z_ready.sem, 1)
        v.wait_ge(self.z_ready.sem, self.z_ready.at(0, 1))


class Mamba:

    N = 16

    def __init__(self, c, g, b, win, cw, cb, wdt_in, wbc, wdt, bdt, alog, Dv, wout, onehot):
        self.c, self.g, self.b, self.win, self.cw, self.cb = c, g, b, win, cw, cb
        self.wdt_in, self.wbc, self.wdt, self.bdt, self.alog, self.Dv = wdt_in, wbc, wdt, bdt, alog, Dv
        self.wout, self.onehot = wout, onehot
        self.x_ready = c.x_ready
        s = c.sig
        N = self.N
        self.var_ready, self.sd_ready = s("var_ready", 1, 1), s("sd_ready", 1, 1)
        self.xn_ready = s("xn_ready", T, 1)
        self.xn_done = s("xn_done", 2, 1)
        self.xn_ev = s("xn_ev", 2, 1)
        self.a_ready = s("a_ready", 1, 1)
        self.uz_done = s("uz_done", 4)
        self.u_ev = s("u_ev", 2)
        self.z_ev = s("z_ev", 1)
        self.uc_ready = s("uc_ready", 2)
        self.us_ready = s("us_ready", 2)
        self.dbc_done = s("dbc_done", 2)
        self.dti_ev = s("dti_ev", 1)
        self.bc_ready = s("bc_ready", 1)
        self.dt_done = s("dt_done", 2)
        self.dtx_ready = s("dtx_ready", 2)
        self.sp_ready = s("sp_ready", 1)
        self.dt_ready = s("dt_ready", 1)
        self.dtu_ready = s("dtu_ready", 1)
        self.da_ready = s("da_ready", N)
        self.bs_ready = s("bs_ready", N)
        self.b_done = s("b_done", N)
        self.c_done = s("c_done", N)
        self.db_ready = s("db_ready", N)
        self.sc_ready = s("sc_ready", N)
        self.hc_ready = s("hc_ready", N)
        self.acc_ready = s("acc_ready", N)
        self.yg_ready = s("yg_ready", 1)
        self.y_done = s("y_done", 1)
        self.z_ready = s("z_ready", 1)
        t = c.take
        self.XN = t(0, T, P)
        self.XNT = t(1024, 1024)
        self.A = t(2048, 32)
        self.up = t(2080, 2, 259)
        self.uc = t(2600, 2, 256)
        self.u = t(3112, 2, 256)
        self.sz = t(3624, 2, 256)
        self.dti = t(4136, 256)
        self.r = t(4392, 256)
        self.BC = t(4648, 128).bitcast(BF16)
        self.dx = t(4776, 2, 256)
        self.ab = t(5288, 2, 256)
        self.dt = t(5800, 2, 256)
        self.dtu = t(6312, 2, 256)
        self.dA = t(6824, 3, 512)
        self.dB = t(8360, 3, 512)
        self.h = t(9896, 2, 512)
        self.hC = t(10920, 3, 512)
        self.bs = t(14504, 3, 256)
        self.y = t(12456, 2, 256)
        self.yD = t(12968, 2, 256)
        self.e1 = t(13480, 2, 256)
        self.lw = t(13992, 2, 256)

    def tensor(self, pe):
        c, PS = self.c, self.c.PS
        pe.wait_ge(self.x_ready.sem, self.x_ready.at(0, 2))
        for n in range(T):
            pe.wait_ge(self.xn_ready.sem, self.xn_ready.at(0, n + 1))
            ins = pe.transpose(PS[:, n // 4, (n % 4) * P:(n % 4) * P + P], self.XN[:, n, :], c.ident)
            if n % 4 == 3:
                ins.then_inc(self.xn_done.sem, 1)
        pe.wait_ge(self.xn_ev.sem, self.xn_ev.at(0, 2))
        with pe.Fori(0, B) as it:
            x = self.XNT[:, bass.ds(it * S, S)]
            for j in range(4):
                if j == 3:
                    pe.wait_ge(self.u_ev.sem, self.u_ev.at(it, 1))
                dst = PS[:, min(j, 2), (256 if j == 3 else 0):(512 if j == 3 else 256)]
                pe.matmul(dst, self.win[:, j * P:(j + 1) * P], x, start=True, stop=True, skip_group_check=True)\
                    .then_inc(self.uz_done.sem, 1)
            for j in range(2):
                pe.wait_ge(self.us_ready.sem, self.us_ready.at(it, j + 1))
                ins = pe.matmul(PS[0:8, 3, 0:256], self.wdt_in[:, j, :], self.u[:, j, :], start=(j == 0), stop=(j == 1))
            ins.then_inc(self.dbc_done.sem, 1)
            pe.wait_ge(self.dti_ev.sem, self.dti_ev.at(it, 1))
            for j in range(2):
                pe.matmul(PS[:, j, 0:256], self.wdt[0:8, j * P:(j + 1) * P], self.dti[0:8, :], start=True, stop=True)\
                    .then_inc(self.dt_done.sem, 1)
            for j in range(2):
                ins = pe.matmul(PS[0:96, 4, 0:256], self.wbc[:, j, :], self.u[:, j, :], start=(j == 0), stop=(j == 1))
            ins.then_inc(self.dbc_done.sem, 1)
            pe.wait_ge(self.bc_ready.sem, self.bc_ready.at(it, 1))
            acc = PS[:, 0, :]

            def add(n):
                pe.wait_ge(self.hc_ready.sem, self.hc_ready.at(it, n + 1))
                pe.matmul(acc, c.ident, self.hC[:, n % 3, :], start=(n == 0), stop=(n == self.N - 1))\
                    .then_inc(self.acc_ready.sem, 1)

            def spread_b(n):
                if n >= 2:
                    pe.wait_ge(self.bs_ready.sem, self.bs_ready.at(it, n - 1))
                pe.matmul(PS[:, 4 + n % 2, 0:256], self.onehot[0:96, n:n + 1].to_broadcast([96, P]),
                          self.BC[0:96, :], start=True, stop=True).then_inc(self.b_done.sem, 1)

            def spread_c(n):
                if n >= 2:
                    pe.wait_ge(self.hc_ready.sem, self.hc_ready.at(it, n - 1))
                pe.matmul(PS[:, 6 + n % 2, 0:256], self.onehot[0:96, 16 + n:17 + n].to_broadcast([96, P]),
                          self.BC[0:96, :], start=True, stop=True).then_inc(self.c_done.sem, 1)

            for n in range(-2, self.N + 2):
                if n + 2 < self.N:
                    spread_b(n + 2)
                if 0 <= n < self.N:
                    spread_c(n)
                if n >= 2:
                    add(n - 2)
            pe.wait_ge(self.yg_ready.sem, self.yg_ready.at(it, 1))
            for t in range(2):
                for j in range(2):
                    ins = pe.matmul(PS[:, 3, t * P:(t + 1) * P], self.y[:, j, t * P:(t + 1) * P], self.wout[:, j, :],
                                    start=(j == 0), stop=(j == 1))
            ins.then_inc(self.y_done.sem, 1)

    def scalar(self, a):
        c, PS = self.c, self.c.PS

        def link(ins):
            c.act.link(a, ins)

        a.activation(self.A, self.alog, ACT.Exp).then_inc(self.a_ready.sem, 1)
        a.wait_ge(self.var_ready.sem, self.var_ready.at(0, 1))
        a.activation(c.sd[:, :], c.mv[:, :, 1], ACT.Sqrt, bias=c.eps, scale=1.0).then_inc(self.sd_ready.sem, 1)
        for i in range(2):
            a.wait_ge(self.xn_done.sem, self.xn_done.at(0, i + 1))
            a.activation(self.XNT[:, i * 512:(i + 1) * 512], PS[:, i, :], ACT.Identity, bias=self.b, scale=self.g)\
                .then_inc(self.xn_ev.sem, 1)
        with a.Fori(0, B) as it:
            c.act.enter(it)
            for j in range(2):
                a.wait_ge(self.uz_done.sem, self.uz_done.at(it, j + 1))
                a.activation(self.up[:, j, 3:259], PS[:, j, 0:256], ACT.Copy).then_inc(self.u_ev.sem, 1)
            a.wait_ge(self.uz_done.sem, self.uz_done.at(it, 4))
            a.activation(self.sz, two(PS[:, 2, :]), ACT.Silu).then_inc(self.z_ev.sem, 1)
            for j in range(2):
                a.wait_ge(self.uc_ready.sem, self.uc_ready.at(it, j + 1))
                a.activation(self.u[:, j, :], self.uc[:, j, :], ACT.Silu).then_inc(self.us_ready.sem, 1)
            a.wait_ge(self.dbc_done.sem, self.dbc_done.at(it, 1))
            a.activation(self.dti[0:8, :], PS[0:8, 3, 0:256], ACT.Copy).then_inc(self.dti_ev.sem, 1)
            a.wait_ge(self.dtx_ready.sem, self.dtx_ready.at(it, 2))
            link(a.activation(self.ab, self.dx, ACT.Abs))
            link(a.activation(self.ab, self.ab, ACT.Exp, scale=-1.0))
            link(a.activation(self.e1, self.ab, ACT.Identity, bias=self.c.one, scale=1.0))
            a.activation(self.lw, self.e1, ACT.Ln).then_inc(self.sp_ready.sem, 1)
            a.wait_ge(self.dt_ready.sem, self.dt_ready.at(it, 1))

            def b_copy(n):
                a.wait_ge(self.b_done.sem, self.b_done.at(it, n + 1))
                if n >= 3:
                    a.wait_ge(self.db_ready.sem, self.db_ready.at(it, n - 2))
                a.activation(self.bs[:, n % 3, :], PS[:, 4 + n % 2, 0:256], ACT.Copy).then_inc(self.bs_ready.sem, 1)

            def decays(n):
                if n >= 3:
                    a.wait_ge(self.sc_ready.sem, self.sc_ready.at(it, n - 2))
                d = two(self.dA[:, n % 3, :])
                for j in range(2):
                    ins = a.activation(d[:, j, 1:256], self.dt[:, j, 1:256], ACT.Exp,
                                       scale=self.A[:, j * 16 + n:j * 16 + n + 1])
                ins.then_inc(self.da_ready.sem, 1)

            for n in range(-1, self.N):
                if n + 1 < self.N:
                    b_copy(n + 1)
                if n >= 0:
                    decays(n)
        c.act.leave(B)

    def vector(self, v):
        c, PS = self.c, self.c.PS

        def link(ins):
            c.dve.link(v, ins)

        v.memset(self.dA, 0.0)
        link(v.memset(self.up, 0.0))
        v.wait_ge(self.a_ready.sem, self.a_ready.at(0, 1))
        link(v.tensor_scalar(self.A, self.A, -1.0, None, ALU.mult))
        for n in range(T):
            ins = v.bn_stats(c.bn[:, n, :], c.X[:, n, :])
        link(ins)
        for n in range(T):
            ins = v.bn_aggr(c.mv[:, n, :], c.bn[:, n, :])
        ins.then_inc(self.var_ready.sem, 1)
        v.wait_ge(self.sd_ready.sem, self.sd_ready.at(0, 1))
        link(v.reciprocal(c.rs[:, :], c.sd[:, :]))
        refine(link, v, c.rs[:, :], c.mv[:, :, 1], EPS, c.rt[:, :])
        for n in range(T):
            v.tensor_scalar(self.XN[:, n, :], c.X[:, n, :], c.mv[:, n, 0:1], c.rs[:, n:n + 1],
                            ALU.subtract, ALU.mult).then_inc(self.xn_ready.sem, 1)
        with v.Fori(0, B) as it:
            c.dve.enter(it)
            for j in range(2):
                v.wait_ge(self.u_ev.sem, self.u_ev.at(it, j + 1))
                up, uc = self.up[:, j, :], self.uc[:, j, :]
                link(v.tensor_scalar(uc, up[:, 0:256], self.cw[:, j, 0:1], self.cb[:, j:j + 1], ALU.mult, ALU.add))
                for k in range(1, 4):
                    ins = v.scalar_tensor_tensor(uc, up[:, k:k + 256], self.cw[:, j, k:k + 1], uc, ALU.mult, ALU.add)
                    if k < 3:
                        link(ins)
                ins.then_inc(self.uc_ready.sem, 1)
            for j in range(2):
                v.wait_ge(self.dt_done.sem, self.dt_done.at(it, j + 1))
                v.tensor_scalar(self.dx[:, j, :], PS[:, j, 0:256], self.bdt[:, j:j + 1], None, ALU.add)\
                    .then_inc(self.dtx_ready.sem, 1)
            v.wait_ge(self.dbc_done.sem, self.dbc_done.at(it, 2))
            bc = PS[:, 4, 0:256]
            link(v.tensor_copy(self.BC[0:96, :], bc[0:96]))
            for k in (1, 2):
                s = slice(32 * k, 32 * k + 32)
                link(v.tensor_tensor(self.r[s, :], bc[s], self.BC[s, :], ALU.subtract))
                link(v.tensor_copy(self.BC[s, :], self.r[s, :]))
            s = slice(64, 96)
            link(v.tensor_tensor(self.r[s, :], self.r[s, :], self.BC[s, :], ALU.subtract))
            v.tensor_copy(self.BC[s, :], self.r[s, :]).then_inc(self.bc_ready.sem, 1)
            v.wait_ge(self.sp_ready.sem, self.sp_ready.at(it, 1))
            link(v.tensor_scalar(self.e1, self.e1, 1.0, None, ALU.subtract))
            link(v.tensor_tensor(self.e1, self.ab, self.e1, ALU.subtract))
            link(v.tensor_tensor(self.e1, self.lw, self.e1, ALU.add))
            v.scalar_tensor_tensor(self.dt, self.dx, 0.0, self.e1, ALU.max, ALU.add).then_inc(self.dt_ready.sem, 1)
            v.wait_ge(self.dt_ready.sem, self.dt_ready.at(it, 1))
            v.tensor_tensor(self.dtu, self.dt, self.u, ALU.mult)
            for j in range(2):
                ins = v.tensor_scalar(self.yD[:, j, :], self.u[:, j, :], self.Dv[:, j:j + 1], None, ALU.mult)
            ins.then_inc(self.dtu_ready.sem, 1)

            def scan(n):
                v.wait_ge(self.da_ready.sem, self.da_ready.at(it, n + 1))
                v.wait_ge(self.db_ready.sem, self.db_ready.at(it, n + 1))
                if n >= 2:
                    v.wait_ge(self.hc_ready.sem, self.hc_ready.at(it, n - 1))
                v.tensor_tensor_scan(self.h[:, n % 2, :], self.dA[:, n % 3, :], self.dB[:, n % 3, :], 0.0,
                                     ALU.mult, ALU.add).then_inc(self.sc_ready.sem, 1)

            def outputs(n):
                v.wait_ge(self.sc_ready.sem, self.sc_ready.at(it, n + 1))
                v.wait_ge(self.c_done.sem, self.c_done.at(it, n + 1))
                if n >= 3:
                    v.wait_ge(self.acc_ready.sem, self.acc_ready.at(it, n - 2))
                cc = PS[:, 6 + n % 2, 0:256].unsqueeze(1).to_broadcast([P, 2, 256])
                v.tensor_tensor(two(self.hC[:, n % 3, :]), two(self.h[:, n % 2, :]), cc, ALU.mult)\
                    .then_inc(self.hc_ready.sem, 1)

            for n in range(self.N + 1):
                if n < self.N:
                    scan(n)
                if n >= 1:
                    outputs(n - 1)
            v.wait_ge(self.acc_ready.sem, self.acc_ready.at(it, self.N))
            v.wait_ge(self.z_ev.sem, self.z_ev.at(it, 1))
            link(v.tensor_tensor(self.y, two(PS[:, 0, :]), self.yD, ALU.add))
            v.tensor_tensor(self.y, self.y, self.sz, ALU.mult).then_inc(self.yg_ready.sem, 1)
            v.wait_ge(self.y_done.sem, self.y_done.at(it, 1))
            z, x = c.Z[:, bass.ds(it * 2, 2), :], c.X[:, bass.ds(it * 2, 2), :]
            link(v.tensor_tensor(z, two(PS[:, 3, 0:256]), x, ALU.add))
            v.tensor_tensor(z, z, x, ALU.add).then_inc(self.z_ready.sem, 1)
        c.dve.leave(B)
        v.wait_ge(self.z_ready.sem, self.z_ready.at(B - 1, 1))

    def gpsimd(self, g):
        with g.Fori(0, B) as it:
            g.wait_ge(self.dtu_ready.sem, self.dtu_ready.at(it, 1))
            for n in range(self.N):
                g.wait_ge(self.bs_ready.sem, self.bs_ready.at(it, n + 1))
                if n >= 3:
                    g.wait_ge(self.sc_ready.sem, self.sc_ready.at(it, n - 2))
                b = self.bs[:, n % 3, :].unsqueeze(1).to_broadcast([P, 2, 256])
                g.tensor_tensor(two(self.dB[:, n % 3, :]), self.dtu, b, ALU.mult).then_inc(self.db_ready.sem, 1)


def rotary_tables():
    f = np.float32
    half = np.arange(0, 64, 2, dtype=f)
    inv = (f(1.0) / f(10000.0) ** (half / f(64))).astype(f)
    t = np.arange(S, dtype=f)
    fr = t[:, None] * inv[None, :]
    fr = np.concatenate([fr, fr], -1).astype(f)
    base = ((half + f(0.4 * 64)) / f(1.4 * 64)).astype(f)
    power = ((t - S // 2) / f(32.0)).astype(f)
    scale = (base[None, :] ** power[:, None]).astype(f)
    scale = np.concatenate([scale, scale], -1)
    cos, sin = np.cos(fr).astype(f), np.sin(fr).astype(f)
    sin[:, 0:32] *= -1
    return np.stack([cos * scale * 8, sin * scale * 8, cos / scale, sin / scale], 1).astype(f)


def local_masks():
    i, j = np.arange(64)[:, None], np.arange(P)[None, :]
    first = np.where(j <= i, 0.0, NEG)
    later = np.where((j <= i + 64) & (j >= i), 0.0, NEG)
    m = np.stack([first, later, later, later], 1)
    return np.concatenate([m, m], 0).astype(np.float32)


class LocalLayer:

    KEYS = (0, 0, 64, 128)
    HID = (P, P, 85)

    def __init__(self, c, depth, wqkv, qs, ks, wo, lg, lb, w1, b1, w2, w2r, b2, tables, maskb):
        self.c, self.depth = c, depth
        self.wqkv, self.qs, self.ks, self.wo, self.lg, self.lb = wqkv, qs, ks, wo, lg, lb
        self.w1, self.b1, self.w2, self.w2r, self.b2, self.tables, self.maskb = w1, b1, w2, w2r, b2, tables, maskb
        self.x_ready = c.x_ready
        s = c.sig
        self.h_ready = s("h_ready", 1)
        self.mask_ready = s("mask_ready", 1, 1)
        self.p_done = s("p_done", 7)
        self.sq_done = s("sq_done", 4)
        self.ab_done = s("ab_done", 4)
        self.qk_sum = s("qk_sum", 4)
        self.ssq_used = s("ssq_used", 4)
        self.sum_ready = s("sum_ready", 1)
        self.nrm_ready = s("nrm_ready", 1)
        self.inv_ready = s("inv_ready", 1)
        self.qk0_ready = s("qk0_ready", 2)
        self.qk1_ready = s("qk1_ready", 2)
        self.v_ev = s("v_ev", 3)
        self.tr_done = s("tr_done", 4)
        self.tr_ev = s("tr_ev", 4)
        self.s_done = s("s_done", 4)
        self.mx_done = s("mx_done", 4)
        self.e_done = s("e_done", 4)
        self.r_done = s("r_done", 4)
        self.pn_done = s("pn_done", 4)
        self.t_done = s("t_done", 4)
        self.pt_ev = s("pt_ev", 4)
        self.o_done = s("o_done", 4)
        self.o_ev = s("o_ev", 4)
        self.y_done = s("y_done", 1)
        self.x1_ready = s("x1_ready", 1)
        self.x1t_done = s("x1t_done", 1)
        self.h2_ready = s("h2_ready", 1)
        self.h2_done = s("h2_done", 1)
        self.var_ready = s("var_ready", 1)
        self.sd_ready = s("sd_ready", 1)
        self.n_ready = s("n_ready", 1)
        self.n_done = s("n_done", 1)
        self.n_ev = s("n_ev", 1)
        self.ag_done = s("ag_done", 6)
        self.g_ready = s("g_ready", 3)
        self.hid_ready = s("hid_ready", 3)
        self.f_done = s("f_done", 1)
        self.z_ready = s("z_ready" if depth else "x2_ready", 1)
        self.x2t_done = None if depth else s("x2t_done", 1)
        self.out_ready = None if depth else s("out_ready", 1)
        t = c.take
        self.XI, self.XIT = t(0, T, P), t(1024, 1024)
        self.Hs = t(2048, 256)
        self.tab = t(2304, 2, 256)
        self.SQ = t(2816, 512)
        self.ssq = t(3328, 4, 8)
        self.inv = t(3360, 4, 8)
        self.nrm = c.small[:, 96:128].rearrange("p (i h) -> p i h", h=8)
        self.nrt = c.small[:, 128:160].rearrange("p (i h) -> p i h", h=8)
        self.QA = t(3400, 4, 512)
        self.QB = t(5448, 2, 512)
        self.QZ = t(6472, 8, 256)
        self.KT = t(8520, 4, 256)
        self.V = t(9544, 3, 512)
        self.Pr = t(11080, 3, 512)
        self.PT = t(12616, 2, 512)
        self.OT = t(13640, 4, 256)
        self.X1 = t(14664, 2, 128)
        self.H2 = t(14920, 256)
        self.HN = t(15176, 2, 128)
        self.HNT = t(15432, 256)
        self.GE = t(15688, 2, 256)
        self.HD = t(16200, 3, 256)
        self.MBK = t(16968, 256).bitcast(BF16)
        self.nm, self.ss, self.ri = (c.small[:, 16 * i:16 * i + 16].rearrange("p (c w) -> p c w", w=4) for i in range(3))
        self.st, self.mv2, self.sd2, self.rs2 = c.small[:, 64:76], c.small[:, 80:84], c.small[:, 84:86], c.small[:, 86:88]

    def source(self, it, ahead=0):
        c = self.c
        if self.depth == 0:
            return c.X[:, bass.ds(it * 2 + 2 * ahead, 2), :], c.XT
        return self.XI[:, bass.ds(it * 2 + 2 * ahead, 2), :], self.XIT


    def tensor(self, pe):
        c, PS = self.c, self.c.PS
        pe.wait_ge(self.mask_ready.sem, self.mask_ready.at(0, 1))

        def project(it, d, i):
            if i == 0:
                pe.wait_ge(self.h_ready.sem, self.h_ready.at(it, 1, d))
            if i >= 2:
                pe.wait_ge(self.sq_done.sem, self.sq_done.at(it, i - 1, d))
            t, j = divmod(i, 2)
            pe.matmul(PS[:, j, :], self.Hs[:, t * P:(t + 1) * P], self.wqkv[:, j * 512:(j + 1) * 512],
                      start=True, stop=True).then_inc(self.p_done.sem, 1)

        def project_v(it, d, w):
            if w == 2:
                pe.wait_ge(self.v_ev.sem, self.v_ev.at(it, 1, d))
            k0 = 64 * w
            pe.matmul(PS[:, 2 + w % 2, :], self.Hs[:, k0:k0 + P], self.wqkv[:, 1024:1536], start=True, stop=True)\
                .then_inc(self.p_done.sem, 1)

        def turn(it, d, i):
            if i == 0:
                pe.wait_ge(self.v_ev.sem, self.v_ev.at(it, 3, d))
            if i >= 2:
                pe.wait_ge(self.tr_ev.sem, self.tr_ev.at(it, i - 1, d))
            ready = self.qk0_ready if i < 2 else self.qk1_ready
            pe.wait_ge(ready.sem, ready.at(it, i % 2 + 1, d))
            for k in range(4):
                ins = pe.transpose(PS[:, 3 - i % 2, k * P:(k + 1) * P], self.QA[:, i, k * P:(k + 1) * P], c.ident)
            ins.then_inc(self.tr_done.sem, 1)

        def scores(it, k):
            if k == 0:
                pe.wait_ge(self.tr_ev.sem, self.tr_ev.at(it, 4))
            if k >= 2:
                pe.wait_ge(self.e_done.sem, self.e_done.at(it, k - 1))
            pe.matmul(PS[:, k % 2, :], c.IDB[:, :], self.MBK, start=True, stop=False, skip_group_check=True)
            for w in range(4):
                for r in range(2):
                    ins = pe.matmul(PS[64 * r:64 * r + 64, k % 2, w * P:(w + 1) * P],
                                    self.QZ[:, 2 * k + r, w * 64:w * 64 + 64],
                                    self.KT[:, k, self.KEYS[w]:self.KEYS[w] + P],
                                    start=False, stop=True, skip_group_check=True)
            ins.then_inc(self.s_done.sem, 1)

        def transposes(it, k):
            pe.wait_ge(self.pn_done.sem, self.pn_done.at(it, k + 1))
            if k >= 2:
                pe.wait_ge(self.pt_ev.sem, self.pt_ev.at(it, k - 1))
            for w in range(4):
                ins = pe.transpose(PS[:, 2 + k % 2, w * P:(w + 1) * P], self.Pr[:, k % 3, w * P:(w + 1) * P], c.ident)
            ins.then_inc(self.t_done.sem, 1)

        def values(it, k):
            pe.wait_ge(self.pt_ev.sem, self.pt_ev.at(it, k + 1))
            if k == 1 and self.depth:
                pe.wait_ge(self.z_ready.sem, self.z_ready.at(it, 0))
            if k >= 2:
                pe.wait_ge(self.o_ev.sem, self.o_ev.at(it, k - 1))
            for w in range(4):
                ins = pe.matmul(PS[:, 4 + k % 2, w * P:(w + 1) * P], self.V[:, self.KEYS[w] // 64, k * P:(k + 1) * P],
                                self.PT[:, k % 2, w * P:(w + 1) * P], start=True, stop=True)
            ins.then_inc(self.o_done.sem, 1)

        def gate_up(it, f):
            m, at = self.HID[f], f * P
            if f == 2:
                pe.wait_ge(self.hid_ready.sem, self.hid_ready.at(it, 1))
            pe.matmul(PS[0:m, 4 + f % 2, 0:256], self.w1[:, at:at + m], self.HNT, start=True, stop=True)\
                .then_inc(self.ag_done.sem, 1)
            pe.matmul(PS[0:m, 6 + f % 2, 0:256], self.w1[:, 341 + at:341 + at + m], self.HNT, start=True, stop=True)\
                .then_inc(self.ag_done.sem, 1)

        def batch(it, more):
            scores(it, 0)
            scores(it, 1)
            for k in range(4):
                if k + 2 < 4:
                    scores(it, k + 2)
                transposes(it, k)
                if k >= 1:
                    values(it, k - 1)
            if more:
                project(it, 1, 0)
                project(it, 1, 1)
            values(it, 3)
            pe.wait_ge(self.o_ev.sem, self.o_ev.at(it, 4))
            for t in range(2):
                for k in range(4):
                    ins = pe.matmul(PS[:, 6, t * P:(t + 1) * P], self.OT[:, k, t * P:(t + 1) * P], self.wo[:, k, :],
                                    start=(k == 0), stop=(k == 3))
            ins.then_inc(self.y_done.sem, 1)
            if more:
                project_v(it, 1, 0)
                project_v(it, 1, 1)
            pe.wait_ge(self.x1_ready.sem, self.x1_ready.at(it, 1))
            for t in range(2):
                ins = pe.transpose(PS[:, 7, t * P:(t + 1) * P], self.X1[:, t, :], c.ident)
            ins.then_inc(self.x1t_done.sem, 1)
            if more:
                project(it, 1, 2)
            pe.wait_ge(self.h2_ready.sem, self.h2_ready.at(it, 1))
            for t in range(2):
                ins = pe.transpose(PS[:, 6, t * P:(t + 1) * P], self.H2[:, t * P:(t + 1) * P], c.ident)
            ins.then_inc(self.h2_done.sem, 1)
            if more:
                project(it, 1, 3)
                project_v(it, 1, 2)
            pe.wait_ge(self.n_ready.sem, self.n_ready.at(it, 1))
            for t in range(2):
                ins = pe.transpose(PS[:, 7, t * P:(t + 1) * P], self.HN[:, t, :], c.ident)
            ins.then_inc(self.n_done.sem, 1)
            pe.wait_ge(self.n_ev.sem, self.n_ev.at(it, 1))
            gate_up(it, 0)
            gate_up(it, 1)
            if more:
                turn(it, 1, 0)
                turn(it, 1, 1)
            gate_up(it, 2)
            if more:
                turn(it, 1, 2)
                turn(it, 1, 3)
            for f, m in enumerate(self.HID):
                pe.wait_ge(self.hid_ready.sem, self.hid_ready.at(it, max(2, f + 1)))
                w = self.w2[:, f, :] if f < 2 else self.w2r[0:m, :]
                for t in range(2):
                    ins = pe.matmul(PS[:, 5, t * P:(t + 1) * P], self.HD[0:m, f, t * P:(t + 1) * P], w,
                                    start=(f == 0 and t == 0), stop=(f == 2), skip_group_check=True)
            ins.then_inc(self.f_done.sem, 1)
            if self.depth == 0:
                pe.wait_ge(self.z_ready.sem, self.z_ready.at(it, 1))
                for t in range(2):
                    ins = pe.transpose(PS[:, 7, t * P:(t + 1) * P], self.HN[:, t, :], c.ident)
                ins.then_inc(self.x2t_done.sem, 1)

        for i in range(2):
            project(0, 0, i)
        for w in range(2):
            project_v(0, 0, w)
        for i in (2, 3):
            project(0, 0, i)
        project_v(0, 0, 2)
        for i in range(4):
            turn(0, 0, i)
        with pe.Fori(0, B - 1) as it:
            batch(it, True)
        batch(B - 1, False)

    def scalar(self, a):
        c, PS = self.c, self.c.PS
        a.wait_ge(self.x_ready.sem, self.x_ready.at(0, 2))
        if self.depth:
            a.wait_ge(self.prev_out.sem, self.prev_out.at(B - 1, 1))

        def shift(it, d):
            _, XT = self.source(it)
            a.activation(self.Hs[64:128, 1:256], XT[64:128, bass.ds(it * S + d * S, S - 1)], ACT.Copy)
            a.activation(self.Hs[0:64, :], XT[0:64, bass.ds(it * S + d * S, S)], ACT.Copy).then_inc(self.h_ready.sem, 1)

        def square(it, d, i):
            a.wait_ge(self.ab_done.sem, self.ab_done.at(it, i + 1, d))
            if i:
                a.wait_ge(self.ssq_used.sem, self.ssq_used.at(it, i, d))
            a.activation(self.SQ, PS[:, i % 2, :], ACT.Square).then_inc(self.sq_done.sem, 1)

        def value(it, d, w):
            a.wait_ge(self.p_done.sem, self.p_done.at(it, (3, 4, 7)[w], d))
            a.activation(self.V[:, w, :], PS[:, 2 + w % 2, :], ACT.Copy).then_inc(self.v_ev.sem, 1)

        def norms(it, d):
            a.wait_ge(self.sum_ready.sem, self.sum_ready.at(it, 1, d))
            a.activation(self.nrm, self.ssq, ACT.Sqrt).then_inc(self.nrm_ready.sem, 1)

        def exps(it, k):
            a.wait_ge(self.mx_done.sem, self.mx_done.at(it, k + 1))
            if k >= 3:
                a.wait_ge(self.t_done.sem, self.t_done.at(it, k - 2))
            for w in range(4):
                s = slice(w * P, (w + 1) * P)
                ins = a.activation(self.Pr[:, k % 3, s], PS[:, k % 2, s], ACT.Exp, bias=self.nm[:, k, w:w + 1],
                                   scale=1.0, accum_out=self.ss[:, k, w:w + 1])
            ins.then_inc(self.e_done.sem, 1)

        def out(it, k):
            a.wait_ge(self.o_done.sem, self.o_done.at(it, k + 1))
            for r in range(2):
                s = slice(64 * r, 64 * r + 64)
                src = PS[s, 4 + k % 2, :].rearrange("p (w q) -> p w q", w=4)[:, :, s]
                ins = a.activation(self.OT[s, k, :].rearrange("p (w q) -> p w q", w=4), src, ACT.Copy)
            ins.then_inc(self.o_ev.sem, 1)

        def batch(it, more):
            exps(it, 0)
            exps(it, 1)
            if more:
                shift(it, 1)
            exps(it, 2)
            exps(it, 3)
            for k in range(4):
                out(it, k)
            if more:
                square(it, 1, 0)
            a.wait_ge(self.x1t_done.sem, self.x1t_done.at(it, 1))
            a.activation(self.H2[64:128, 1:256], PS[64:128, 7, 0:255], ACT.Copy)
            a.activation(self.H2[0:64, :], PS[0:64, 7, 0:256], ACT.Copy).then_inc(self.h2_ready.sem, 1)
            if more:
                value(it, 1, 0)
                value(it, 1, 1)
                square(it, 1, 1)
            a.wait_ge(self.var_ready.sem, self.var_ready.at(it, 1))
            a.activation(self.sd2, self.mv2.rearrange("p (t k) -> p t k", k=2)[:, :, 1], ACT.Sqrt, bias=c.eps, scale=1.0)\
                .then_inc(self.sd_ready.sem, 1)
            if more:
                square(it, 1, 2)
                value(it, 1, 2)
            a.wait_ge(self.n_done.sem, self.n_done.at(it, 1))
            a.activation(self.HNT, PS[:, 7, 0:256], ACT.Identity, bias=self.lb, scale=self.lg).then_inc(self.n_ev.sem, 1)
            if more:
                square(it, 1, 3)
                norms(it, 1)
            for f, m in enumerate(self.HID):
                a.wait_ge(self.ag_done.sem, self.ag_done.at(it, 2 * f + 2))
                if f == 2:
                    a.wait_ge(self.hid_ready.sem, self.hid_ready.at(it, 1))
                a.activation(self.GE[0:m, f % 2, :], PS[0:m, 6 + f % 2, 0:256], ACT.Gelu, bias=self.b1[0:m, 3 + f:4 + f],
                             scale=1.0).then_inc(self.g_ready.sem, 1)
            if self.depth == 0:
                a.wait_ge(self.x2t_done.sem, self.x2t_done.at(it, 1))
                a.activation(self.XIT[:, bass.ds(it * S, S)], PS[:, 7, 0:256], ACT.Copy).then_inc(self.out_ready.sem, 1)

        shift(0, 0)
        square(0, 0, 0)
        value(0, 0, 0)
        value(0, 0, 1)
        for i in range(1, 4):
            square(0, 0, i)
        value(0, 0, 2)
        norms(0, 0)
        with a.Fori(0, B - 1) as it:
            batch(it, True)
        batch(B - 1, False)

    def vector(self, v):
        c, PS = self.c, self.c.PS

        def link(ins):
            c.dve.link(v, ins)

        v.wait_ge(self.x_ready.sem, self.x_ready.at(0, 2))
        if self.depth:
            v.wait_ge(self.prev_out.sem, self.prev_out.at(B - 1, 1))
        v.memset(self.Hs[64:128, 0:1], 0.0)
        v.memset(self.H2[64:128, 0:1], 0.0)
        v.memset(self.QZ[0:64, 1:8:2, :], 0.0)
        v.memset(self.QZ[64:128, 0:8:2, :], 0.0)
        for t in range(2):
            for i, sc in enumerate((self.qs, self.ks)):
                cos = self.tables[:, t, 2 * i, :]
                sin = self.tables[:, t, 2 * i + 1, :]
                o = self.tab[:, t, i * 128:(i + 1) * 128]
                v.tensor_tensor(o[:, 0:64], cos, sc, ALU.mult)
                v.tensor_tensor(o[:, 64:96], sin[:, 0:32], sc[:, 32:64], ALU.mult)
                v.tensor_tensor(o[:, 96:128], sin[:, 32:64], sc[:, 0:32], ALU.mult)
        link(v.tensor_copy(self.MBK, self.maskb))
        v.memset(self.nm, 0.0).then_inc(self.mask_ready.sem, 1)
        v.wait_ge(self.mask_ready.sem, self.mask_ready.at(0, 1))

        def rotate(it, d, i):
            t, j = divmod(i, 2)
            v.wait_ge(self.p_done.sem, self.p_done.at(it, (1, 2, 5, 6)[i], d))
            if i >= 2:
                v.wait_ge(self.qk_sum.sem, self.qk_sum.at(it, i - 1, d))
            tab = self.tab[:, t, j * 128:(j + 1) * 128]
            q = PS[:, j, :].rearrange("p (h d) -> p h d", h=8)
            qa = self.QA[:, i, :].rearrange("p (h d) -> p h d", h=8)
            qb = self.QB[:, i % 2, :].rearrange("p (h d) -> p h d", h=8)

            def tb(a, b):
                return tab[:, a:b].unsqueeze(1).to_broadcast([P, 8, b - a])

            v.tensor_tensor(qa, q, tb(0, 64), ALU.mult)
            v.tensor_tensor(qb[:, :, 0:32], q[:, :, 32:64], tb(64, 96), ALU.mult)
            v.tensor_tensor(qb[:, :, 32:64], q[:, :, 0:32], tb(96, 128), ALU.mult).then_inc(self.ab_done.sem, 1)

        def sums(it, d, i):
            v.wait_ge(self.sq_done.sem, self.sq_done.at(it, i + 1, d))
            v.tensor_reduce(self.ssq[:, i, :], self.SQ.rearrange("p (h d) -> p h d", h=8), AX.X, ALU.add)\
                .then_inc(self.ssq_used.sem, 1)
            if i == 3:
                v.wait_ge(self.ssq_used.sem, self.ssq_used.at(it, 4, d))
                v.tensor_scalar(self.ssq, self.ssq, 1e-24, None, ALU.max).then_inc(self.sum_ready.sem, 1)

        def inverses(it, d):
            v.wait_ge(self.nrm_ready.sem, self.nrm_ready.at(it, 1, d))
            link(v.reciprocal(self.inv, self.nrm))
            refine(link, v, self.inv, self.ssq, 0.0, self.nrt)
            v.tensor_scalar(self.inv, self.inv, 1.0, None, ALU.mult).then_inc(self.inv_ready.sem, 1)
            v.wait_ge(self.inv_ready.sem, self.inv_ready.at(it, 1, d))
            v.wait_ge(self.qk_sum.sem, self.qk_sum.at(it, 2, d))
            for i in range(2):
                q = self.QA[:, i, :].rearrange("p (h d) -> p h d", h=8)
                v.tensor_tensor(q, q, self.inv[:, i, :].unsqueeze(2).to_broadcast([P, 8, 64]), ALU.mult)\
                    .then_inc(self.qk0_ready.sem, 1)

        def turned(it, d, i):
            v.wait_ge(self.tr_done.sem, self.tr_done.at(it, i + 1, d))
            t, j = divmod(i, 2)
            src = PS[:, 3 - i % 2, :].rearrange("p (k q) -> p k q", k=4)
            if j == 0:
                v.tensor_copy(self.QZ[0:64, 0:8:2, t * P:(t + 1) * P], src[0:64])
                ins = v.tensor_copy(self.QZ[64:128, 1:8:2, t * P:(t + 1) * P], src[64:128])
            else:
                ins = v.tensor_copy(self.KT[:, :, t * P:(t + 1) * P], src)
            ins.then_inc(self.tr_ev.sem, 1)

        def maxima(it, k):
            v.wait_ge(self.s_done.sem, self.s_done.at(it, k + 1))
            v.tensor_reduce(self.nm[:, k, :], PS[:, k % 2, :].rearrange("p (w j) -> p w j", w=4), AX.X, ALU.max,
                            negate=True).then_inc(self.mx_done.sem, 1)

        def reciprocals(it, k):
            v.wait_ge(self.e_done.sem, self.e_done.at(it, k + 1))
            v.reciprocal(self.ri[:, k, :], self.ss[:, k, :]).then_inc(self.r_done.sem, 1)

        def spread(it, k):
            v.wait_ge(self.t_done.sem, self.t_done.at(it, k + 1))
            if k >= 2:
                v.wait_ge(self.o_done.sem, self.o_done.at(it, k - 1))
            v.tensor_copy(self.PT[:, k % 2, :], PS[:, 2 + k % 2, :]).then_inc(self.pt_ev.sem, 1)

        def hidden(it, f):
            m = self.HID[f]
            v.wait_ge(self.g_ready.sem, self.g_ready.at(it, f + 1))
            v.scalar_tensor_tensor(self.HD[0:m, f, :], PS[0:m, 4 + f % 2, 0:256], self.b1[0:m, f:f + 1],
                                   self.GE[0:m, f % 2, :], ALU.add, ALU.mult).then_inc(self.hid_ready.sem, 1)

        def batch(it, more):
            xin, _ = self.source(it)
            maxima(it, 0)
            maxima(it, 1)
            reciprocals(it, 0)
            maxima(it, 2)
            reciprocals(it, 1)
            spread(it, 0)
            maxima(it, 3)
            reciprocals(it, 2)
            spread(it, 1)
            reciprocals(it, 3)
            spread(it, 2)
            spread(it, 3)
            if more:
                rotate(it, 1, 0)
            v.wait_ge(self.y_done.sem, self.y_done.at(it, 1))
            v.tensor_tensor(self.X1, two(PS[:, 6, 0:256]), xin, ALU.add).then_inc(self.x1_ready.sem, 1)
            if more:
                rotate(it, 1, 1)
                sums(it, 1, 0)
            v.wait_ge(self.h2_done.sem, self.h2_done.at(it, 1))
            for t in range(2):
                ins = v.bn_stats(self.st[:, 6 * t:6 * t + 6], PS[:, 6, t * P:(t + 1) * P])
            link(ins)
            v.tensor_tensor(self.X1, self.X1, self.b2.unsqueeze(1).to_broadcast([P, 2, P]), ALU.add)
            for t in range(2):
                ins = v.bn_aggr(self.mv2[:, 2 * t:2 * t + 2], self.st[:, 6 * t:6 * t + 6])
            ins.then_inc(self.var_ready.sem, 1)
            if more:
                sums(it, 1, 1)
                rotate(it, 1, 2)
            v.wait_ge(self.sd_ready.sem, self.sd_ready.at(it, 1))
            link(v.reciprocal(self.rs2, self.sd2))
            refine(link, v, self.rs2, self.mv2.rearrange("p (t k) -> p t k", k=2)[:, :, 1], EPS, c.rt[:, 0:2])
            for t in range(2):
                ins = v.tensor_scalar(self.HN[:, t, :], PS[:, 6, t * P:(t + 1) * P], self.mv2[:, 2 * t:2 * t + 1],
                                      self.rs2[:, t:t + 1], ALU.subtract, ALU.mult)
            ins.then_inc(self.n_ready.sem, 1)
            if more:
                sums(it, 1, 2)
                rotate(it, 1, 3)
                sums(it, 1, 3)
                inverses(it, 1)
            hidden(it, 0)
            hidden(it, 1)
            if more:
                turned(it, 1, 0)
                turned(it, 1, 1)
            hidden(it, 2)
            if more:
                turned(it, 1, 2)
                turned(it, 1, 3)
            v.wait_ge(self.f_done.sem, self.f_done.at(it, 1))
            y = two(PS[:, 5, 0:256])
            if self.depth == 0:
                v.tensor_tensor(self.XI[:, bass.ds(it * 2, 2), :], self.X1, y, ALU.add)
                v.tensor_tensor(self.HN, self.X1, y, ALU.add).then_inc(self.z_ready.sem, 1)
                v.wait_ge(self.x2t_done.sem, self.x2t_done.at(it, 1))
            else:
                link(v.tensor_tensor(self.X1, self.X1, y, ALU.add))
                v.tensor_tensor(c.Z[:, bass.ds(it * 2, 2), :], self.X1, c.X[:, bass.ds(it * 2, 2), :], ALU.add)\
                    .then_inc(self.z_ready.sem, 1)

        rotate(0, 0, 0)
        for i in range(1, 4):
            rotate(0, 0, i)
            sums(0, 0, i - 1)
        sums(0, 0, 3)
        inverses(0, 0)
        for i in range(4):
            turned(0, 0, i)
        with v.Fori(0, B - 1) as it:
            c.dve.enter(it)
            batch(it, True)
        c.dve.leave(B - 1)
        batch(B - 1, False)
        v.wait_ge(self.z_ready.sem, self.z_ready.at(B - 1, 1))

    def gpsimd(self, g):
        def queries_keys(it, d):
            for i in range(4):
                g.wait_ge(self.ab_done.sem, self.ab_done.at(it, i + 1, d))
                g.tensor_tensor(self.QA[:, i, :], self.QA[:, i, :], self.QB[:, i % 2, :], ALU.add)\
                    .then_inc(self.qk_sum.sem, 1)
            g.wait_ge(self.inv_ready.sem, self.inv_ready.at(it, 1, d))
            g.wait_ge(self.qk_sum.sem, self.qk_sum.at(it, 4, d))
            for i in (2, 3):
                q = self.QA[:, i, :].rearrange("p (h d) -> p h d", h=8)
                g.tensor_tensor(q, q, self.inv[:, i, :].unsqueeze(2).to_broadcast([P, 8, 64]), ALU.mult)\
                    .then_inc(self.qk1_ready.sem, 1)

        def probabilities(it):
            for k in range(4):
                g.wait_ge(self.r_done.sem, self.r_done.at(it, k + 1))
                p = self.Pr[:, k % 3, :].rearrange("p (w j) -> p w j", w=4)
                g.tensor_tensor(p, p, self.ri[:, k, :].unsqueeze(2).to_broadcast([P, 4, P]), ALU.mult)\
                    .then_inc(self.pn_done.sem, 1)

        queries_keys(0, 0)
        with g.Fori(0, B - 1) as it:
            probabilities(it)
            queries_keys(it, 1)
        probabilities(B - 1)


def chunks(w):
    return w.reshape(-1, P, w.shape[-1]).transpose(1, 0, 2)


def head_rows(w):
    out = np.zeros((4, 4, 32, w.shape[-1]), w.dtype)
    out[:, :, 0:8] = w.reshape(4, 4, 8, -1)
    return out.reshape(4, P, -1).transpose(1, 0, 2)


def over(b):
    return np.broadcast_to(b.reshape(1, -1), (P, b.size))


def constants():
    i = np.arange(P)
    f = np.float32
    headmask = (i[:, None] // 8 == np.arange(16)[None, :]).astype(f)
    rel, band = (t.reshape(WIN_Q, -1) for t in window_tables())
    return [("ident", np.eye(P, dtype=f)), ("headmask", headmask),
            ("eps", np.full((P, 1), EPS, f)), ("rel", rel), ("one", np.ones((P, 1), f)),
            ("onehot", (i[:, None] % 32 == np.arange(32)[None, :]).astype(f)), ("band", band),
            ("iota8", np.broadcast_to(np.arange(8, dtype=f), (P, 8)))]


def weights(w):
    i = np.arange(P)
    l0a = [("causal", np.where(i[None, :] <= i[:, None], 0.0, NEG).astype(np.float32)), ("L0a_wlat", w["L0_attn_w_kv_down"]), ("L0a_wkv", w["L0_attn_w_kv_up"]), ("L0a_wq", w["L0_attn_w_q"]),
           ("L0a_wo", chunks(w["L0_attn_w_out"]))]
    l1x = [("L1x_wq", w["L1_xattn_W_q"].T), ("L1x_wk", w["L1_xattn_W_k"].T), ("L1x_wv", w["L1_xattn_W_v"].T),
           ("L1x_wo", head_rows(w["L1_xattn_W_out"].T)), ("L1x_bq", w["L1_xattn_b_q"][:, None]),
           ("L1x_bk", w["L1_xattn_b_k"][:, None]), ("L1x_bv", over(w["L1_xattn_b_v"])),
           ("L1x_bo", over(w["L1_xattn_b_out"]))]
    l2x = [("L2x_wq", w["L2_xattn_wq"].T), ("L2x_wk", w["L2_xattn_wk"].T),
           ("L2x_wo", head_rows(w["L2_xattn_wo"].T)), ("L2x_bq", w["L2_xattn_bq"][:, None]),
           ("L2x_bk", w["L2_xattn_bk"][:, None]), ("L2x_bv", over(w["L2_xattn_bk"])),
           ("L2x_bo", over(w["L2_xattn_bo"]))]
    l3x = [("L3x_wq", w["L3_xattn_Wq"]), ("L3x_wk", w["L3_xattn_Wk"]), ("L3x_wv", w["L3_xattn_Wv"]),
           ("L3x_wo", chunks(w["L3_xattn_Wo"])), ("L3x_bo", over(w["L3_xattn_bo"]))]
    names = ("Wq_c", "Wk_s", "Wv_s", "Wq_s", "Wk_c", "Wv_c")
    l0x = [("L0x_w", np.stack([w["L0_xattn_" + n].T for n in names], 1)),
           ("L0x_bq", np.stack([w["L0_xattn_bq_c"], w["L0_xattn_bq_s"]], 1)),
           ("L0x_bk", np.stack([w["L0_xattn_bk_s"], w["L0_xattn_bk_c"]], 1)),
           ("L0x_bv", np.stack([over(w["L0_xattn_bv_s"]), over(w["L0_xattn_bv_c"])], 1)),
           ("L0x_wg", chunks(w["L0_xattn_Wg"].T)), ("L0x_bg", w["L0_xattn_bg"][:, None])]
    l1f = [("L1f_w1", w["L1_ffn_w1"].T), ("L1f_w2", chunks(w["L1_ffn_w2"].T)),
           ("L1f_cw", chunks(w["L1_ffn_conv_w"][:, 0, :])), ("L1f_cb", chunks(w["L1_ffn_conv_b"][:, None])[:, :, 0])]
    up = np.concatenate([w["L2_ffn_w_up"], w["L2_ffn_sw_up"][None]], 0).transpose(1, 0, 2)
    gate = np.concatenate([w["L2_ffn_w_gate"], w["L2_ffn_sw_gate"][None]], 0).transpose(1, 0, 2)
    down = np.concatenate([w["L2_ffn_w_down"], w["L2_ffn_sw_down"][None]], 0).transpose(1, 0, 2)
    gap = np.zeros((P, up.shape[1], 64 - (up.shape[2] - P)), up.dtype)
    l2f = [("L2f_gu", np.concatenate([gate[:, :, :P], up[:, :, :P]], 2)),
           ("L2f_rest", np.concatenate([gate[:, :, P:], gap, up[:, :, P:]], 2)),
           ("L2f_down", down[:P]), ("L2f_drest", down[P:]),
           ("L2f_router", np.concatenate([w["L2_ffn_gate_w"], w["L2_ffn_shared_gate_w"]], 0).T)]
    up = np.concatenate([w["L3_ffn_routed_up"], w["L3_ffn_shared_up"][None]], 0).transpose(2, 0, 1)
    gate = np.concatenate([w["L3_ffn_routed_gate"], w["L3_ffn_shared_gate"][None]], 0).transpose(2, 0, 1)
    down = np.concatenate([w["L3_ffn_routed_down"], w["L3_ffn_shared_down"][None]], 0)
    n = up.shape[1] * 4
    l3f = [("L3f_gu", np.concatenate([gate.reshape(P, n, P), up.reshape(P, n, P)], 2)),
           ("L3f_down", down.transpose(0, 2, 1).reshape(-1, 4, P, P).transpose(2, 0, 1, 3).reshape(P, n, P))]
    router = np.zeros((P, 8), np.float32)
    router[:, 0:7] = w["L3_ffn_router_w"].T
    l3r = [("L3f_router", router)]
    rel = w["L2_attn_rel_pos_keys"][13:20, 0:8]
    l2a = [("L2a_win", w["L2_attn_in_proj_weight"].T), ("L2a_bin", over(w["L2_attn_in_proj_bias"])),
           ("L2a_rel", np.broadcast_to(np.tile(rel, (1, 16)), (P, 7, P))), ("L2a_wout", w["L2_attn_out_w"].T),
           ("L2a_bout", over(w["L2_attn_out_b"]))]
    wx = w["L1_attn_W_x"].T
    l1a = [("L1a_g", w["L1_attn_ln_g"][:, None]), ("L1a_b", w["L1_attn_ln_b"][:, None]), ("L1a_win", w["L1_attn_W_in"].T),
           ("L1a_cw", chunks(w["L1_attn_conv_w"])), ("L1a_cb", chunks(w["L1_attn_conv_b"][:, None])[:, :, 0]),
           ("L1a_wdti", chunks(wx[:, 0:8])), ("L1a_wbc", chunks(np.tile(wx[:, 8:40], (1, 3)))),
           ("L1a_wdt", w["L1_attn_W_dt"].T), ("L1a_bdt", chunks(w["L1_attn_dt_bias"][:, None])[:, :, 0]),
           ("L1a_alog", chunks(w["L1_attn_A_log"]).reshape(P, 32)), ("L1a_D", chunks(w["L1_attn_D"][:, None])[:, :, 0]),
           ("L1a_wout", chunks(w["L1_attn_W_out"].T))]
    l0f = [("rotary", rotary_tables().reshape(2, P, 4, 64).transpose(1, 0, 2, 3)),
           ("local", local_masks().reshape(P, 512))]
    for d in range(2):
        b1 = np.zeros((2, 384), np.float32)
        b1[:, 0:341] = w["L0_ffn_b1"][d].reshape(2, 341)
        l0f += [(f"L0f{d}_wqkv", w["L0_ffn_wqkv"][d]), (f"L0f{d}_qs", over(w["L0_ffn_q_scale"][d])),
                (f"L0f{d}_ks", over(w["L0_ffn_k_scale"][d])), (f"L0f{d}_wo", chunks(w["L0_ffn_wo"][d])),
                (f"L0f{d}_lg", w["L0_ffn_ln_g"][d][:, None]), (f"L0f{d}_lb", w["L0_ffn_ln_b"][d][:, None]),
                (f"L0f{d}_w1", w["L0_ffn_w1"][d]), (f"L0f{d}_b1", b1.reshape(6, P).T),
                (f"L0f{d}_w2", chunks(w["L0_ffn_w2"][d][0:256])), (f"L0f{d}_w2r", w["L0_ffn_w2"][d][256:341]),
                (f"L0f{d}_b2", over(w["L0_ffn_b2"][d]))]
    l3a = [("L3a_wq", w["L3_attn_Wq"].T), ("L3a_wk", w["L3_attn_Wk"].T), ("L3a_wv", w["L3_attn_Wv"].T),
           ("L3a_wo", head_rows(w["L3_attn_Wo"].T)), ("L3a_slopes", over(w["L3_attn_slopes"]))]
    return {"first": l0a + l0x + l0f, "rest": l1a + l1x + l1f + l2a + l2x + l2f + l3a, "last": l3x + l3r + l3f}


def pack(pieces):
    table, at = {}, 0
    for name, a in pieces:
        n = int(np.prod(a.shape[1:]))
        table[name] = (at, a.shape)
        at += n
    out = np.zeros((P, at), np.float32)
    for name, a in pieces:
        o, shape = table[name]
        out[0:shape[0], o:o + int(np.prod(shape[1:]))] = a.reshape(shape[0], -1)
    return out, table


def build(nc, dram, tables, totals, names):
    with ExitStack() as ctx:
        c = Core(ctx, nc, totals)
        packs = {k: c.sb(f"w_{k}", [P, dram[k].shape[1]]) for k in tables if k != "first"}
        packs["first"] = packs["last"][:, 0:dram["first"].shape[1]]
        mask = c.sb("mask", [P, T, S], U8)
        loaded = {k: ctx.enter_context(nc.semaphore(f"loaded_{k}")) for k in list(tables) + ["x", "ctx", "mask", "L0a"]}
        stored = ctx.enter_context(nc.semaphore("stored"))
        x_loaded_tr = c.sig("x_loaded_tr", 2, 1)
        start_x = c.x_ready

        def W(name):
            for k, table in tables.items():
                if name in table:
                    o, shape = table[name]
                    ap = packs[k][0:shape[0], o:o + int(np.prod(shape[1:]))]
                    if len(shape) == 3:
                        ap = ap.rearrange("p (a b) -> p a b", a=shape[1])
                    if len(shape) == 4:
                        ap = ap.rearrange("p (a b c) -> p a b c", a=shape[1], b=shape[2])
                    return ap

        c.W = W
        c.ident, c.eps, c.one = W("ident"), W("eps"), W("one")
        onehot = c.sb("onehot", [P, 32], BF16)

        def wait_weights(eng, stage):
            if stage.region == "first" and isinstance(stage, Attention):
                eng.wait_ge(loaded["L0a"], 16)
                return
            eng.wait_ge(loaded["ctx"], 16)
            eng.wait_ge(loaded["mask"], 16)
            eng.wait_ge(loaded[stage.region], 16)
        c.wait_weights = wait_weights

        def local(d):
            w = [W(f"L0f{d}_{n}") for n in ("wqkv", "qs", "ks", "wo", "lg", "lb", "w1", "b1", "w2", "w2r", "b2")]
            return LocalLayer(c, d, *w, W("rotary"), W("local"))

        makers = {
            "L1a": lambda: Mamba(c, *(W(f"L1a_{n}") for n in ("g", "b", "win", "cw", "cb", "wdti", "wbc", "wdt", "bdt",
                                                             "alog", "D", "wout")), onehot),
            "L0a": lambda: Attention(c, 64, W("L0a_wq"), W("L0a_wkv")[:, 0:1024], W("L0a_wkv")[:, 1024:2048],
                                     W("L0a_wo"), "x", wlat=W("L0a_wlat"), causal=W("causal")),
            "L0x": lambda: TwoWay(c, W("L0x_w"), W("L0x_bq"), W("L0x_bk"), W("L0x_bv"), W("L0x_wg"), W("L0x_bg")),
            "L1f": lambda: BitLinear(c, W("L1f_w1"), W("L1f_w2"), W("L1f_cw"), W("L1f_cb")),
            "L2a": lambda: FourTokenAttention(c, W("L2a_win"), W("L2a_bin"), W("L2a_rel"), W("L2a_wout"), W("L2a_bout")),
            "L3a": lambda: BandedAttention(c, W("L3a_wq"), W("L3a_wk"), W("L3a_wv"), W("L3a_wo"), W("L3a_slopes"),
                                           W("rel"), W("band"), W("headmask"),
                                           packs["rest"]),
            "L2f": lambda: Experts(c, 8, 1, 48, W("L2f_gu"), W("L2f_rest"), W("L2f_down"), W("L2f_drest"),
                                   W("L2f_router"), W("iota8"), True, 0.0),
            "L3f": lambda: Experts(c, 7, 4, 0, W("L3f_gu"), None, W("L3f_down"), None,
                                   W("L3f_router"), W("iota8"), False, 1e-9),
            "L1x": lambda: Attention(c, 8, W("L1x_wq"), W("L1x_wk"), W("L1x_wv"), W("L1x_wo"), "ctx",
                                     bq=W("L1x_bq"), bk=W("L1x_bk"), bv=W("L1x_bv"), bo=W("L1x_bo"),
                                     headmask=W("headmask")),
            "L2x": lambda: Attention(c, 8, W("L2x_wq"), W("L2x_wk"), W("L2x_wk"), W("L2x_wo"), "ctx",
                                     bq=W("L2x_bq"), bk=W("L2x_bk"), bv=W("L2x_bv"), bo=W("L2x_bo"),
                                     headmask=W("headmask")),
            "L3x": lambda: Attention(c, 64, W("L3x_wq"), W("L3x_wk"), W("L3x_wv"), W("L3x_wo"), "ctx",
                                     mask=mask, bo=W("L3x_bo")),
        }
        regions = {"L0a": "first", "L0x": "first", "L0f": "first", "L3x": "last", "L3f": "last"}
        stages = []
        for i, n in enumerate(names):
            if n == "L0f":
                first = local(0)
                first.region = "first"
                stages.append(first)
                s = local(1)
                s.prev_out = first.out_ready
            else:
                s = makers[n]()
            s.region = regions.get(n, "rest")
            if s.region == "first":
                last_first = s.z_ready
            s.end = LayerEnd(c, s.z_ready, last=i == len(names) - 1, early=isinstance(s, Attention),
                             counted=s.ITERS if isinstance(s, Experts) else 0)
            stages += [s, s.end]
        last_x = stages[-1].x_tile
        block = ctx.enter_context(nc.Block())

        @block.sync
        def _(sp):
            sp.dma_start(packs["consts"][:, :], dram["consts"]).then_inc(loaded["consts"], 16)
            sp.dma_start(c.X[:, :, :], dram["x"].rearrange("(t p) d -> p t d", p=P)).then_inc(loaded["x"], 16)
            if "L0" in names[0]:
                n = tables["first"]["L0x_w"][0]
                sp.dma_start(packs["first"][:, 0:n], dram["first"][:, 0:n]).then_inc(loaded["L0a"], 16)
            sp.dma_start(c.CT[:, :], dram["ctxT"]).then_inc(loaded["ctx"], 16)
            if "L0" in names[0]:
                sp.dma_start(packs["first"][:, n:], dram["first"][:, n:]).then_inc(loaded["first"], 16)
            sp.dma_start(mask[:, :, :], dram["mask"].rearrange("(t p) k -> p t k", p=P)).then_inc(loaded["mask"], 16)
            sp.dma_start(packs["rest"][:, :], dram["rest"]).then_inc(loaded["rest"], 16)
            if "L3" in names[-1]:
                if "L0" in names[0]:
                    sp.wait_ge(last_first.sem, last_first.at(B - 1, 1))
                sp.dma_start(packs["last"][:, :], dram["last"]).then_inc(loaded["last"], 16)
            sp.wait_ge(last_x.sem, last_x.at(0, T))
            sp.dma_start(dram["out"].rearrange("(t p) d -> p t d", p=P), c.X[:, :, :]).then_inc(stored, 16)
            sp.wait_ge(stored, 16)

        @block.tensor
        def _(pe):
            pe.wait_ge(loaded["consts"], 16)
            pe.wait_ge(loaded["x"], 16)
            for n in range(T):
                ins = pe.transpose(c.PS[:, n // 4, (n % 4) * P:(n % 4) * P + P], c.X[:, n, :], c.ident)
                if n % 4 == 3:
                    ins.then_inc(x_loaded_tr.sem, 1)
            for s in stages:
                if isinstance(s, LayerEnd) is False:
                    wait_weights(pe, s)
                s.tensor(pe)

        @block.vector
        def _(v):
            v.wait_ge(loaded["consts"], 16)
            v.tensor_copy(c.IDB[:, :], c.ident)
            v.tensor_copy(onehot[:, :], W("onehot"))
            v.wait_ge(x_loaded_tr.sem, 1)
            v.tensor_copy(c.XT[:, 0:512], c.PS[:, 0, :]).then_inc(start_x.sem, 1)
            for s in stages:
                if not isinstance(s, LayerEnd):
                    wait_weights(v, s)
                s.vector(v)

        @block.scalar
        def _(a):
            a.wait_ge(x_loaded_tr.sem, 2)
            a.activation(c.XT[:, 512:1024], c.PS[:, 1, :], ACT.Copy).then_inc(start_x.sem, 1)
            for s in stages:
                if not isinstance(s, LayerEnd):
                    wait_weights(a, s)
                s.scalar(a)

        @block.gpsimd
        def _(g):
            for s in stages:
                if not isinstance(s, LayerEnd):
                    wait_weights(g, s)
                s.gpsimd(g)


def lay_out(w):
    arrays = {"x": np.ascontiguousarray(w["x"]).reshape(B * S, P),
              "ctxT": np.ascontiguousarray(w["ctx_1024"].reshape(B * S, P).T),
              "mask": np.ascontiguousarray(w["mask_BxSxS2_bk1"]).reshape(B * S, S)}
    tables = {}
    arrays["consts"], tables["consts"] = pack(constants())
    for k, pieces in weights(w).items():
        arrays[k], tables[k] = pack(pieces)
    return arrays, tables


def program(nc, arrays, tables, totals, names):
    dram = {k: nc.dram_tensor(f"in_{k}", a.shape, mybir.dt.from_np(a.dtype), kind="ExternalInput").ap()
            for k, a in arrays.items()}
    dram["out"] = nc.dram_tensor("out_0", (B * S, P), F32, kind="ExternalOutput").ap()
    build(nc, dram, tables, totals, names)


ORDER = ["L0a", "L0x", "L0f", "L1a", "L1x", "L1f", "L2a", "L2x", "L2f", "L3a", "L3x", "L3f"]


def kernel(**inputs):
    import concourse.bacc as bacc
    from concourse.bass_utils import run_bass_kernel_spmd as run

    w = {k: np.asarray(v) for k, v in inputs.items()}
    arrays, tables = lay_out(w)
    totals = {}
    for _ in range(2):
        nc = bacc.Bacc("TRN2", target_bir_lowering=False, num_devices=1)
        program(nc, arrays, tables, totals, ORDER)
    r = run(nc, [{f"in_{k}": a for k, a in arrays.items()}], core_ids=[0])
    return r.results[0]["out_0"].reshape(B, S, P)
```
